# Optimizing a Trainium2 kernel written in Bass

```python
import numpy as np
import jax
import jax.numpy as jnp

def _softmax(x, axis=-1):
    return jax.nn.softmax(x, axis=axis)

def _gelu(x):
    return jax.nn.gelu(x, approximate=True)

def _silu(x):
    return jax.nn.silu(x)

def _sigmoid(x):
    return jax.nn.sigmoid(x)

def _layernorm(x, axis=-1, eps=1e-05):
    m = jnp.mean(x, axis=axis, keepdims=True)
    v = jnp.var(x, axis=axis, keepdims=True)
    return (x - m) / jnp.sqrt(v + eps)

def _scatter_add(tgt, idx, src, axis=0):
    return tgt.at[idx].add(src)

def _segment_sum(src, seg, n):
    return jax.ops.segment_sum(src, seg, n)
kernel_name = 'mk_gnn_resnorm_d4_gnn_r16_c746c1'

def setup_inputs(seed: int=0):
    np.random.seed(seed)
    _w = jnp.asarray

    def _rec_inputs():
        import jax
        import jax.numpy as jnp
        _gk = jax.random.key(seed)
        x = -0.0003713 + 1 * jax.random.normal(jax.random.fold_in(_gk, 1), (6250, 128), jnp.float32)
        _s = jax.random.randint(jax.random.fold_in(_gk, 2), (50000,), 0, 6250, jnp.int32)
        _d = jax.random.randint(jax.random.fold_in(_gk, 3), (50000,), 0, 6250, jnp.int32)
        _loop = jnp.arange(6250, dtype=jnp.int32)
        src = jnp.concatenate([_s, _d, _loop])
        dst = jnp.concatenate([_d, _s, _loop])
        _o = jnp.argsort(dst, stable=True)
        src = src[_o]
        dst = dst[_o]
        edge_attr_2 = 0.000126197 + 0.999763 * jax.random.normal(jax.random.fold_in(_gk, 12), (106250, 2), jnp.float32)
        edge_type_4 = jax.random.randint(jax.random.fold_in(_gk, 14), (106250,), 0, 4, jnp.int32)
        edge_type_8 = jax.random.randint(jax.random.fold_in(_gk, 15), (106250,), 0, 8, jnp.int32)
        edge_weight = jax.random.uniform(jax.random.fold_in(_gk, 16), (106250,), jnp.float32, 0.0, 0.999999)
        return (x, src, dst, edge_attr_2, edge_type_4, edge_type_8, edge_weight)
    x, src, dst, edge_attr_2, edge_type_4, edge_type_8, edge_weight = _rec_inputs()

    def _L0_gnn_setup():
        import jax, jax.numpy as jnp
        import numpy as np
        N_NODES = 6250
        N_EDGES = 100000
        IN_FEATS = 128
        OUT_FEATS = 128
        key = jax.random.key(seed)
        k1, k2, k3, k4, k5 = jax.random.split(key, 5)
        feat = jax.random.normal(k1, (N_NODES, IN_FEATS), dtype=jnp.float32)
        src = jax.random.randint(k2, (N_EDGES,), 0, N_NODES, dtype=jnp.int32)
        dst = jax.random.randint(k3, (N_EDGES,), 0, N_NODES, dtype=jnp.int32)
        gain = float(np.sqrt(2.0))
        bound = gain * float(np.sqrt(6.0 / (IN_FEATS + OUT_FEATS)))
        W_neigh = jax.random.uniform(k4, (OUT_FEATS, IN_FEATS), minval=-bound, maxval=bound, dtype=jnp.float32)
        b_neigh = jax.random.uniform(k5, (OUT_FEATS,), minval=-1.0 / np.sqrt(IN_FEATS), maxval=1.0 / np.sqrt(IN_FEATS), dtype=jnp.float32)
        return {'feat': feat, 'src': src, 'dst': dst, 'W_neigh': W_neigh, 'b_neigh': b_neigh}
    _L0_gnn_all = _L0_gnn_setup()
    _L0_gnn_in = {k: v for k, v in _L0_gnn_all.items() if k in ('W_neigh', 'b_neigh')}
    del _L0_gnn_all

    def _L1_gnn_setup():
        import jax, jax.numpy as jnp
        import numpy as np
        N = 3125
        E = 50000
        IN = 128
        H = 256
        EMB = 128
        R = 4
        HEADS = 2

        def _segmean(msg, seg, num_segments):
            s = jax.ops.segment_sum(msg, seg, num_segments=num_segments)
            c = jax.ops.segment_sum(jnp.ones((seg.shape[0], 1), msg.dtype), seg, num_segments=num_segments)
            return s / jnp.maximum(c, 1.0)

        def _sage(x, src, dst, Wl, Wr, b, n):
            agg = _segmean(x[src], dst, n)
            return agg @ Wl + x @ Wr + b

        def _gat(x, src, dst, W, a_src, a_dst, b, n):
            loop = jnp.arange(n, dtype=src.dtype)
            src = jnp.concatenate([src, loop])
            dst = jnp.concatenate([dst, loop])
            h = (x @ W).reshape(n, HEADS, -1)
            al_src = (h * a_src).sum(-1)
            al_dst = (h * a_dst).sum(-1)
            e = jax.nn.leaky_relu(al_src[src] + al_dst[dst], 0.2)
            m = jax.ops.segment_max(e, dst, num_segments=n)
            ex = jnp.exp(e - m[dst])
            den = jax.ops.segment_sum(ex, dst, num_segments=n)
            alpha = ex / jnp.maximum(den[dst], 1e-16)
            out = jax.ops.segment_sum(alpha[:, :, None] * h[src], dst, num_segments=n)
            return out.mean(axis=1) + b

        def _rgcn(x, src, dst, etype, Wrel, Wroot, b, n, r):
            xt = jnp.einsum('nh,rhe->rne', x, Wrel)
            m = xt[etype, src]
            seg = dst * r + etype
            agg = _segmean(m, seg, n * r).reshape(n, r, -1).sum(axis=1)
            return agg + x @ Wroot + b
        key = jax.random.key(seed)
        ks = jax.random.split(key, 20)
        w = lambda k, shape: jax.random.normal(k, shape, dtype=jnp.float32) * 0.05
        return dict(x=jax.random.normal(ks[0], (N, IN), dtype=jnp.float32), edge_index=jax.random.randint(ks[1], (2, E), 0, N, dtype=jnp.int32), edge_type=jax.random.randint(ks[2], (E,), 0, R, dtype=jnp.int32), sage1_Wl=w(ks[3], (IN, H)), sage1_Wr=w(ks[4], (IN, H)), sage1_b=jnp.zeros((H,), jnp.float32), sage2_Wl=w(ks[5], (H, H)), sage2_Wr=w(ks[6], (H, H)), sage2_b=jnp.zeros((H,), jnp.float32), gat_W=w(ks[7], (H, HEADS * H)), gat_att_src=w(ks[8], (HEADS, H)), gat_att_dst=w(ks[9], (HEADS, H)), gat_b=jnp.zeros((H,), jnp.float32), rgcn_Wrel=w(ks[10], (R, H, EMB)), rgcn_Wroot=w(ks[11], (H, EMB)), rgcn_b=jnp.zeros((EMB,), jnp.float32), fusion_W=w(ks[12], (H + H + EMB, EMB)), fusion_b=jnp.zeros((EMB,), jnp.float32))
    _L1_gnn_all = _L1_gnn_setup()
    _L1_gnn_in = {k: v for k, v in _L1_gnn_all.items() if k in ('sage1_Wl', 'sage1_Wr', 'sage1_b', 'sage2_Wl', 'sage2_Wr', 'sage2_b', 'gat_W', 'gat_att_src', 'gat_att_dst', 'gat_b', 'rgcn_Wrel', 'rgcn_Wroot', 'rgcn_b', 'fusion_W', 'fusion_b')}
    del _L1_gnn_all

    def _L2_gnn_setup():
        import jax, jax.numpy as jnp
        import numpy as np
        N = 2500
        E = 40000
        CIN = 128
        COUT = 128
        EDGE_DIM = 2
        BN_EPS = 1e-05
        key = jax.random.key(seed)
        ks = jax.random.split(key, 9)
        din = 2 * CIN + EDGE_DIM
        x = jax.random.normal(ks[0], (N, CIN), dtype=jnp.float32)
        edge_index = jax.random.randint(ks[1], (2, E), 0, N, dtype=jnp.int64)
        edge_attr = jax.random.normal(ks[2], (E, EDGE_DIM), dtype=jnp.float32)
        W1 = jax.random.normal(ks[3], (din, COUT), dtype=jnp.float32) / np.sqrt(din)
        b1 = jax.random.normal(ks[4], (COUT,), dtype=jnp.float32) * 0.01
        gamma = jnp.ones((COUT,), dtype=jnp.float32)
        beta = jnp.zeros((COUT,), dtype=jnp.float32)
        W2 = jax.random.normal(ks[5], (COUT, COUT), dtype=jnp.float32) / np.sqrt(COUT)
        b2 = jax.random.normal(ks[6], (COUT,), dtype=jnp.float32) * 0.01
        return {'x': x, 'edge_index': edge_index, 'edge_attr': edge_attr, 'W1': W1, 'b1': b1, 'gamma': gamma, 'beta': beta, 'W2': W2, 'b2': b2}
    _L2_gnn_all = _L2_gnn_setup()
    _L2_gnn_in = {k: v for k, v in _L2_gnn_all.items() if k in ('W1', 'b1', 'gamma', 'beta', 'W2', 'b2')}
    del _L2_gnn_all

    def _L3_gnn_setup():
        import jax, jax.numpy as jnp
        import numpy as np
        N_NODES = 3125
        N_EDGES = 50000
        IN_DIM = 128
        OUT_DIM = 128
        N_REL = 8
        key = jax.random.key(seed)
        k1, k2, k3, k4, k5, k6 = jax.random.split(key, 6)
        x = jax.random.normal(k1, (N_NODES, IN_DIM), dtype=jnp.float32)
        edge_index = jax.random.randint(k2, (2, N_EDGES), 0, N_NODES, dtype=jnp.int32)
        edge_type = jax.random.randint(k3, (N_EDGES,), 0, N_REL, dtype=jnp.int32)
        edge_weight = jax.random.uniform(k4, (N_EDGES,), dtype=jnp.float32)
        W = jax.random.normal(k5, (N_REL, IN_DIM, OUT_DIM), dtype=jnp.float32) * 0.02
        W0 = jax.random.normal(k6, (IN_DIM, OUT_DIM), dtype=jnp.float32) * 0.02
        return {'x': x, 'edge_index': edge_index, 'edge_type': edge_type, 'edge_weight': edge_weight, 'W': W, 'W0': W0, 'num_nodes': N_NODES}
    _L3_gnn_all = _L3_gnn_setup()
    _L3_gnn_in = {k: v for k, v in _L3_gnn_all.items() if k in ('W', 'W0')}
    del _L3_gnn_all
    return {'x': x, 'src': src, 'dst': dst, 'edge_attr_2': edge_attr_2, 'edge_type_4': edge_type_4, 'edge_type_8': edge_type_8, 'edge_weight': edge_weight, 'L0_gnn_W_neigh': _L0_gnn_in['W_neigh'], 'L0_gnn_b_neigh': _L0_gnn_in['b_neigh'], 'L1_gnn_sage1_Wl': _L1_gnn_in['sage1_Wl'], 'L1_gnn_sage1_Wr': _L1_gnn_in['sage1_Wr'], 'L1_gnn_sage1_b': _L1_gnn_in['sage1_b'], 'L1_gnn_sage2_Wl': _L1_gnn_in['sage2_Wl'], 'L1_gnn_sage2_Wr': _L1_gnn_in['sage2_Wr'], 'L1_gnn_sage2_b': _L1_gnn_in['sage2_b'], 'L1_gnn_gat_W': _L1_gnn_in['gat_W'], 'L1_gnn_gat_att_src': _L1_gnn_in['gat_att_src'], 'L1_gnn_gat_att_dst': _L1_gnn_in['gat_att_dst'], 'L1_gnn_gat_b': _L1_gnn_in['gat_b'], 'L1_gnn_rgcn_Wrel': _L1_gnn_in['rgcn_Wrel'], 'L1_gnn_rgcn_Wroot': _L1_gnn_in['rgcn_Wroot'], 'L1_gnn_rgcn_b': _L1_gnn_in['rgcn_b'], 'L1_gnn_fusion_W': _L1_gnn_in['fusion_W'], 'L1_gnn_fusion_b': _L1_gnn_in['fusion_b'], 'L2_gnn_W1': _L2_gnn_in['W1'], 'L2_gnn_b1': _L2_gnn_in['b1'], 'L2_gnn_gamma': _L2_gnn_in['gamma'], 'L2_gnn_beta': _L2_gnn_in['beta'], 'L2_gnn_W2': _L2_gnn_in['W2'], 'L2_gnn_b2': _L2_gnn_in['b2'], 'L3_gnn_W': _L3_gnn_in['W'], 'L3_gnn_W0': _L3_gnn_in['W0']}

def reference(x, src, dst, edge_attr_2, edge_type_4, edge_type_8, edge_weight, L0_gnn_W_neigh, L0_gnn_b_neigh, L1_gnn_sage1_Wl, L1_gnn_sage1_Wr, L1_gnn_sage1_b, L1_gnn_sage2_Wl, L1_gnn_sage2_Wr, L1_gnn_sage2_b, L1_gnn_gat_W, L1_gnn_gat_att_src, L1_gnn_gat_att_dst, L1_gnn_gat_b, L1_gnn_rgcn_Wrel, L1_gnn_rgcn_Wroot, L1_gnn_rgcn_b, L1_gnn_fusion_W, L1_gnn_fusion_b, L2_gnn_W1, L2_gnn_b1, L2_gnn_gamma, L2_gnn_beta, L2_gnn_W2, L2_gnn_b2, L3_gnn_W, L3_gnn_W0):
    import jax
    import jax.numpy as jnp

    def _L0_gnn_ref(feat, src, dst, W_neigh, b_neigh):
        import jax, jax.numpy as jnp
        import numpy as np
        N_NODES = 6250
        N_EDGES = 100000
        IN_FEATS = 128
        OUT_FEATS = 128
        n = feat.shape[0]
        msg = feat[src]
        h_sum = jax.ops.segment_sum(msg, dst, num_segments=n)
        deg = jax.ops.segment_sum(jnp.ones((src.shape[0],), dtype=feat.dtype), dst, num_segments=n)
        h_neigh = jnp.where(deg[:, None] > 0, h_sum / jnp.maximum(deg, 1.0)[:, None], 0.0)
        return h_neigh @ W_neigh.T + b_neigh

    def _L1_gnn_ref(x, edge_index, edge_type, sage1_Wl, sage1_Wr, sage1_b, sage2_Wl, sage2_Wr, sage2_b, gat_W, gat_att_src, gat_att_dst, gat_b, rgcn_Wrel, rgcn_Wroot, rgcn_b, fusion_W, fusion_b):
        import jax, jax.numpy as jnp
        import numpy as np
        N = 3125
        E = 50000
        IN = 128
        H = 256
        EMB = 128
        R = 4
        HEADS = 2

        def _segmean(msg, seg, num_segments):
            s = jax.ops.segment_sum(msg, seg, num_segments=num_segments)
            c = jax.ops.segment_sum(jnp.ones((seg.shape[0], 1), msg.dtype), seg, num_segments=num_segments)
            return s / jnp.maximum(c, 1.0)

        def _sage(x, src, dst, Wl, Wr, b, n):
            agg = _segmean(x[src], dst, n)
            return agg @ Wl + x @ Wr + b

        def _gat(x, src, dst, W, a_src, a_dst, b, n):
            loop = jnp.arange(n, dtype=src.dtype)
            src = jnp.concatenate([src, loop])
            dst = jnp.concatenate([dst, loop])
            h = (x @ W).reshape(n, HEADS, -1)
            al_src = (h * a_src).sum(-1)
            al_dst = (h * a_dst).sum(-1)
            e = jax.nn.leaky_relu(al_src[src] + al_dst[dst], 0.2)
            m = jax.ops.segment_max(e, dst, num_segments=n)
            ex = jnp.exp(e - m[dst])
            den = jax.ops.segment_sum(ex, dst, num_segments=n)
            alpha = ex / jnp.maximum(den[dst], 1e-16)
            out = jax.ops.segment_sum(alpha[:, :, None] * h[src], dst, num_segments=n)
            return out.mean(axis=1) + b

        def _rgcn(x, src, dst, etype, Wrel, Wroot, b, n, r):
            xt = jnp.einsum('nh,rhe->rne', x, Wrel)
            m = xt[etype, src]
            seg = dst * r + etype
            agg = _segmean(m, seg, n * r).reshape(n, r, -1).sum(axis=1)
            return agg + x @ Wroot + b
        src, dst = (edge_index[0], edge_index[1])
        n = x.shape[0]
        x1 = jax.nn.relu(_sage(x, src, dst, sage1_Wl, sage1_Wr, sage1_b, n))
        x_sage = jax.nn.relu(_sage(x1, src, dst, sage2_Wl, sage2_Wr, sage2_b, n))
        x_gat = jax.nn.relu(_gat(x_sage, src, dst, gat_W, gat_att_src, gat_att_dst, gat_b, n))
        x_rgcn = _rgcn(x_gat, src, dst, edge_type, rgcn_Wrel, rgcn_Wroot, rgcn_b, n, R)
        x_all = jnp.concatenate([x_sage, x_gat, x_rgcn], axis=1)
        out = x_all @ fusion_W + fusion_b
        norm = jnp.maximum(jnp.linalg.norm(out, axis=1, keepdims=True), 1e-12)
        return out / norm

    def _L2_gnn_ref(x, edge_index, edge_attr, W1, b1, gamma, beta, W2, b2):
        import jax, jax.numpy as jnp
        import numpy as np
        N = 2500
        E = 40000
        CIN = 128
        COUT = 128
        EDGE_DIM = 2
        BN_EPS = 1e-05
        n_nodes = x.shape[0]
        row, col = (edge_index[0], edge_index[1])
        ef = jnp.concatenate([x[row], x[col], edge_attr], axis=-1)
        h = ef @ W1 + b1
        mu = jnp.mean(h, axis=0)
        var = jnp.mean((h - mu) ** 2, axis=0)
        h = (h - mu) * jax.lax.rsqrt(var + BN_EPS) * gamma + beta
        h = jax.nn.relu(h)
        msgs = h @ W2 + b2
        sums = jax.ops.segment_sum(msgs, row, num_segments=n_nodes)
        counts = jax.ops.segment_sum(jnp.ones((msgs.shape[0],), dtype=msgs.dtype), row, num_segments=n_nodes)
        out = sums / (counts + 1.0)[:, None]
        return out + x

    def _L3_gnn_ref(x, edge_index, edge_type, edge_weight, W, W0, num_nodes):
        import jax, jax.numpy as jnp
        import numpy as np
        N_NODES = 3125
        N_EDGES = 50000
        IN_DIM = 128
        OUT_DIM = 128
        N_REL = 8
        src, dst = (edge_index[0], edge_index[1])
        out = x @ W0
        h = jnp.einsum('nd,rdo->rno', x, W)
        msg = h[edge_type, src] * edge_weight[:, None]
        out = out + jax.ops.segment_sum(msg, dst, num_segments=num_nodes)
        deg = jax.ops.segment_sum(jnp.ones_like(edge_weight), dst, num_segments=num_nodes)
        deg = jnp.maximum(deg, 1.0)
        return out / deg[:, None]
    edge_index = jnp.stack([src, dst])
    x = _layernorm(x + _L0_gnn_ref(x, src, dst, L0_gnn_W_neigh, L0_gnn_b_neigh), axis=-1)
    x = _layernorm(x + _L1_gnn_ref(x, edge_index, edge_type_4, L1_gnn_sage1_Wl, L1_gnn_sage1_Wr, L1_gnn_sage1_b, L1_gnn_sage2_Wl, L1_gnn_sage2_Wr, L1_gnn_sage2_b, L1_gnn_gat_W, L1_gnn_gat_att_src, L1_gnn_gat_att_dst, L1_gnn_gat_b, L1_gnn_rgcn_Wrel, L1_gnn_rgcn_Wroot, L1_gnn_rgcn_b, L1_gnn_fusion_W, L1_gnn_fusion_b), axis=-1)
    x = _layernorm(x + _L2_gnn_ref(x, edge_index, edge_attr_2, L2_gnn_W1, L2_gnn_b1, L2_gnn_gamma, L2_gnn_beta, L2_gnn_W2, L2_gnn_b2), axis=-1)
    x = _layernorm(x + _L3_gnn_ref(x, edge_index, edge_type_8, edge_weight, L3_gnn_W, L3_gnn_W0, 6250), axis=-1)
    return x

_drawn_inputs = setup_inputs


def setup_inputs(seed=0):
    import zlib

    import numpy as np

    out = dict(_drawn_inputs(seed))
    spreads = {'L1_gnn_sage1_b': (0.0, 0.698),
     'L1_gnn_sage2_b': (0.0, 0.48),
     'L1_gnn_gat_b': (0.0, 0.354),
     'L1_gnn_rgcn_b': (0.0, 1.382),
     'L1_gnn_fusion_b': (0.0, 0.823),
     'L2_gnn_gamma': (1.0, 0.2),
     'L2_gnn_beta': (0.0, 0.287)}
    factors = {'edge_attr_2': 8.0,
     'edge_weight': 3.503,
     'L1_gnn_sage1_Wl': 11.003,
     'L1_gnn_gat_att_src': 51.406,
     'L1_gnn_gat_att_dst': 64.0,
     'L1_gnn_rgcn_Wroot': 4.386,
     'L2_gnn_b1': 64.0,
     'L2_gnn_b2': 8.0,
     'L3_gnn_W0': 3.934,
     'L1_gnn_sage1_Wr': 3.087}
    for name, (base, spread) in spreads.items():
        noise = np.random.default_rng([zlib.crc32(name.encode()), seed]).standard_normal(out[name].shape)
        drawn = base * np.exp(spread * noise) if base else spread * noise
        out[name] = jnp.asarray(drawn.astype(out[name].dtype))
    for name, factor in factors.items():
        out[name] = (out[name] * factor).astype(out[name].dtype)
    return out
```

```python
from contextlib import ExitStack

import numpy as np

import concourse.bass as bass
from concourse import mybir

F32 = mybir.dt.float32
I32 = mybir.dt.int32
ALU = mybir.AluOpType
ACT = mybir.ActivationFunctionType
AX = mybir.AxisListType
DVE = mybir.EngineType.DVE
SP = mybir.EngineType.SP

P = 128
NODES, EDGES = 6250, 106250
C = 128
H = 256
R4, R8 = 4, 8
NT = -(-NODES // P)
GN = 7
NG = NT // GN
GW = GN * P
ROWS = NT * P
TAIL = NODES - (NT - 1) * P
U = 16
HU = U // 2
QU = 4
QUADS = U // QU
ITERS = -(-EDGES // (P * U))
T = ITERS * U
EB = -(-T // P)
TP = EB * P
FULL = EDGES // P
REST = EDGES - FULL * P
ACCW = 6400
COPIES = 8
SW = C + 1
SROWS = ROWS + P
BIG = 1e30
EPS = 1e-5
assert NT == NG * GN and EB * P >= T + HU and NODES + P <= ACCW


def chain(engine, m):
    def link(instruction):
        m.steps += 1
        instruction.then_inc(m.step, 1)
        engine.wait_ge(m.step, m.steps)
    return link


class LoopChain:
    def __init__(self, engine, sem, g, per):
        self.engine, self.sem, self.g, self.per, self.n = engine, sem, g, per, 0

    def __call__(self, instruction):
        self.n += 1
        assert self.n <= self.per
        instruction.then_inc(self.sem, 1)
        self.engine.wait_ge(self.sem, self.g * self.per + self.n)

    def end(self):
        assert self.n == self.per, (self.n, self.per)


def place(nc, ctx, phase):
    def sb(name, shape, dt=F32):
        return ctx.enter_context(nc.sbuf_tensor(f"{phase}_{name}", shape, dt))

    def pb(name, shape):
        return ctx.enter_context(nc.psum_tensor(f"{phase}_{name}", shape, F32))

    def sem(*names):
        made = [nc.alloc_semaphore(f"{phase}_{n}") for n in names]
        return made if len(made) > 1 else made[0]
    return sb, pb, sem


def node_rows(table, g, width):
    return table[bass.ds(g * GW, GW), 0:width].rearrange("(j p) f -> p j f", p=P)


def edge_blocks(array, b0, b1):
    return array[b0 * P * P:b1 * P * P].rearrange("(b t p) -> t b p", t=P, p=P)


def load_edge_rows(engine, tile, array, sem):
    last = FULL - (EB - 1) * P
    engine.dma_start(tile[:, 0:EB - 1, :], edge_blocks(array, 0, EB - 1)).then_inc(sem, 16)
    engine.dma_start(tile[0:last, EB - 1, :], array[(EB - 1) * P * P:FULL * P].rearrange("(t p) -> t p", p=P)).then_inc(sem, 16)
    engine.dma_start(tile[last:last + 1, EB - 1, 0:REST], array[FULL * P:EDGES].rearrange("(t p) -> t p", t=1)).then_inc(sem, 16)


def constants(nc, m, a):
    with ExitStack() as ctx:
        sb, _, sem = place(nc, ctx, "constants")
        ioted, loaded, cleared, zeros_ready = sem("ioted", "loaded", "cleared", "zeros_ready")
        iota_i, col_i = sb("iota_i", [P, P], I32), sb("col_i", [P, 1], I32)
        zeros = sb("zeros", [P, (SROWS // P) * SW])
        block = ctx.enter_context(nc.Block())

        @block.gpsimd
        def _(pool):
            nc.gpsimd.iota(iota_i[:], pattern=[[1, P]], base=0, channel_multiplier=0).then_inc(ioted, 1)
            nc.gpsimd.iota(col_i[:], pattern=[[1, 1]], base=0, channel_multiplier=1).then_inc(ioted, 1)

        @block.vector
        def _(dve):
            nc.vector.memset(zeros[:], 0.0).then_inc(zeros_ready, 1)
            nc.vector.memset(m.x[:], 0.0).then_inc(zeros_ready, 1)
            dve.wait_ge(ioted, 2)
            link = chain(dve, m)
            link(nc.vector.tensor_copy(m.iota[:], iota_i[:]))
            link(nc.vector.tensor_copy(m.column[:], col_i[:]))
            link(nc.vector.tensor_scalar(m.ident[:], m.iota[:], m.column[:], None, ALU.is_equal))
            link(nc.vector.tensor_scalar(m.before[:], m.iota[:], m.column[:], None, ALU.is_lt))
            link(nc.vector.memset(m.ones[:], 1.0))
            link(nc.vector.memset(m.ones_i[:], 1))
            link(nc.vector.memset(m.epsilon[:], EPS))

        @block.sync
        def _(sp):
            sp.wait_ge(zeros_ready, 2)
            sp.dma_start(m.x[:, 0:NT - 1, :], a["x"][0:(NT - 1) * P, :].rearrange("(j p) f -> p j f", p=P)).then_inc(loaded, 16)
            sp.dma_start(m.x[0:TAIL, NT - 1, :], a["x"][(NT - 1) * P:NODES, :]).then_inc(loaded, 16)
            for k in range(COPIES):
                sp.dma_start(m.scatter[k].rearrange("(p r) w -> p (r w)", p=P), zeros[:]).then_inc(cleared, 16)
            sp.dma_start(m.t_q[ROWS:ACCW, :], zeros[:, 0:C]).then_inc(cleared, 16)
            sp.dma_start(m.t_al[ROWS:ACCW, :], zeros[:, 0:4]).then_inc(cleared, 16)
            sp.wait_ge(loaded, 32)
            sp.wait_ge(cleared, 16 * (COPIES + 2))


class Segments:
    def __init__(self, nc, ctx, phase, q):
        sb, _, _ = place(nc, ctx, phase)
        self.dst_i, self.dst = sb("dst_i", [P, EB, P], I32), sb("dst_rows", [P, EB, P])
        self.same_prev, self.same_next = sb("same_prev", [P, EB, P]), sb("same_next", [P, EB, P])
        self.in_first, self.in_last = sb("in_first", [P, EB, P]), sb("in_last", [P, EB, P])
        self.ends = sb("ends", [P, EB, 2, q])
        self.first, self.last = sb("first_row", [q, TP]), sb("last_row", [q, TP])
        self.cont, self.whole = sb("cont", [q, TP]), sb("whole", [q, TP])
        self.run_in, self.run_out = sb("run_in", [q, TP]), sb("run_out", [q, TP])


def segment_masks(nc, m, a, s, phase, q):
    with ExitStack() as ctx:
        _, pb, sem = place(nc, ctx, phase)
        padded, loaded, turned, ends_ready = sem("padded", "loaded", "turned", "ends_ready")
        rows = pb("ends_rows", [q, 2, 1024])
        block = ctx.enter_context(nc.Block())

        @block.sync
        def _(sp):
            sp.wait_ge(padded, 1)
            load_edge_rows(sp, s.dst_i, a["dst"], loaded)
            sp.wait_ge(loaded, 48)

        @block.vector
        def _(dve):
            nc.vector.memset(s.dst_i[:], NODES).then_inc(padded, 1)
            link = chain(dve, m)
            dve.wait_ge(padded, 1)
            dve.wait_ge(loaded, 48)
            link(nc.vector.tensor_copy(s.dst[:], s.dst_i[:]))
            d = s.dst
            link(nc.vector.memset(s.same_prev[:], 0.0))
            link(nc.vector.memset(s.same_next[:], 0.0))
            link(nc.vector.tensor_tensor(s.same_prev[:, :, 1:P], d[:, :, 1:P], d[:, :, 0:P - 1], ALU.is_equal))
            link(nc.vector.tensor_tensor(s.same_next[:, :, 0:P - 1], d[:, :, 1:P], d[:, :, 0:P - 1], ALU.is_equal))
            link(nc.vector.tensor_tensor(s.in_first[:], d[:], d[:, :, 0:1].to_broadcast([P, EB, P]), ALU.is_equal))
            link(nc.vector.tensor_tensor(s.in_last[:], d[:], d[:, :, P - 1:P].to_broadcast([P, EB, P]), ALU.is_equal))
            nc.vector.tensor_copy(s.ends[:, :, 0, :], d[:, :, 0:1].to_broadcast([P, EB, q])).then_inc(ends_ready, 1)
            nc.vector.tensor_copy(s.ends[:, :, 1, :], d[:, :, P - 1:P].to_broadcast([P, EB, q])).then_inc(ends_ready, 1)
            link(nc.vector.memset(s.cont[:], 0.0))
            link(nc.vector.memset(s.run_in[:], 0.0))
            dve.wait_ge(turned, 2 * EB)
            link(nc.vector.tensor_copy(s.first[:], rows[:, 0, 0:TP]))
            link(nc.vector.tensor_copy(s.last[:], rows[:, 1, 0:TP]))
            link(nc.vector.tensor_tensor(s.cont[:, 1:TP], s.first[:, 1:TP], s.last[:, 0:TP - 1], ALU.is_equal))
            link(nc.vector.tensor_tensor(s.whole[:], s.first[:], s.last[:], ALU.is_equal))
            link(nc.vector.tensor_tensor(s.run_in[:, 1:TP], s.cont[:, 1:TP], s.whole[:, 0:TP - 1], ALU.mult))
            link(nc.vector.memset(s.run_out[:], 0.0))
            link(nc.vector.tensor_tensor(s.run_out[:, 0:TP - 1], s.cont[:, 1:TP], s.whole[:, 1:TP], ALU.mult))

        @block.tensor
        def _(pe):
            pe.wait_ge(ends_ready, 2)
            for b in range(EB):
                for k in range(2):
                    nc.tensor.transpose(rows[:, k, b * P:(b + 1) * P], s.ends[:, b, k, :], m.ident[:]).then_inc(turned, 1)


def segment_totals(nc, m, s, phase, values, total, q, maximum=False):
    with ExitStack() as ctx:
        sb, pb, sem = place(nc, ctx, phase)
        tips_ready, turned, carries_ready, returned = sem("tips_ready", "turned", "carries_ready", "returned")
        back = sb("back", [P, q, EB, P])
        mask = sb("mask", [P, EB, P])
        carry = sb("carry", [q, 2, TP])
        gate, inflow = sb("gate", [q, TP]), sb("inflow", [q, TP])
        tips, carried = sb("tips", [P, EB, 2, q]), sb("carried", [P, EB, 2, q])
        rows = pb("tip_rows", [q, 2, 1024])
        cols = pb("carry_cols", [P, EB, 2, q])
        block = ctx.enter_context(nc.Block())
        join = ALU.max if maximum else ALU.add
        decay = ALU.add if maximum else ALU.mult
        flat = lambda t: t.rearrange("p b e -> p (b e)")

        @block.vector
        def _(dve):
            link = chain(dve, m)

            def gates(out, keep):
                if maximum:
                    link(nc.vector.tensor_scalar(out, keep, 1.0, BIG, ALU.subtract, ALU.mult))
                else:
                    link(nc.vector.tensor_copy(out, keep))

            gates(mask[:], s.same_prev[:])
            for k in range(q):
                link(nc.vector.tensor_tensor_scan(flat(total[:, k]), flat(mask[:]), flat(values[:, k]),
                                                  -BIG if maximum else 0.0, decay, join))
            gates(mask[:], s.same_next[:])
            for k in range(q):
                link(nc.vector.tensor_tensor_scan(flat(back[:, k])[:, ::-1], flat(mask[:])[:, ::-1], flat(values[:, k])[:, ::-1],
                                                  -BIG if maximum else 0.0, decay, join))
            link(nc.vector.tensor_copy(tips[:, :, 0, :].rearrange("p b q -> p q b"), total[:, :, :, P - 1]))
            nc.vector.tensor_copy(tips[:, :, 1, :].rearrange("p b q -> p q b"), back[:, :, :, 0]).then_inc(tips_ready, 1)
            if maximum:
                link(nc.vector.tensor_tensor(total[:], total[:], back[:], ALU.max))
            else:
                dve.wait_ge(tips_ready, 1)
                link(nc.vector.tensor_tensor(back[:], back[:], values[:], ALU.subtract))
                link(nc.vector.tensor_tensor(total[:], total[:], back[:], ALU.add))
            dve.wait_ge(turned, 2 * EB)
            link(nc.vector.memset(inflow[:], -BIG if maximum else 0.0))
            if maximum:
                gates(gate[:], s.cont[:])
                link(nc.vector.tensor_tensor(inflow[:, 1:TP], rows[:, 0, 0:TP - 1], gate[:, 1:TP], ALU.add))
            else:
                link(nc.vector.tensor_tensor(inflow[:, 1:TP], rows[:, 0, 0:TP - 1], s.cont[:, 1:TP], ALU.mult))
            gates(gate[:], s.run_in[:])
            link(nc.vector.tensor_tensor_scan(carry[:, 0], gate[:], inflow[:], -BIG if maximum else 0.0, decay, join))
            link(nc.vector.memset(inflow[:], -BIG if maximum else 0.0))
            if maximum:
                gates(gate[:], s.cont[:])
                link(nc.vector.tensor_tensor(inflow[:, 0:TP - 1], rows[:, 1, 1:TP], gate[:, 1:TP], ALU.add))
            else:
                link(nc.vector.tensor_tensor(inflow[:, 0:TP - 1], rows[:, 1, 1:TP], s.cont[:, 1:TP], ALU.mult))
            gates(gate[:], s.run_out[:])
            nc.vector.tensor_tensor_scan(carry[:, 1, ::-1], gate[:, ::-1], inflow[:, ::-1],
                                         -BIG if maximum else 0.0, decay, join).then_inc(carries_ready, 1)
            dve.wait_ge(returned, 2 * EB)
            link(nc.vector.tensor_copy(carried[:], cols[:]))
            for k in range(2):
                inside = s.in_first if k == 0 else s.in_last
                gates(mask[:], inside[:])
                for j in range(q):
                    per_tile = carried[:, :, k, j:j + 1].to_broadcast([P, EB, P])
                    link(nc.vector.tensor_tensor(back[:, j], mask[:], per_tile, ALU.add if maximum else ALU.mult))
                    link(nc.vector.tensor_tensor(total[:, j], total[:, j], back[:, j], join))

        @block.tensor
        def _(pe):
            pe.wait_ge(tips_ready, 1)
            for b in range(EB):
                for k in range(2):
                    nc.tensor.transpose(rows[:, k, b * P:(b + 1) * P], tips[:, b, k, :], m.ident[:]).then_inc(turned, 1)
            pe.wait_ge(carries_ready, 1)
            for b in range(EB):
                for k in range(2):
                    nc.tensor.transpose(cols[:, b, k, :], carry[:, k, b * P:(b + 1) * P], m.ident[0:q, 0:q]).then_inc(returned, 1)


def turn_edges(nc, m, phase, pairs):
    with ExitStack() as ctx:
        _, pb, sem = place(nc, ctx, phase)
        turned, kept = sem("turned", "kept")
        ps = [pb(f"turn{k}", [P, 4, P]) for k in range(4)]
        block = ctx.enter_context(nc.Block())
        work = [(source, target, b, min(4, EB - b)) for source, target in pairs for b in range(0, EB, 4)]

        @block.tensor
        def _(pe):
            for n, (source, _, b, count) in enumerate(work):
                if n >= 4:
                    pe.wait_ge(kept, n - 3)
                for k in range(count):
                    last = nc.tensor.transpose(ps[n % 4][:, k, :], source[:, b + k, :], m.ident[:])
                last.then_inc(turned, 1)

        @block.vector
        def _(dve):
            for n, (_, target, b, count) in enumerate(work):
                dve.wait_ge(turned, n + 1)
                nc.vector.tensor_copy(target[:, b:b + count, :], ps[n % 4][:, 0:count, :]).then_inc(kept, 1)


def by_block(t):
    return t.rearrange("p (b t) -> p b t", t=P)


def edge_setup(nc, m, a):
    with ExitStack() as ctx:
        sb, _, _ = place(nc, ctx, "setup")
        s = Segments(nc, ctx, "setup_masks", R4)
        segment_masks(nc, m, a, s, "setup_masks", R4)
        kind = sb("kind", [P, R4, EB, P])
        count = sb("count", [P, R4, EB, P])
        ints = sb("ints", [P, 3, EB, P])
        src_key = sb("src_key", [P, EB, P])
        rel = sb("rel", [P, EB, P])
        weight = sb("weight", [P, EB, P])
        with ExitStack() as inner:
            sb, _, sem = place(nc, inner, "setup_load")
            padded, loaded, split, keyed, kept = sem("padded", "loaded", "split", "keyed", "kept")
            raw = sb("raw", [P, 3, EB, P], I32)
            ea = sb("ea", [P, EB, 2 * P])
            ea2 = sb("ea2", [P, 2, EB, P])
            block = inner.enter_context(nc.Block())

            @block.sync
            def _(sp):
                sp.wait_ge(padded, 3)
                load_edge_rows(sp, raw[:, 0], a["src"], loaded)
                load_edge_rows(sp, raw[:, 1], a["edge_type_4"], loaded)
                load_edge_rows(sp, raw[:, 2], a["edge_type_8"], loaded)
                load_edge_rows(sp, weight, a["edge_weight"], loaded)
                flat = a["edge_attr_2"].rearrange("e k -> (e k)")
                last = FULL - (EB - 1) * P
                full, most = FULL * P * 2, (EB - 1) * P * P * 2
                sp.dma_start(ea[:, 0:EB - 1, :], flat[0:most].rearrange("(b t p) -> t b p", t=P, p=2 * P)).then_inc(loaded, 16)
                sp.dma_start(ea[0:last, EB - 1, :], flat[most:full].rearrange("(t p) -> t p", p=2 * P)).then_inc(loaded, 16)
                sp.dma_start(ea[last:last + 1, EB - 1, 0:2 * REST], flat[full:2 * EDGES].rearrange("(t p) -> t p", t=1)).then_inc(loaded, 16)
                sp.wait_ge(split, 3)
                for k in range(2):
                    sp.dma_start(m.t_ea[k].rearrange("(b t p) -> t b p", t=P, p=P), ea2[:, k]).then_inc(kept, 16)
                sp.wait_ge(keyed, 1)
                sp.dma_start(m.t_src.rearrange("(b t p) -> t b p", t=P, p=P), src_key[:]).then_inc(kept, 16)
                sp.wait_ge(kept, 48)

            @block.vector
            def _(dve):
                nc.vector.memset(raw[:], 0).then_inc(padded, 1)
                nc.vector.memset(weight[:], 0.0).then_inc(padded, 1)
                nc.vector.memset(ea[:], 0.0).then_inc(padded, 1)
                dve.wait_ge(padded, 3)
                dve.wait_ge(loaded, 16 * 15)
                link = chain(dve, m)
                nc.vector.tensor_copy(ints[:], raw[:]).then_inc(split, 1)
                for k in range(2):
                    nc.vector.tensor_copy(ea2[:, k], ea[:].rearrange("t b (p k) -> t k b p", k=2)[:, k]).then_inc(split, 1)
                dve.wait_ge(split, 3)
                for r in range(R4):
                    link(nc.vector.tensor_scalar(kind[:, r], ints[:, 1], float(r), None, ALU.is_equal))
                valid = count[:, 0]
                link(nc.vector.tensor_scalar(valid, s.dst[:], float(NODES), None, ALU.is_lt))
                link(nc.vector.tensor_tensor(rel[:], s.dst[:], s.dst[:, :, 0:1].to_broadcast([P, EB, P]), ALU.subtract))
                link(nc.vector.scalar_tensor_tensor(rel[:], rel[:], 1.0, valid, ALU.add, ALU.mult))
                link(nc.vector.tensor_scalar(rel[:], rel[:], 1.0, None, ALU.subtract))
                link(nc.vector.scalar_tensor_tensor(src_key[:], ints[:, 0], 1.0, valid, ALU.add, ALU.mult))
                nc.vector.tensor_scalar(src_key[:], src_key[:], 1.0, None, ALU.subtract).then_inc(keyed, 1)
        segment_totals(nc, m, s, "setup_count", kind, count, R4)
        with ExitStack() as inner:
            _, pb, sem = place(nc, inner, "setup_index")
            turned = sem("turned")
            row = pb("base_row", [1, 1024])
            block = inner.enter_context(nc.Block())

            @block.vector
            def _(dve):
                link = chain(dve, m)
                link(nc.vector.tensor_tensor(kind[:], kind[:], count[:], ALU.mult))
                link(nc.vector.tensor_tensor(kind[:, 0:2], kind[:, 0:2], kind[:, 2:4], ALU.add))
                link(nc.vector.tensor_tensor(kind[:, 0], kind[:, 0], kind[:, 1], ALU.add))
                link(nc.vector.tensor_scalar(kind[:, 0], kind[:, 0], 1.0, None, ALU.max))
                link(nc.vector.reciprocal(kind[:, 3], kind[:, 0]))
                link(nc.vector.scalar_tensor_tensor(ints[:, 1], ints[:, 0], float(R4), ints[:, 1], ALU.mult, ALU.add))
                link(nc.vector.scalar_tensor_tensor(ints[:, 2], ints[:, 0], float(R8), ints[:, 2], ALU.mult, ALU.add))
                dve.wait_ge(turned, EB)
                link(nc.vector.tensor_copy(m.base[:], row[:, 0:TP]))

            @block.tensor
            def _(pe):
                for b in range(EB):
                    nc.tensor.transpose(row[:, b * P:(b + 1) * P], s.dst[:, b, 0:1], m.ident[:]).then_inc(turned, 1)
        turn_edges(nc, m, "setup_turn", [
            (ints[:, 0], by_block(m.src)), (src_key, by_block(m.src_key)), (ints[:, 1], by_block(m.src4)),
            (ints[:, 2], by_block(m.src8)), (rel, by_block(m.rel)), (kind[:, 3], by_block(m.w_rgcn)),
            (weight, by_block(m.w_edge))])


def bases(nc, m, t, engine):
    return nc.values_load_multi_w_load_instructions(
        m.base[0:1, bass.ds(t, HU)], engines=[engine], min_val=0, max_val=NODES,
        skip_runtime_bounds_check_because="a first destination is a node, or NODES in the padding")[1]


def aggregate(nc, m, phase, table, index, weights, blocks, clear=True, degree=False):
    e = m.edge
    heads = max(1, len(weights))
    row = heads * blocks * P
    outs = 2 if degree else blocks
    n = e.passes
    e.passes += 1
    hots0, e.hots = e.hots, e.hots + (T + HU) * heads
    half0, done0, used0, staged0 = n * ITERS, n * ITERS * (U - 2), n * T, n * 2 * ITERS
    with ExitStack() as ctx:
        sb, pb, sem = place(nc, ctx, phase)
        message = [sb(f"message{u}", [P, row]) for u in range(U)]
        hot = sb("hot", [P, U, heads * P])
        stage = [sb(f"index_stage{h}", [P, HU], I32) for h in range(2)]
        ps = [pb(f"window{k}", [P, outs, P]) for k in range(HU)]
        cleared = sem("cleared")
        block = ctx.enter_context(nc.Block())

        @block.scalar
        def _(act):
            with act.Fori(0, ITERS, 1) as it:
                for h in range(2):
                    act.wait_ge(e.half_used[h], half0 + it)
                    nc.scalar.copy(stage[h][:], index[:, bass.ds(it * U + h * HU, HU)]).then_inc(e.staged, 1)

        @block.gpsimd
        def _(pool):
            with pool.Fori(0, ITERS, 1) as it:
                for u in range(U):
                    h, k = divmod(u, HU)
                    if k == 0:
                        pool.wait_ge(e.carried, staged0 + it * 2 + h)
                        pool.wait_ge(e.staged, staged0 + it * 2 + h + 1)
                        nc.gpsimd.tensor_tensor(m.carrier[:], m.ones_i[:], m.ones_i[:], ALU.add).then_inc(e.carried, 1)
                    pool.indirect_dma_start(message[u][:], None, table,
                                            bass.IndirectOffsetOnAxis(ap=stage[h][:, k:k + 1], axis=0)).then_inc(e.gathered[u], 16)

        @block.vector
        def _(dve):
            def one_hot(t, u):
                for k in range(heads):
                    if weights:
                        ins = nc.vector.tensor_scalar(hot[:, u, k * P:(k + 1) * P], m.iota[:], m.rel[:, t], weights[k][:, t],
                                                      ALU.is_equal, ALU.mult)
                    else:
                        ins = nc.vector.tensor_scalar(hot[:, u, :], m.iota[:], m.rel[:, t], None, ALU.is_equal)
                    ins.then_inc(e.hot_ready, 1)

            if clear:
                nc.vector.memset(m.acc[:, 0:outs, :], 0.0).then_inc(cleared, 1)
                dve.wait_ge(cleared, 1)
            for u in range(HU):
                one_hot(slice(u, u + 1), u)
            with dve.Fori(0, ITERS, 1) as it:
                for u in range(U):
                    h, k = divmod(u, HU)
                    if k == 0:
                        dve.wait_ge(e.half_used[1 - h], half0 + it + h)
                        base = bases(nc, m, it * U + u, DVE)
                    one_hot(bass.ds(it * U + u + HU, 1), (u + HU) % U)
                    if k == HU - 1:
                        dve.wait_ge(e.half_used[h], half0 + it + 1)
                    else:
                        dve.wait_ge(e.window_ready, done0 + it * (U - 2) + u + 1 - h)
                    window = m.acc[:, 0:outs, bass.ds(base[k], P)]
                    nc.vector.tensor_tensor(window, window, ps[k][:], ALU.add).then_inc(e.window_used, 1)
                    dve.wait_ge(e.window_used, used0 + it * U + u + 1)

        @block.tensor
        def _(pe):
            with pe.Fori(0, ITERS, 1) as it:
                for u in range(U):
                    h, k = divmod(u, HU)
                    if k == 0:
                        pe.wait_ge(e.window_used, used0 + it * U + u)
                    pe.wait_ge(e.hot_ready, hots0 + (it * U + u + 1) * heads)
                    pe.wait_ge(e.gathered[u], 16 * (half0 + it + 1))
                    for b in range(blocks):
                        for j in range(heads):
                            f = (j * blocks + b) * P
                            last = nc.tensor.matmul(ps[k][:, b, :], message[u][:, f:f + P], hot[:, u, j * P:(j + 1) * P],
                                                    start=(j == 0), stop=(j == heads - 1))
                    if degree:
                        last = nc.tensor.matmul(ps[k][:, 1, :], m.ones[:], hot[:, u, :], start=True, stop=True)
                    last.then_inc(e.half_used[h] if k == HU - 1 else e.window_ready, 1)


def load_weights(nc, m, phase, loads):
    with ExitStack() as ctx:
        _, _, sem = place(nc, ctx, phase)
        loaded = sem("weights")
        block = ctx.enter_context(nc.Block())

        @block.sync
        def _(sp):
            for tile, source in loads:
                sp.dma_start(tile, source).then_inc(loaded, 16)
            sp.wait_ge(loaded, 16 * len(loads))


def row_of(vector):
    return vector.rearrange("(a n) -> a n", a=1)


def layer_norm(nc, dve, link, b, y, out):
    for j in range(GN):
        ins = nc.vector.bn_stats(b.stats[:, j, :], y[:, j, :])
        if j == GN - 1:
            link(ins)
        else:
            ins.then_inc(b.stat_ready, 1)
    dve.wait_ge(b.stat_ready, b.g * (GN - 1) + GN - 1)
    nc.vector.memset(b.spare[:], 0.0)
    for j in range(GN):
        ins = nc.vector.bn_aggr(b.moments[:, j, :], b.stats[:, j, :])
        ins.then_inc(b.var_ready, 1)
    dve.wait_ge(b.root_ready, b.g + 1)
    link(nc.vector.reciprocal(b.rstd[:], b.root[:]))
    for j in range(GN):
        ins = nc.vector.tensor_scalar(out[:, j, :], y[:, j, :], b.moments[:, j, 0:1], b.rstd[:, j:j + 1], ALU.subtract, ALU.mult)
        ins.then_inc(b.norm_ready, 1)


def layer_norm_root(nc, act, m, b):
    act.wait_ge(b.var_ready, (b.g + 1) * GN)
    nc.scalar.activation(b.root[:], b.moments[:, :, 1], ACT.Sqrt, bias=m.epsilon[:], scale=1.0).then_inc(b.root_ready, 1)


class NormBuffers:
    def __init__(self, sb, sem):
        self.g = None
        self.stats, self.moments = sb("stats", [P, GN, 6]), sb("moments", [P, GN, 2])
        self.root, self.rstd, self.spare = sb("root", [P, GN]), sb("rstd", [P, GN]), sb("spare", [P, 1])
        self.stat_ready, self.var_ready, self.root_ready, self.norm_ready = sem("stat_ready", "var_ready", "root_ready", "norm_ready")


def degrees(nc, m):
    with ExitStack() as ctx:
        sb, _, _ = place(nc, ctx, "degrees")
        ends = sb("ends", [P, NT, P])
        block = ctx.enter_context(nc.Block())
        degree = m.acc[:, 1, 0:ROWS]

        @block.vector
        def _(dve):
            link = chain(dve, m)
            flat = ends[:].rearrange("p j n -> p (j n)")
            diagonal = m.ident[:].rearrange("p (j n) -> p j n", j=1).to_broadcast([P, NT, P])
            link(nc.vector.tensor_tensor_scan(flat, degree, degree, 0.0, ALU.add, ALU.max))
            link(nc.vector.tensor_tensor(ends[:], ends[:], diagonal, ALU.mult))
            link(nc.vector.tensor_reduce(m.last_edge_f[:], ends[:], AX.X, ALU.add))
            link(nc.vector.tensor_scalar(m.last_edge_f[:], m.last_edge_f[:], 1.0, 0.0, ALU.subtract, ALU.max))
            link(nc.vector.tensor_copy(m.last_edge[:], m.last_edge_f[:]))
            link(nc.vector.tensor_tensor(ends[:], degree.rearrange("p (j n) -> p j n", n=P), diagonal, ALU.mult))
            link(nc.vector.tensor_reduce(m.has_edges[:], ends[:], AX.X, ALU.add))
            link(nc.vector.tensor_scalar(m.has_edges[:], m.has_edges[:], 1.0, None, ALU.min))
            link(nc.vector.tensor_scalar(m.inv_degree[:], degree, 1.0, None, ALU.max))
            link(nc.vector.reciprocal(m.inv_degree[:], m.inv_degree[:]))


def group_cols(g):
    return bass.ds(g * GW, GW)


def group_tiles(g):
    return bass.ds(g * GN, GN)


def after_block0(nc, m, a):
    with ExitStack() as ctx:
        sb, pb, sem = place(nc, ctx, "n0")
        w_in, w_t = sb("w_in", [P, C]), sb("w_t", [P, C])
        bias = sb("bias", [1, C])
        load_weights(nc, m, "n0_load", [(w_in[:], a["L0_gnn_W_neigh"]), (bias[:], row_of(a["L0_gnn_b_neigh"]))])
        mean = sb("mean", [P, GN, P])
        y = sb("y", [P, GN, C])
        ps_w, ps = pb("ps_w", [P, C]), pb("ps", [P, 8, C])
        b = NormBuffers(sb, sem)
        w_turned, w_ready, staged, made, taken, steps, stored = sem("w_turned", "w_ready", "staged", "made", "taken", "steps", "stored")
        block = ctx.enter_context(nc.Block())

        @block.tensor
        def _(pe):
            nc.tensor.transpose(ps_w[:], w_in[:], m.ident[:]).then_inc(w_turned, 1)
            pe.wait_ge(w_ready, 1)
            with pe.Fori(0, NG, 1) as g:
                pe.wait_ge(staged, g + 1)
                pe.wait_ge(taken, g)
                for j in range(GN):
                    nc.tensor.matmul(ps[:, j, :], m.ones[0:1, :], bias[:], start=True, stop=False)
                    last = nc.tensor.matmul(ps[:, j, :], mean[:, j, :], w_t[:], start=False, stop=True)
                last.then_inc(made, 1)

        @block.scalar
        def _(act):
            with act.Fori(0, NG, 1) as g:
                b.g = g
                layer_norm_root(nc, act, m, b)

        @block.vector
        def _(dve):
            dve.wait_ge(w_turned, 1)
            nc.vector.tensor_copy(w_t[:], ps_w[:]).then_inc(w_ready, 1)
            with dve.Fori(0, NG, 1) as g:
                b.g = g
                link = LoopChain(dve, steps, g, 2)
                dve.wait_ge(made, g)
                nc.vector.tensor_tensor(mean[:].rearrange("p j n -> p (j n)"), m.acc[:, 0, group_cols(g)],
                                        m.inv_degree[:, group_cols(g)], ALU.mult).then_inc(staged, 1)
                dve.wait_ge(made, g + 1)
                dve.wait_ge(b.norm_ready, g * GN)
                nc.vector.tensor_tensor(y[:], ps[:, 0:GN, :], m.x[:, group_tiles(g), :], ALU.add).then_inc(taken, 1)
                dve.wait_ge(taken, g + 1)
                layer_norm(nc, dve, link, b, y, m.x[:, group_tiles(g), :])
                link.end()

        @block.sync
        def _(sp):
            with sp.Fori(0, NG, 1) as g:
                sp.wait_ge(b.norm_ready, (g + 1) * GN)
                sp.dma_start(node_rows(m.t_x, g, C), m.x[:, group_tiles(g), :]).then_inc(stored, 16)
            sp.wait_ge(stored, 16 * NG)


def after_sage1(nc, m, a):
    with ExitStack() as ctx:
        sb, pb, sem = place(nc, ctx, "n1")
        wl, wr, bias = sb("wl", [P, H]), sb("wr", [P, H]), sb("bias", [1, H])
        load_weights(nc, m, "n1_load", [(wl[:], a["L1_gnn_sage1_Wl"]), (wr[:], a["L1_gnn_sage1_Wr"]), (bias[:], row_of(a["L1_gnn_sage1_b"]))])
        mean, x, x_t = sb("mean", [P, GN, P]), sb("x", [P, GN, P]), sb("x_t", [P, GN, P])
        out = sb("out", [P, GN, H])
        ps_t, ps = pb("ps_t", [P, 8, P]), pb("ps", [P, 8, H])
        staged, copied, turned, kept, made, taken, stored = sem("staged", "copied", "turned", "kept", "made", "taken", "stored")
        block = ctx.enter_context(nc.Block())

        @block.scalar
        def _(act):
            with act.Fori(0, NG, 1) as g:
                act.wait_ge(turned, g)
                nc.scalar.copy(x[:], m.x[:, group_tiles(g), :]).then_inc(copied, 1)
                act.wait_ge(made, g + 1)
                act.wait_ge(stored, 16 * g)
                nc.scalar.activation(out[:], ps[:, 0:GN, :], ACT.Relu).then_inc(taken, 1)

        @block.vector
        def _(dve):
            with dve.Fori(0, NG, 1) as g:
                dve.wait_ge(made, g)
                nc.vector.tensor_tensor(mean[:].rearrange("p j n -> p (j n)"), m.acc[:, 0, group_cols(g)],
                                        m.inv_degree[:, group_cols(g)], ALU.mult).then_inc(staged, 1)
                dve.wait_ge(turned, g + 1)
                nc.vector.tensor_copy(x_t[:], ps_t[:, 0:GN, :]).then_inc(kept, 1)

        @block.tensor
        def _(pe):
            with pe.Fori(0, NG, 1) as g:
                pe.wait_ge(copied, g + 1)
                for j in range(GN):
                    last = nc.tensor.transpose(ps_t[:, j, :], x[:, j, :], m.ident[:])
                last.then_inc(turned, 1)
                pe.wait_ge(staged, g + 1)
                pe.wait_ge(kept, g + 1)
                pe.wait_ge(taken, g)
                for j in range(GN):
                    nc.tensor.matmul(ps[:, j, :], m.ones[0:1, :], bias[:], start=True, stop=False)
                    nc.tensor.matmul(ps[:, j, :], mean[:, j, :], wl[:], start=False, stop=False)
                    last = nc.tensor.matmul(ps[:, j, :], x_t[:, j, :], wr[:], start=False, stop=True)
                last.then_inc(made, 1)

        @block.sync
        def _(sp):
            with sp.Fori(0, NG, 1) as g:
                sp.wait_ge(taken, g + 1)
                sp.dma_start(node_rows(m.t_s1, g, H), out[:]).then_inc(stored, 16)
            sp.wait_ge(stored, 16 * NG)


def attention_weights(nc, m, a, phase, w, w_al):
    with ExitStack() as ctx:
        sb, _, sem = place(nc, ctx, phase)
        att = sb("att", [P, 2, 2 * H])
        product = sb("product", [P, 2, H])
        loaded = sem("loaded")
        block = ctx.enter_context(nc.Block())

        @block.sync
        def _(sp):
            for k, vectors in enumerate((a["L1_gnn_gat_att_src"], a["L1_gnn_gat_att_dst"])):
                row = vectors.rearrange("(a h) c -> a (h c)", a=1)
                sp.dma_start(att[:, k, :], row.to_broadcast([P, 2 * H])).then_inc(loaded, 16)
            sp.wait_ge(loaded, 32)

        @block.vector
        def _(dve):
            link = chain(dve, m)
            dve.wait_ge(loaded, 32)
            for k in range(2):
                for b in range(2):
                    link(nc.vector.tensor_tensor(product[:].rearrange("p h c -> p (h c)"), w[:, b, :], att[:, k, :], ALU.mult))
                    link(nc.vector.tensor_reduce(w_al[:, b, 2 * k:2 * k + 2], product[:], AX.X, ALU.add))


def by_half(weights):
    return weights.rearrange("(b k) n -> k b n", k=P)


def after_sage2(nc, m, a):
    FA = C + 4
    with ExitStack() as ctx:
        sb, pb, sem = place(nc, ctx, "n2")
        wl, wr, wg = sb("wl", [P, 2, H]), sb("wr", [P, 2, H]), sb("wg", [P, 2, 2 * H])
        wf, w_al = sb("wf", [P, 2, C]), sb("w_al", [P, 2, 4])
        bias, bias_f = sb("bias", [1, H]), sb("bias_f", [1, C])
        load_weights(nc, m, "n2_load", [
            (wl[:], by_half(a["L1_gnn_sage2_Wl"])), (wr[:], by_half(a["L1_gnn_sage2_Wr"])), (wg[:], by_half(a["L1_gnn_gat_W"])),
            (wf[:], by_half(a["L1_gnn_fusion_W"][0:H, :])), (bias[:], row_of(a["L1_gnn_sage2_b"])), (bias_f[:], row_of(a["L1_gnn_fusion_b"]))])
        attention_weights(nc, m, a, "n2_att", wg, w_al)
        mean = sb("mean", [P, 2, GN, P])
        s1, s2 = sb("s1", [P, GN, H]), sb("s2", [P, GN, H])
        turned_rows = sb("turned_rows", [P, 2, GN, P])
        h_out, fa_out = sb("h_out", [P, GN, 2 * H]), sb("fa_out", [P, GN, FA])
        ps_t, ps = pb("ps_t", [P, 4, 512]), pb("ps", [P, 4, 512])
        loaded, staged, turned1, kept1, made, relued, turned2, kept2, fa_made, fa_taken, h_made, h_taken, stored = sem(
            "loaded", "staged", "turned1", "kept1", "made", "relued", "turned2", "kept2", "fa_made", "fa_taken", "h_made", "h_taken", "stored")
        block = ctx.enter_context(nc.Block())
        tile = lambda k, j: ps_t[:].rearrange("p b (s n) -> p (b s) n", n=P)[:, k * 8 + j, :]
        halves = ps_t[:].rearrange("p (k b) (s n) -> p k (b s) n", k=2, n=P)
        wide = ps[:].rearrange("p b (s n) -> p (b s) n", n=H)
        fa = ps_t[:].rearrange("p b (s n) -> p (b s) n", n=H)

        @block.sync
        def _(sp):
            with sp.Fori(0, NG, 1) as g:
                sp.wait_ge(turned1, g)
                sp.dma_start(s1[:], node_rows(m.t_s1, g, H)).then_inc(loaded, 16)
                sp.wait_ge(fa_taken, g + 1)
                sp.dma_start(node_rows(m.t_f, g, C), fa_out[:, :, 0:C]).then_inc(stored, 16)
                sp.dma_start(node_rows(m.t_al, g, 4), fa_out[:, :, C:FA]).then_inc(stored, 16)
                sp.wait_ge(h_taken, (g + 1) * GN)
                sp.dma_start(node_rows(m.t_h, g, 2 * H), h_out[:]).then_inc(stored, 16)
            sp.wait_ge(stored, 48 * NG)

        @block.vector
        def _(dve):
            with dve.Fori(0, NG, 1) as g:
                dve.wait_ge(made, g)
                for k in range(2):
                    nc.vector.tensor_tensor(mean[:, k].rearrange("p j n -> p (j n)"), m.acc[:, k, group_cols(g)],
                                            m.inv_degree[:, group_cols(g)], ALU.mult).then_inc(staged, 1)
                dve.wait_ge(fa_made, g + 1)
                dve.wait_ge(stored, 48 * g)
                nc.vector.tensor_copy(fa_out[:], fa[:, 0:GN, 0:FA]).then_inc(fa_taken, 1)
                for j in range(GN):
                    dve.wait_ge(h_made, g * GN + j + 1)
                    nc.vector.tensor_copy(h_out[:, j, :], ps[:, j % 4, :]).then_inc(h_taken, 1)

        @block.scalar
        def _(act):
            with act.Fori(0, NG, 1) as g:
                act.wait_ge(turned1, g + 1)
                act.wait_ge(h_made, g * GN)
                nc.scalar.copy(turned_rows[:], halves[:, :, 0:GN, :]).then_inc(kept1, 1)
                act.wait_ge(made, g + 1)
                nc.scalar.activation(s2[:], wide[:, 0:GN, :], ACT.Relu).then_inc(relued, 1)
                act.wait_ge(turned2, g + 1)
                nc.scalar.copy(turned_rows[:], halves[:, :, 0:GN, :]).then_inc(kept2, 1)

        @block.tensor
        def _(pe):
            with pe.Fori(0, NG, 1) as g:
                pe.wait_ge(loaded, 16 * (g + 1))
                pe.wait_ge(fa_taken, g)
                for j in range(GN):
                    for k in range(2):
                        last = nc.tensor.transpose(tile(k, j), s1[:, j, k * P:(k + 1) * P], m.ident[:])
                last.then_inc(turned1, 1)
                pe.wait_ge(staged, 2 * (g + 1))
                pe.wait_ge(kept1, g + 1)
                pe.wait_ge(h_taken, g * GN)
                for j in range(GN):
                    nc.tensor.matmul(wide[:, j, :], m.ones[0:1, :], bias[:], start=True, stop=False)
                    for k in range(2):
                        nc.tensor.matmul(wide[:, j, :], mean[:, k, j, :], wl[:, k, :], start=False, stop=False)
                        last = nc.tensor.matmul(wide[:, j, :], turned_rows[:, k, j, :], wr[:, k, :], start=False, stop=(k == 1))
                last.then_inc(made, 1)
                pe.wait_ge(relued, g + 1)
                for j in range(GN):
                    for k in range(2):
                        last = nc.tensor.transpose(tile(k, j), s2[:, j, k * P:(k + 1) * P], m.ident[:])
                last.then_inc(turned2, 1)
                pe.wait_ge(kept2, g + 1)
                for j in range(GN):
                    nc.tensor.matmul(fa[:, j, 0:C], m.ones[0:1, :], bias_f[:], start=True, stop=False)
                    for k in range(2):
                        nc.tensor.matmul(fa[:, j, 0:C], turned_rows[:, k, j, :], wf[:, k, :], start=False, stop=(k == 1))
                    for k in range(2):
                        last = nc.tensor.matmul(fa[:, j, C:FA], turned_rows[:, k, j, :], w_al[:, k, :], start=(k == 0), stop=(k == 1))
                last.then_inc(fa_made, 1)
                for j in range(GN):
                    if j >= 4:
                        pe.wait_ge(h_taken, g * GN + j - 3)
                    for k in range(2):
                        last = nc.tensor.matmul(ps[:, j % 4, :], turned_rows[:, k, j, :], wg[:, k, :], start=(k == 0), stop=(k == 1))
                    last.then_inc(h_made, 1)


class Window:
    def __init__(self, nc, sb, pb, sem, width):
        self.hot, self.hot_t = sb("hot", [P, U, P]), sb("hot_t", [P, U, P])
        self.rows = sb("rows", [P, U, width])
        self.ps_hot = [pb(f"ps_hot{k}", [P, QU, P]) for k in range(2)]
        self.loaded = [sem(f"window{u}") for u in range(U)]
        self.hot_ready, self.turned, self.kept, self.half = sem("hot_ready", "turned", "kept", "half")


def window_turn(nc, m, pe, w, it, q):
    pe.wait_ge(w.hot_ready, it * U + (q + 1) * QU)
    pe.wait_ge(w.kept, it * QUADS + max(q - 1, 0))
    for k in range(QU):
        last = nc.tensor.transpose(w.ps_hot[q % 2][:, k, :], w.hot[:, q * QU + k, :], m.ident[:])
    last.then_inc(w.turned, 1)


def window_keep(nc, act, w, it, q):
    act.wait_ge(w.turned, it * QUADS + q + 1)
    nc.scalar.copy(w.hot_t[:, q * QU:(q + 1) * QU, :], w.ps_hot[q % 2][:]).then_inc(w.kept, 1)


def window_hot(nc, m, dve, w, it):
    dve.wait_ge(w.turned, it * QUADS)
    for u in range(U):
        nc.vector.tensor_scalar(w.hot[:, u, :], m.iota[:], m.rel[:, bass.ds(it * U + u, 1)], None, ALU.is_equal).then_inc(w.hot_ready, 1)


def window_load(nc, m, sp, w, table, width, it, h):
    base = bases(nc, m, it * U + h * HU, SP)
    for k in range(HU):
        sp.dma_start(w.rows[:, h * HU + k, :], table[bass.ds(base[k], P), 0:width]).then_inc(w.loaded[h * HU + k], 16)


def attention_terms(nc, m):
    with ExitStack() as ctx:
        sb, pb, sem = place(nc, ctx, "al")
        w = Window(nc, sb, pb, sem, 4)
        source = [sb(f"source{h}", [P, HU, 4]) for h in range(2)]
        gathered = [sem(f"gathered{h}") for h in range(2)]
        stage = [sb(f"stage{h}", [P, HU], I32) for h in range(2)]
        at_dst = sb("at_dst", [P, 2, HU, 4])
        ps = [pb(f"ps{h}", [P, HU, 4]) for h in range(2)]
        staged, carried, copied, zeroed = sem("staged", "carried", "copied", "zeroed")
        looked = [sem(f"looked{h}") for h in range(2)]
        added = [sem(f"added{h}") for h in range(2)]
        block = ctx.enter_context(nc.Block())

        @block.sync
        def _(sp):
            with sp.Fori(0, ITERS, 1) as it:
                for h in range(2):
                    sp.wait_ge(looked[h], it)
                    window_load(nc, m, sp, w, m.t_al, 4, it, h)

        @block.gpsimd
        def _(pool):
            with pool.Fori(0, ITERS, 1) as it:
                for u in range(U):
                    h, k = divmod(u, HU)
                    if k == 0:
                        pool.wait_ge(carried, it * 2 + h)
                        pool.wait_ge(staged, it * 2 + h + 1)
                        nc.gpsimd.tensor_tensor(m.carrier[:], m.ones_i[:], m.ones_i[:], ALU.add).then_inc(carried, 1)
                    pool.indirect_dma_start(source[h][:, k, :], None, m.t_al[0:ROWS, :],
                                            bass.IndirectOffsetOnAxis(ap=stage[h][:, k:k + 1], axis=0)).then_inc(gathered[h], 16)

        @block.scalar
        def _(act):
            with act.Fori(0, ITERS, 1) as it:
                for h in range(2):
                    act.wait_ge(added[h], 2 * it)
                    nc.scalar.copy(stage[h][:], m.src[:, bass.ds(it * U + h * HU, HU)]).then_inc(staged, 1)
                for q in range(QUADS):
                    if q % 2 == 0:
                        act.wait_ge(looked[q // 2], it)
                    window_keep(nc, act, w, it, q)

        @block.vector
        def _(dve):
            nc.vector.memset(m.e[:], 0.0).then_inc(zeroed, 1)
            nc.vector.memset(m.e_self[:], 0.0).then_inc(zeroed, 1)
            dve.wait_ge(zeroed, 2)
            with dve.Fori(0, ITERS, 1) as it:
                window_hot(nc, m, dve, w, it)
                for h in range(2):
                    dve.wait_ge(looked[h], it + 1)
                    dve.wait_ge(added[h], 2 * it)
                    nc.vector.tensor_copy(at_dst[:, h], ps[h][:]).then_inc(copied, 1)
                    dve.wait_ge(copied, it * 2 + h + 1)
                    dve.wait_ge(gathered[h], (it + 1) * 16 * HU)
                    tiles = bass.ds(it * U + h * HU, HU)
                    nc.vector.tensor_tensor(m.e[:, :, tiles].rearrange("p k t -> p t k"), at_dst[:, h, :, 2:4],
                                            source[h][:, :, 0:2], ALU.add).then_inc(added[h], 1)
                    nc.vector.tensor_tensor(m.e_self[:, :, tiles].rearrange("p k t -> p t k"), at_dst[:, h, :, 2:4],
                                            at_dst[:, h, :, 0:2], ALU.add).then_inc(added[h], 1)

        @block.tensor
        def _(pe):
            def look_up(it, q):
                h = q // 2
                if q % 2 == 0:
                    pe.wait_ge(copied, it * 2 + h)
                pe.wait_ge(w.kept, it * QUADS + q + 1)
                for u in range(q * QU, (q + 1) * QU):
                    pe.wait_ge(w.loaded[u], (it + 1) * 16)
                    last = nc.tensor.matmul(ps[h][:, u % HU, :], w.hot_t[:, u, :], w.rows[:, u, :], start=True, stop=True)
                if q % 2 == 1:
                    last.then_inc(looked[h], 1)

            with pe.Fori(0, ITERS, 1) as it:
                for q in range(QUADS):
                    window_turn(nc, m, pe, w, it, q)
                    if q >= 1:
                        look_up(it, q - 1)
                look_up(it, QUADS - 1)


def attention_softmax(nc, m, a):
    with ExitStack() as ctx:
        sb, _, _ = place(nc, ctx, "softmax")
        s = Segments(nc, ctx, "softmax_masks", 2)
        segment_masks(nc, m, a, s, "softmax_masks", 2)
        e, own, top, total = (sb(n, [P, 2, EB, P]) for n in ("e", "own", "top", "total"))
        self_weight = sb("self_weight", [P, EB, P, 2])
        turn_edges(nc, m, "softmax_turn", [(by_block(m.e[:, k]), e[:, k]) for k in range(2)] + [(by_block(m.e_self[:, k]), own[:, k]) for k in range(2)])
        with ExitStack() as inner:
            block = inner.enter_context(nc.Block())

            @block.vector
            def _(dve):
                link = chain(dve, m)
                for t in (e, own):
                    link(nc.vector.tensor_scalar(total[:], t[:], 0.2, None, ALU.mult))
                    link(nc.vector.tensor_tensor(t[:], t[:], total[:], ALU.max))
        segment_totals(nc, m, s, "softmax_top", e, top, 2, maximum=True)
        with ExitStack() as inner:
            _, _, sem = place(nc, inner, "softmax_exp")
            shifted, raised = sem("shifted", "raised")
            block = inner.enter_context(nc.Block())

            @block.vector
            def _(dve):
                link = chain(dve, m)
                link(nc.vector.tensor_tensor(top[:], top[:], own[:], ALU.max))
                nc.vector.tensor_tensor(e[:], e[:], top[:], ALU.subtract).then_inc(shifted, 1)
                nc.vector.tensor_tensor(own[:], own[:], top[:], ALU.subtract).then_inc(shifted, 1)

            @block.scalar
            def _(act):
                for n, t in enumerate((e, own)):
                    act.wait_ge(shifted, n + 1)
                    nc.scalar.activation(t[:], t[:], ACT.Exp).then_inc(raised, 1)
                act.wait_ge(raised, 2)
        segment_totals(nc, m, s, "softmax_sum", e, total, 2)
        with ExitStack() as inner:
            sb, _, sem = place(nc, inner, "softmax_self")
            weighed, kept = sem("weighed", "kept")
            block = inner.enter_context(nc.Block())

            @block.vector
            def _(dve):
                link = chain(dve, m)
                link(nc.vector.tensor_tensor(total[:], total[:], own[:], ALU.add))
                link(nc.vector.tensor_scalar(total[:], total[:], 1e-16, None, ALU.max))
                link(nc.vector.reciprocal(top[:], total[:]))
                link(nc.vector.tensor_scalar(top[:], top[:], 0.5, None, ALU.mult))
                link(nc.vector.tensor_tensor(e[:], e[:], top[:], ALU.mult))
                nc.vector.tensor_tensor(self_weight[:].rearrange("p b t k -> p k b t"), own[:], top[:], ALU.mult).then_inc(weighed, 1)

            @block.sync
            def _(sp):
                sp.wait_ge(weighed, 1)
                sp.dma_start(m.t_self.rearrange("(b t p) k -> t b (p k)", t=P, p=P),
                             self_weight[:].rearrange("t b p k -> t b (p k)")).then_inc(kept, 16)
                sp.wait_ge(kept, 16)
        turn_edges(nc, m, "softmax_back", [(e[:, k], by_block(m.alpha[:, k])) for k in range(2)])
        with ExitStack() as inner:
            sb, _, sem = place(nc, inner, "softmax_nodes")
            got = sem("got")
            rows = sb("rows", [P, NT, 2])
            block = inner.enter_context(nc.Block())

            @block.gpsimd
            def _(pool):
                for j in range(NT):
                    pool.indirect_dma_start(rows[:, j, :], None, m.t_self,
                                            bass.IndirectOffsetOnAxis(ap=m.last_edge[:, j:j + 1], axis=0)).then_inc(got, 16)

            @block.vector
            def _(dve):
                link = chain(dve, m)
                dve.wait_ge(got, 16 * NT)
                link(nc.vector.tensor_scalar(rows[:], rows[:], 0.5, None, ALU.subtract))
                link(nc.vector.tensor_tensor(rows[:], rows[:], m.has_edges[:].rearrange("p (j k) -> p j k", k=1).to_broadcast([P, NT, 2]), ALU.mult))
                link(nc.vector.tensor_scalar(m.self_weight[:], rows[:], 0.5, None, ALU.add))


def after_gat(nc, m, a):
    with ExitStack() as ctx:
        sb, pb, sem = place(nc, ctx, "n3")
        wrel, wroot, wf = sb("wrel", [P, 2, R4, C]), sb("wroot", [P, 2, C]), sb("wf", [P, 2, C])
        bias, bias_root = sb("bias", [1, H]), sb("bias_root", [P, 1])
        load_weights(nc, m, "n3_load", [
            *[(wrel[:, k], a["L1_gnn_rgcn_Wrel"].rearrange("r (b k) n -> b k r n", k=P)[k]) for k in range(2)],
            (wroot[:], by_half(a["L1_gnn_rgcn_Wroot"])), (wf[:], by_half(a["L1_gnn_fusion_W"][H:2 * H, :])),
            (bias[:], row_of(a["L1_gnn_gat_b"])), (bias_root[:], a["L1_gnn_rgcn_b"].rearrange("(n a) -> n a", a=1))])
        sums = sb("sums", [P, 2, GN, P])
        h, f = sb("h", [P, GN, 2 * H]), sb("f", [P, GN, C])
        y = sb("y", [P, GN, H])
        y_t = sb("y_t", [P, 2, GN, P])
        ps_t, ps = pb("ps_t", [P, 4, 512]), pb("ps", [P, 4, 512])
        loaded, staged, made, partly, summed, relued, turned, kept, f_made, f_taken, root_made, root_taken, x_made, x_taken, stored = sem(
            "loaded", "staged", "made", "partly", "summed", "relued", "turned", "kept", "f_made", "f_taken", "root_made", "root_taken",
            "x_made", "x_taken", "stored")
        block = ctx.enter_context(nc.Block())
        tile = lambda k, j: ps_t[:].rearrange("p b (s n) -> p (b s) n", n=P)[:, k * 8 + j, :]
        halves = ps_t[:].rearrange("p (k b) (s n) -> p k (b s) n", k=2, n=P)
        quarter = ps_t[:].rearrange("p b (s n) -> p (b s) n", n=P)
        root = ps_t[:, 2:4, 0:GW // 2]
        wide = ps[:].rearrange("p b (s n) -> p (b s) n", n=H)

        @block.sync
        def _(sp):
            with sp.Fori(0, NG, 1) as g:
                sp.wait_ge(stored, 32 * g)
                sp.dma_start(h[:], node_rows(m.t_h, g, 2 * H)).then_inc(loaded, 16)
                sp.dma_start(f[:], node_rows(m.t_f, g, C)).then_inc(loaded, 16)
                sp.wait_ge(f_taken, g + 1)
                sp.dma_start(node_rows(m.t_f, g, C), f[:]).then_inc(stored, 16)
                sp.wait_ge(x_taken, (g + 1) * GN)
                sp.dma_start(node_rows(m.t_rel4, g, R4 * C), h[:]).then_inc(stored, 16)
            sp.wait_ge(stored, 32 * NG)

        @block.scalar
        def _(act):
            with act.Fori(0, NG, 1) as g:
                act.wait_ge(made, g)
                nc.scalar.copy(sums[:].rearrange("p k j n -> p k (j n)"), m.acc[:, 0:2, group_cols(g)]).then_inc(staged, 1)
                act.wait_ge(summed, (g + 1) * GN)
                nc.scalar.activation(y[:], y[:], ACT.Relu).then_inc(relued, 1)
                act.wait_ge(turned, g + 1)
                act.wait_ge(x_made, g * GN)
                nc.scalar.copy(y_t[:], halves[:, :, 0:GN, :]).then_inc(kept, 1)

        @block.vector
        def _(dve):
            with dve.Fori(0, NG, 1) as g:
                dve.wait_ge(loaded, 32 * (g + 1))
                dve.wait_ge(made, g + 1)
                dve.wait_ge(turned, g)
                for j in range(GN):
                    nc.vector.scalar_tensor_tensor(y[:, j, :], h[:, j, 0:H], m.self_weight[:, bass.ds(g * GN + j, 1), 0], wide[:, j, :],
                                                   ALU.mult, ALU.add).then_inc(partly, 1)
                dve.wait_ge(partly, (g + 1) * GN)
                for j in range(GN):
                    nc.vector.scalar_tensor_tensor(y[:, j, :], h[:, j, H:2 * H], m.self_weight[:, bass.ds(g * GN + j, 1), 1], y[:, j, :],
                                                   ALU.mult, ALU.add).then_inc(summed, 1)
                dve.wait_ge(f_made, g + 1)
                nc.vector.tensor_tensor(f[:], f[:], quarter[:, 0:GN, :], ALU.add).then_inc(f_taken, 1)
                dve.wait_ge(root_made, g + 1)
                nc.vector.tensor_scalar(m.acc[:, 0, group_cols(g)].rearrange("p (b n) -> p b n", b=2), root, bias_root[:], None,
                                        ALU.add).then_inc(root_taken, 1)
                dve.wait_ge(summed, (g + 1) * GN)
                for j in range(GN):
                    dve.wait_ge(x_made, g * GN + j + 1)
                    nc.vector.tensor_copy(h[:, j, :], ps[:, j % 4, :]).then_inc(x_taken, 1)

        @block.tensor
        def _(pe):
            with pe.Fori(0, NG, 1) as g:
                pe.wait_ge(staged, g + 1)
                pe.wait_ge(x_taken, g * GN)
                for j in range(GN):
                    nc.tensor.matmul(wide[:, j, :], m.ones[0:1, :], bias[:], start=True, stop=False, skip_group_check=True)
                    for k in range(2):
                        last = nc.tensor.matmul(wide[:, j, k * P:(k + 1) * P], sums[:, k, j, :], m.ident[:], start=False, stop=True,
                                                skip_group_check=True)
                last.then_inc(made, 1)
                pe.wait_ge(relued, g + 1)
                pe.wait_ge(root_taken, g)
                for j in range(GN):
                    for k in range(2):
                        last = nc.tensor.transpose(tile(k, j), y[:, j, k * P:(k + 1) * P], m.ident[:])
                last.then_inc(turned, 1)
                pe.wait_ge(kept, g + 1)
                for j in range(GN):
                    for k in range(2):
                        last = nc.tensor.matmul(quarter[:, j, :], y_t[:, k, j, :], wf[:, k, :], start=(k == 0), stop=(k == 1))
                last.then_inc(f_made, 1)
                for b in range(2):
                    for k in range(2):
                        nodes = y_t[:, k].rearrange("p j n -> p (j n)")[:, b * (GW // 2):(b + 1) * (GW // 2)]
                        last = nc.tensor.matmul(root[:, b, :], wroot[:, k, :], nodes, start=(k == 0), stop=(k == 1))
                last.then_inc(root_made, 1)
                for j in range(GN):
                    if j >= 4:
                        pe.wait_ge(x_taken, g * GN + j - 3)
                    for k in range(2):
                        last = nc.tensor.matmul(ps[:, j % 4, :], y_t[:, k, j, :], wrel[:, k].rearrange("p r n -> p (r n)"), start=(k == 0), stop=(k == 1))
                    last.then_inc(x_made, 1)


def after_rgcn(nc, m, a):
    with ExitStack() as ctx:
        sb, pb, sem = place(nc, ctx, "n4")
        wf, w1 = sb("wf", [P, C]), sb("w1", [P, 2, C])
        bias = sb("bias", [1, C])
        load_weights(nc, m, "n4_load", [(wf[:], a["L1_gnn_fusion_W"][2 * H:2 * H + C, :]), (w1[:], by_half(a["L2_gnn_W1"][0:2 * C, :])),
                                        (bias[:], row_of(a["L2_gnn_b1"]))])
        rgcn, f = sb("rgcn", [P, GN, P]), sb("f", [P, GN, C])
        out, square = sb("out", [P, GN, C]), sb("square", [P, GN, C])
        length = sb("length", [P, 3, GN])
        x, x_t = sb("x", [P, GN, C]), sb("x_t", [P, GN, P])
        pq = sb("pq", [P, GN, 2 * C])
        ps_f, ps_t, ps = pb("ps_f", [P, 8, C]), pb("ps_t", [P, 8, P]), pb("ps", [P, 8, 2 * C])
        b = NormBuffers(sb, sem)
        loaded, staged, made, fused, squared, length_ready, length_root, steps, joined, turned, kept, pq_made, pq_taken, stored = sem(
            "loaded", "staged", "made", "fused", "squared", "length_ready", "length_root", "steps", "joined", "turned", "kept", "pq_made",
            "pq_taken", "stored")
        x_kept = sem("x_kept")
        block = ctx.enter_context(nc.Block())

        @block.sync
        def _(sp):
            with sp.Fori(0, NG, 1) as g:
                sp.wait_ge(fused, g)
                sp.dma_start(f[:], node_rows(m.t_f, g, C)).then_inc(loaded, 16)
                sp.wait_ge(pq_taken, g + 1)
                sp.dma_start(node_rows(m.t_p, g, C), pq[:, :, 0:C]).then_inc(stored, 16)
                sp.dma_start(node_rows(m.t_q, g, C), pq[:, :, C:2 * C]).then_inc(stored, 16)
            sp.wait_ge(stored, 32 * NG)

        @block.scalar
        def _(act):
            with act.Fori(0, NG, 1) as g:
                b.g = g
                act.wait_ge(made, g)
                nc.scalar.copy(rgcn[:].rearrange("p j n -> p (j n)"), m.acc[:, 0, group_cols(g)]).then_inc(staged, 1)
                act.wait_ge(length_ready, g + 1)
                nc.scalar.activation(length[:, 1, :], length[:, 0, :], ACT.Sqrt).then_inc(length_root, 1)
                layer_norm_root(nc, act, m, b)
                act.wait_ge(turned, g + 1)
                nc.scalar.copy(x_t[:], ps_t[:, 0:GN, :]).then_inc(kept, 1)
                nc.scalar.copy(m.x[:, group_tiles(g), :], x[:]).then_inc(x_kept, 1)
                act.wait_ge(pq_made, g + 1)
                act.wait_ge(stored, 32 * g)
                nc.scalar.copy(pq[:], ps[:, 0:GN, :]).then_inc(pq_taken, 1)

        @block.vector
        def _(dve):
            with dve.Fori(0, NG, 1) as g:
                b.g = g
                link = LoopChain(dve, steps, g, 3 + 2)
                dve.wait_ge(loaded, 16 * (g + 1))
                dve.wait_ge(made, g + 1)
                nc.vector.tensor_tensor(out[:], ps_f[:, 0:GN, :], f[:], ALU.add).then_inc(fused, 1)
                dve.wait_ge(fused, g + 1)
                link(nc.vector.tensor_tensor(square[:], out[:], out[:], ALU.mult))
                nc.vector.tensor_reduce(length[:, 0, :], square[:], AX.X, ALU.add).then_inc(length_ready, 1)
                dve.wait_ge(length_root, g + 1)
                link(nc.vector.tensor_scalar(length[:, 1, :], length[:, 1, :], 1e-12, None, ALU.max))
                link(nc.vector.reciprocal(length[:, 2, :], length[:, 1, :]))
                for j in range(GN):
                    nc.vector.scalar_tensor_tensor(out[:, j, :], out[:, j, :], length[:, 2, j:j + 1], m.x[:, bass.ds(g * GN + j, 1), :],
                                                   ALU.mult, ALU.add).then_inc(joined, 1)
                dve.wait_ge(joined, (g + 1) * GN)
                dve.wait_ge(x_kept, g)
                layer_norm(nc, dve, link, b, out, x)
                link.end()

        @block.tensor
        def _(pe):
            with pe.Fori(0, NG, 1) as g:
                pe.wait_ge(staged, g + 1)
                pe.wait_ge(fused, g)
                for j in range(GN):
                    last = nc.tensor.matmul(ps_f[:, j, :], rgcn[:, j, :], wf[:], start=True, stop=True)
                last.then_inc(made, 1)
                pe.wait_ge(b.norm_ready, (g + 1) * GN)
                for j in range(GN):
                    last = nc.tensor.transpose(ps_t[:, j, :], x[:, j, :], m.ident[:])
                last.then_inc(turned, 1)
                pe.wait_ge(kept, g + 1)
                pe.wait_ge(pq_taken, g)
                for j in range(GN):
                    nc.tensor.matmul(ps[:, j, :], x_t[:, j, :], w1[:].rearrange("p b n -> p (b n)"), start=True, stop=False, skip_group_check=True)
                    last = nc.tensor.matmul(ps[:, j, 0:C], m.ones[0:1, :], bias[:], start=False, stop=True, skip_group_check=True)
                last.then_inc(pq_made, 1)


def edge_hidden(nc, m, a):
    with ExitStack() as ctx:
        sb, pb, sem = place(nc, ctx, "eh")
        w1c = sb("w1c", [2, C])
        load_weights(nc, m, "eh_load", [(w1c[:], a["L2_gnn_W1"][2 * C:2 * C + 2, :])])
        w = Window(nc, sb, pb, sem, C)
        message = sb("message", [P, U, C])
        stage = [sb(f"stage{h}", [P, HU], I32) for h in range(2)]
        attr = sb("attr", [2, 2, HU * P])
        keys = sb("keys", [P, 2, HU, P])
        hidden, square = sb("hidden", [P, U, C]), sb("square", [P, U, C])
        seen = sb("seen", [P, 2, HU])
        junk = sb("junk", [P, P])
        valid = sb("valid", [P, TP])
        ps = pb("ps", [P, U, C])
        ps_sum = [pb(f"sum{h}", [P, 2]) for h in range(2)]
        gathered = [sem(f"gathered{u}") for u in range(U)]
        made = [sem(f"made{h}") for h in range(2)]
        added = [sem(f"added{h}") for h in range(2)]
        summed = [sem(f"summed{h}") for h in range(2)]
        attr_in = [sem(f"attr_in{h}") for h in range(2)]
        keys_in = [sem(f"keys_in{h}") for h in range(2)]
        stored = [sem(f"stored{h}") for h in range(2)]
        staged, carried, squared, totalled, counted, kept_seen, zeroed = sem(
            "staged", "carried", "squared", "totalled", "counted", "kept_seen", "zeroed")
        block = ctx.enter_context(nc.Block())

        @block.sync
        def _(sp):
            def store(it, h):
                sp.wait_ge(added[h], (it + 1) * 2)
                sp.dma_start(m.t_hidden[bass.ds((it * U + h * HU) * P, HU * P), :].rearrange("(t p) f -> p t f", p=P),
                             hidden[:, h * HU:(h + 1) * HU, :]).then_inc(stored[h], 16)

            def load(it, h):
                sp.wait_ge(made[h], it * 2)
                window_load(nc, m, sp, w, m.t_q, C, it, h)
                first = (it * U + h * HU) * P
                sp.dma_start(attr[:, h, :], m.t_ea[:, bass.ds(first, HU * P)]).then_inc(attr_in[h], 16)
                sp.wait_ge(kept_seen, it * 2)
                sp.dma_start(keys[:, h].rearrange("p t e -> p (t e)"),
                             row_of(m.t_src[bass.ds(first, HU * P)]).to_broadcast([P, HU * P])).then_inc(keys_in[h], 16)

            load(0, 0)
            load(0, 1)
            with sp.Fori(0, ITERS - 1, 1) as it:
                for h in range(2):
                    store(it, h)
                for h in range(2):
                    load(it + 1, h)
            for h in range(2):
                store(ITERS - 1, h)
            for h in range(2):
                sp.wait_ge(stored[h], 16 * ITERS)

        @block.gpsimd
        def _(pool):
            with pool.Fori(0, ITERS, 1) as it:
                for u in range(U):
                    h, k = divmod(u, HU)
                    if k == 0:
                        pool.wait_ge(carried, it * 2 + h)
                        pool.wait_ge(staged, it * 2 + h + 1)
                        nc.gpsimd.tensor_tensor(m.carrier[:], m.ones_i[:], m.ones_i[:], ALU.add).then_inc(carried, 1)
                    pool.indirect_dma_start(message[:, u, :], None, m.t_p, bass.IndirectOffsetOnAxis(ap=stage[h][:, k:k + 1], axis=0)).then_inc(gathered[u], 16)

        @block.scalar
        def _(act):
            with act.Fori(0, ITERS, 1) as it:
                for h in range(2):
                    act.wait_ge(added[h], it * 2)
                    nc.scalar.copy(stage[h][:], m.src[:, bass.ds(it * U + h * HU, HU)]).then_inc(staged, 1)
                for q in range(QUADS):
                    if q % 2 == 0:
                        act.wait_ge(made[q // 2], it * 2)
                    window_keep(nc, act, w, it, q)
                for q in range(QUADS):
                    if q % 2 == 0:
                        act.wait_ge(summed[q // 2], it)
                    act.wait_ge(added[q // 2], it * 2 + q % 2 + 1)
                    quad = slice(q * QU, (q + 1) * QU)
                    nc.scalar.activation(square[:, quad, :], hidden[:, quad, :], ACT.Square).then_inc(squared, 1)

        @block.vector
        def _(dve):
            nc.vector.memset(m.totals[:], 0.0).then_inc(zeroed, 1)
            nc.vector.tensor_scalar(valid[:], m.rel[:], 0.0, None, ALU.is_ge).then_inc(zeroed, 1)
            for h in range(2):
                nc.vector.memset(ps_sum[h][:], 0.0).then_inc(zeroed, 1)
            dve.wait_ge(zeroed, 4)
            with dve.Fori(0, ITERS, 1) as it:
                window_hot(nc, m, dve, w, it)
                for h in range(2):
                    dve.wait_ge(stored[h], 16 * it)
                    dve.wait_ge(summed[h], it)
                    dve.wait_ge(totalled, it * 2 + h)
                    dve.wait_ge(keys_in[h], 16 * (it + 1))
                    nc.vector.tensor_tensor(m.totals[:], m.totals[:], ps_sum[h][:], ALU.add).then_inc(totalled, 1)
                    for q in range(2 * h, 2 * h + 2):
                        for u in range(q * QU, (q + 1) * QU):
                            t = it * U + u
                            dve.wait_ge(counted, t)
                            nc.vector.scalar_tensor_tensor(junk[:], keys[:, h, u % HU, :], m.src_key[:, bass.ds(t, 1)], m.before[:],
                                                           ALU.is_equal, ALU.mult, accum_out=seen[:, h, u % HU:u % HU + 1]).then_inc(counted, 1)
                        for u in range(q * QU, (q + 1) * QU):
                            dve.wait_ge(gathered[u], 16 * (it + 1))
                        dve.wait_ge(made[h], it * 2 + q % 2 + 1)
                        quad = slice(q * QU, (q + 1) * QU)
                        nc.vector.tensor_tensor(hidden[:, quad, :], ps[:, quad, :], message[:, quad, :], ALU.add).then_inc(added[h], 1)
                    dve.wait_ge(counted, it * U + (h + 1) * HU)
                    nc.vector.tensor_copy(m.seen[:, bass.ds(it * U + h * HU, HU)], seen[:, h, :]).then_inc(kept_seen, 1)
            for h in range(2):
                dve.wait_ge(summed[h], ITERS)
                dve.wait_ge(totalled, ITERS * 2 + h)
                nc.vector.tensor_tensor(m.totals[:], m.totals[:], ps_sum[h][:], ALU.add).then_inc(totalled, 1)

        @block.tensor
        def _(pe):
            def look_up(it, q):
                h = q // 2
                pe.wait_ge(attr_in[h], 16 * (it + 1))
                pe.wait_ge(added[h], it * 2)
                pe.wait_ge(w.kept, it * QUADS + q + 1)
                for u in range(q * QU, (q + 1) * QU):
                    pe.wait_ge(w.loaded[u], (it + 1) * 16)
                    nc.tensor.matmul(ps[:, u, :], w.hot_t[:, u, :], w.rows[:, u, :], start=True, stop=False)
                    last = nc.tensor.matmul(ps[:, u, :], attr[:, h, (u % HU) * P:(u % HU + 1) * P], w1c[:], start=False, stop=True)
                last.then_inc(made[h], 1)

            pe.wait_ge(zeroed, 4)
            with pe.Fori(0, ITERS, 1) as it:
                for q in range(QUADS):
                    window_turn(nc, m, pe, w, it, q)
                    if q >= 1:
                        look_up(it, q - 1)
                look_up(it, QUADS - 1)
                for h in range(2):
                    pe.wait_ge(totalled, it * 2 + h + 1)
                    for c, rows in enumerate((hidden, square)):
                        for k in range(HU):
                            u = h * HU + k
                            if k % QU == 0:
                                pe.wait_ge(squared, it * QUADS + u // QU + 1)
                            last = nc.tensor.matmul(ps_sum[h][:, c:c + 1], rows[:, u, :], valid[:, bass.ds(it * U + u, 1)],
                                                    start=(k == 0), stop=(k == HU - 1))
                    last.then_inc(summed[h], 1)


def batch_norm_rows(nc, m, a):
    with ExitStack() as ctx:
        sb, pb, sem = place(nc, ctx, "bn")
        gamma, beta = sb("gamma", [P, 1]), sb("beta", [P, 1])
        load_weights(nc, m, "bn_load", [(gamma[:], a["L2_gnn_gamma"].rearrange("(n a) -> n a", a=1)), (beta[:], a["L2_gnn_beta"].rearrange("(n a) -> n a", a=1))])
        v = sb("v", [P, 6])
        diag = sb("diag", [P, 2, C])
        first, target = sb("first", [P, TP]), sb("target", [P, TP])
        ps = pb("ps", [P, 2, C])
        var_ready, root_ready, diag_ready, spread = sem("var_ready", "root_ready", "diag_ready", "spread")
        block = ctx.enter_context(nc.Block())

        @block.vector
        def _(dve):
            link = chain(dve, m)
            ts, stt = nc.vector.tensor_scalar, nc.vector.scalar_tensor_tensor
            link(ts(v[:, 0:2], m.totals[:], 1.0 / EDGES, None, ALU.mult))
            link(stt(v[:, 2:3], v[:, 0:1], v[:, 0:1], v[:, 1:2], ALU.mult, ALU.subtract))
            ts(v[:, 3:4], v[:, 2:3], -1.0, 0.0, ALU.mult, ALU.max).then_inc(var_ready, 1)
            dve.wait_ge(root_ready, 1)
            link(nc.vector.reciprocal(v[:, 5:6], v[:, 4:5]))
            link(nc.vector.tensor_tensor(v[:, 5:6], v[:, 5:6], gamma[:], ALU.mult))
            link(nc.vector.tensor_tensor(v[:, 4:5], v[:, 0:1], v[:, 5:6], ALU.mult))
            link(nc.vector.tensor_tensor(v[:, 4:5], beta[:], v[:, 4:5], ALU.subtract))
            ts(diag[:, 0], m.ident[:], v[:, 5:6], None, ALU.mult).then_inc(diag_ready, 1)
            ts(diag[:, 1], m.ident[:], v[:, 4:5], None, ALU.mult).then_inc(diag_ready, 1)
            link(ts(first[:], m.seen[:], 0.5, None, ALU.is_lt))
            link(ts(target[:], m.rel[:], 0.0, None, ALU.is_ge))
            link(nc.vector.tensor_tensor(first[:], first[:], target[:], ALU.mult))
            link(ts(m.column[:], m.column[:], float(ROWS), None, ALU.add))
            link(ts(target[:], m.src_key[:], m.column[:], None, ALU.subtract))
            link(nc.vector.tensor_tensor(target[:], target[:], first[:], ALU.mult))
            link(ts(target[:], target[:], m.column[:], None, ALU.add))
            link(nc.vector.tensor_copy(m.target[:], target[:]))
            dve.wait_ge(spread, 2)
            link(nc.vector.tensor_copy(m.norm_rows[:], ps[:]))

        @block.scalar
        def _(act):
            act.wait_ge(var_ready, 1)
            nc.scalar.activation(v[:, 4:5], v[:, 3:4], ACT.Sqrt, bias=m.epsilon[:], scale=1.0).then_inc(root_ready, 1)

        @block.tensor
        def _(pe):
            pe.wait_ge(diag_ready, 2)
            for k in range(2):
                nc.tensor.matmul(ps[:, k, :], m.ones[:], diag[:, k], start=True, stop=True).then_inc(spread, 1)


def scatter_by_source(nc, m, a):
    Q = COPIES // 2
    with ExitStack() as ctx:
        sb, pb, sem = place(nc, ctx, "sc")
        rows = sb("rows", [P, 2, HU, C])
        message = sb("message", [P, 2, HU, SW])
        keys = sb("keys", [P, 2, HU, P])
        same = sb("same", [P, U, P])
        total = sb("total", [P, U, SW])
        stage = [sb(f"stage{q}", [P, Q], I32) for q in range(U // Q)]
        ps = pb("ps", [P, U, 256])
        rows_in = [sem(f"rows_in{h}") for h in range(2)]
        keys_in = [sem(f"keys_in{h}") for h in range(2)]
        scattered = [sem(f"scattered{k}") for k in range(COPIES)]
        scaled, shifted, relued, matched, staged, carried, counts_set = sem(
            "scaled", "shifted", "relued", "matched", "staged", "carried", "counts_set")
        summed = [sem(f"summed{h}") for h in range(2)]
        taken = [sem(f"taken{h}") for h in range(2)]
        block = ctx.enter_context(nc.Block())
        batches = U // Q
        pairs = HU // 2

        @block.sync
        def _(sp):
            with sp.Fori(0, ITERS, 1) as it:
                for h in range(2):
                    first = (it * U + h * HU) * P
                    sp.wait_ge(summed[h], pairs * it)
                    sp.dma_start(rows[:, h], m.t_hidden[bass.ds(first, HU * P), :].rearrange("(t p) f -> p t f", p=P)).then_inc(rows_in[h], 16)
                    sp.dma_start(keys[:, h].rearrange("p t e -> p (t e)"),
                                 row_of(m.t_src[bass.ds(first, HU * P)]).to_broadcast([P, HU * P])).then_inc(keys_in[h], 16)

        @block.vector
        def _(dve):
            nc.vector.memset(message[:], 1.0).then_inc(counts_set, 1)
            with dve.Fori(0, ITERS, 1) as it:
                for h in range(2):
                    wide = lambda k: m.norm_rows[:, k:k + 1, :].to_broadcast([P, HU, C])
                    dve.wait_ge(rows_in[h], 16 * (it + 1))
                    nc.vector.tensor_tensor(rows[:, h], rows[:, h], wide(0), ALU.mult).then_inc(scaled, 1)
                    dve.wait_ge(scaled, it * 2 + h + 1)
                    nc.vector.tensor_tensor(rows[:, h], rows[:, h], wide(1), ALU.add).then_inc(shifted, 1)
                    dve.wait_ge(keys_in[h], 16 * (it + 1))
                    for k in range(HU):
                        u = h * HU + k
                        nc.vector.tensor_scalar(same[:, u, :], keys[:, h, k, :], m.src_key[:, bass.ds(it * U + u, 1)], None,
                                                ALU.is_equal).then_inc(matched, 1)
                for u in range(0, U, 2):
                    h, pair = u // HU, u % HU // 2
                    if u % Q == 0:
                        dve.wait_ge(staged, it * batches + u // Q + 1)
                    dve.wait_ge(summed[h], it * pairs + pair + 1)
                    nc.vector.tensor_copy(total[:, u:u + 2, :], ps[:, u:u + 2, 0:SW]).then_inc(taken[h], 1)

        @block.scalar
        def _(act):
            act.wait_ge(counts_set, 1)
            with act.Fori(0, ITERS, 1) as it:
                for h in range(2):
                    act.wait_ge(summed[h], it * pairs)
                    act.wait_ge(shifted, it * 2 + h + 1)
                    nc.scalar.activation(message[:, h, :, 0:C], rows[:, h], ACT.Relu).then_inc(relued, 1)
                for q in range(batches):
                    for k in range(Q):
                        act.wait_ge(scattered[(q % 2) * Q + k], 16 * 2 * it)
                    nc.scalar.copy(stage[q][:], m.target[:, bass.ds(it * U + q * Q, Q)]).then_inc(staged, 1)

        @block.tensor
        def _(pe):
            with pe.Fori(0, ITERS, 1) as it:
                for h in range(2):
                    pe.wait_ge(relued, it * 2 + h + 1)
                    pe.wait_ge(taken[h], it * pairs)
                    for k in range(HU):
                        u = h * HU + k
                        pe.wait_ge(matched, it * U + u + 1)
                        last = nc.tensor.matmul(ps[:, u, 0:SW], same[:, u, :], message[:, h, k, :], start=True, stop=True)
                        if k % 2 == 1:
                            last.then_inc(summed[h], 1)

        @block.gpsimd
        def _(pool):
            with pool.Fori(0, ITERS, 1) as it:
                for u in range(U):
                    q, k = divmod(u, Q)
                    if k == 0:
                        pool.wait_ge(carried, it * batches + q)
                        pool.wait_ge(taken[q // 2], it * pairs + (q % 2 + 1) * Q // 2)
                        for c in range(Q):
                            pool.wait_ge(scattered[(q % 2) * Q + c], 16 * (it * 2 + q // 2))
                        nc.gpsimd.tensor_tensor(m.carrier[:], m.ones_i[:], m.ones_i[:], ALU.add).then_inc(carried, 1)
                    copy = (q % 2) * Q + k
                    pool.indirect_dma_start(m.scatter[copy], bass.IndirectOffsetOnAxis(ap=stage[q][:, k:k + 1], axis=0), total[:, u, :], None,
                                            compute_op=ALU.add).then_inc(scattered[copy], 16)
            for c in range(COPIES):
                pool.wait_ge(scattered[c], 16 * 2 * ITERS)


def after_block2(nc, m, a):
    with ExitStack() as ctx:
        sb, pb, sem = place(nc, ctx, "n5")
        w2, w0, w8 = sb("w2", [P, C]), sb("w0", [P, C]), sb("w8", [P, R8, C])
        b2 = sb("b2", [P, C])
        load_weights(nc, m, "n5_load", [(w2[:], a["L2_gnn_W2"]), (w0[:], a["L3_gnn_W0"]), (w8[:], a["L3_gnn_W"].rearrange("r k n -> k r n")),
                                        (b2[:], row_of(a["L2_gnn_b2"]).to_broadcast([P, C]))])
        copies = sb("copies", [P, COPIES, GN, SW])
        sums_t = sb("sums_t", [P, GN, P])
        count = sb("count", [P, 2, GN])
        y = sb("y", [P, GN, C])
        x, x_t = sb("x", [P, GN, C]), sb("x_t", [P, GN, P])
        h = sb("h", [P, GN, R8, C])
        ps_t, ps, ps_h = pb("ps_t", [P, 8, P]), pb("ps", [P, 8, C]), pb("ps_h", [P, 4, 512])
        b = NormBuffers(sb, sem)
        loaded, steps, summed, turned, kept, made, joined, taken, turned2, kept2, root_made, root_taken, h_made, h_even, h_odd, stored, x_kept = sem(
            "loaded", "steps", "summed", "turned", "kept", "made", "joined", "taken", "turned2", "kept2", "root_made", "root_taken", "h_made",
            "h_even", "h_odd", "stored", "x_kept")
        tail_cleared = sem("tail_cleared")
        block = ctx.enter_context(nc.Block())
        root = ps[:].rearrange("p (b j) n -> p b (j n)", b=2)[:, :, 0:GW // 2]

        @block.sync
        def _(sp):
            with sp.Fori(0, NG, 1) as g:
                sp.wait_ge(joined, g * GN)
                for c in range(COPIES):
                    sp.dma_start(copies[:, c], node_rows(m.scatter[c], g, SW)).then_inc(loaded, 16)
                sp.wait_ge(h_even, (g + 1) * GN)
                sp.wait_ge(h_odd, (g + 1) * GN)
                sp.dma_start(node_rows(m.t_rel8, g, R8 * C), h[:].rearrange("p j r n -> p j (r n)")).then_inc(stored, 16)
            sp.wait_ge(stored, 16 * NG)

        @block.vector
        def _(dve):
            nc.vector.memset(m.acc[:, :, ROWS:ACCW], 0.0).then_inc(tail_cleared, 1)
            with dve.Fori(0, NG, 1) as g:
                b.g = g
                link = LoopChain(dve, steps, g, 2 + 2 + 1 + 2)
                dve.wait_ge(loaded, 16 * COPIES * (g + 1))
                span = COPIES
                while span > 2:
                    span //= 2
                    link(nc.vector.tensor_tensor(copies[:, 0:span], copies[:, 0:span], copies[:, span:2 * span], ALU.add))
                nc.vector.tensor_tensor(copies[:, 0], copies[:, 0], copies[:, 1], ALU.add).then_inc(summed, 1)
                dve.wait_ge(summed, g + 1)
                link(nc.vector.tensor_scalar(count[:, 0], copies[:, 0, :, C], 1.0, None, ALU.add))
                link(nc.vector.reciprocal(count[:, 1], count[:, 0]))
                dve.wait_ge(made, g + 1)
                for j in range(GN):
                    nc.vector.scalar_tensor_tensor(y[:, j, :], b2[:], copies[:, 0, j, C:C + 1], ps[:, j, :], ALU.mult, ALU.add).then_inc(joined, 1)
                dve.wait_ge(joined, (g + 1) * GN)
                for j in range(GN):
                    nc.vector.scalar_tensor_tensor(y[:, j, :], y[:, j, :], count[:, 1, j:j + 1], m.x[:, bass.ds(g * GN + j, 1), :],
                                                   ALU.mult, ALU.add).then_inc(taken, 1)
                dve.wait_ge(taken, (g + 1) * GN)
                link(nc.vector.tensor_tensor(y[:], y[:], m.x[:, group_tiles(g), :], ALU.add))
                dve.wait_ge(x_kept, g)
                dve.wait_ge(turned2, g)
                layer_norm(nc, dve, link, b, y, x)
                link.end()
                dve.wait_ge(stored, 16 * g)
                for j in range(GN):
                    dve.wait_ge(h_made, (g * GN + j + 1) * 2 - 1)
                    nc.vector.tensor_copy(h[:, j, 0:R8 // 2].rearrange("p r n -> p (r n)"), ps_h[:, (2 * j) % 4, :]).then_inc(h_even, 1)

        @block.scalar
        def _(act):
            with act.Fori(0, NG, 1) as g:
                b.g = g
                act.wait_ge(turned, g + 1)
                act.wait_ge(made, g)
                nc.scalar.copy(sums_t[:], ps_t[:, 0:GN, :]).then_inc(kept, 1)
                layer_norm_root(nc, act, m, b)
                act.wait_ge(b.norm_ready, (g + 1) * GN)
                nc.scalar.copy(m.x[:, group_tiles(g), :], x[:]).then_inc(x_kept, 1)
                act.wait_ge(turned2, g + 1)
                act.wait_ge(h_made, 2 * GN * g)
                nc.scalar.copy(x_t[:], ps_t[:, 0:GN, :]).then_inc(kept2, 1)
                act.wait_ge(root_made, g + 1)
                nc.scalar.copy(m.acc[:, 0, group_cols(g)].rearrange("p (b n) -> p b n", b=2), root).then_inc(root_taken, 1)
                act.wait_ge(stored, 16 * g)
                for j in range(GN):
                    act.wait_ge(h_made, (g * GN + j + 1) * 2)
                    nc.scalar.copy(h[:, j, R8 // 2:R8].rearrange("p r n -> p (r n)"), ps_h[:, (2 * j + 1) % 4, :]).then_inc(h_odd, 1)

        @block.tensor
        def _(pe):
            with pe.Fori(0, NG, 1) as g:
                pe.wait_ge(summed, g + 1)
                pe.wait_ge(kept2, g)
                for j in range(GN):
                    last = nc.tensor.transpose(ps_t[:, j, :], copies[:, 0, j, 0:C], m.ident[:])
                last.then_inc(turned, 1)
                pe.wait_ge(kept, g + 1)
                pe.wait_ge(root_taken, g)
                for j in range(GN):
                    last = nc.tensor.matmul(ps[:, j, :], sums_t[:, j, :], w2[:], start=True, stop=True)
                last.then_inc(made, 1)
                pe.wait_ge(b.norm_ready, (g + 1) * GN)
                for j in range(GN):
                    last = nc.tensor.transpose(ps_t[:, j, :], x[:, j, :], m.ident[:])
                last.then_inc(turned2, 1)
                pe.wait_ge(kept2, g + 1)
                for c in range(2):
                    nodes = x_t[:].rearrange("p j n -> p (j n)")[:, c * (GW // 2):(c + 1) * (GW // 2)]
                    last = nc.tensor.matmul(root[:, c, :], w0[:], nodes, start=True, stop=True)
                last.then_inc(root_made, 1)
                for j in range(GN):
                    if j >= 2:
                        pe.wait_ge(h_even, g * GN + j - 1)
                        pe.wait_ge(h_odd, g * GN + j - 1)
                    else:
                        pe.wait_ge(h_even, g * GN)
                        pe.wait_ge(h_odd, g * GN)
                    for c in range(2):
                        last = nc.tensor.matmul(ps_h[:, (2 * j + c) % 4, :], x_t[:, j, :], w8[:, c * 4:c * 4 + 4].rearrange("p r n -> p (r n)"),
                                                start=True, stop=True)
                        last.then_inc(h_made, 1)


def after_block3(nc, m, a):
    with ExitStack() as ctx:
        sb, pb, sem = place(nc, ctx, "n6")
        scaled = sb("scaled", [P, GN, P])
        y = sb("y", [P, GN, C])
        ps = pb("ps", [P, 8, C])
        b = NormBuffers(sb, sem)
        staged, made, taken, steps, stored = sem("staged", "made", "taken", "steps", "stored")
        block = ctx.enter_context(nc.Block())

        @block.tensor
        def _(pe):
            with pe.Fori(0, NG, 1) as g:
                pe.wait_ge(staged, g + 1)
                pe.wait_ge(taken, g)
                for j in range(GN):
                    last = nc.tensor.transpose(ps[:, j, :], scaled[:, j, :], m.ident[:])
                last.then_inc(made, 1)

        @block.scalar
        def _(act):
            with act.Fori(0, NG, 1) as g:
                b.g = g
                layer_norm_root(nc, act, m, b)

        @block.vector
        def _(dve):
            with dve.Fori(0, NG, 1) as g:
                b.g = g
                link = LoopChain(dve, steps, g, 2)
                dve.wait_ge(made, g)
                nc.vector.tensor_tensor(scaled[:].rearrange("p j n -> p (j n)"), m.acc[:, 0, group_cols(g)],
                                        m.inv_degree[:, group_cols(g)], ALU.mult).then_inc(staged, 1)
                dve.wait_ge(made, g + 1)
                dve.wait_ge(b.norm_ready, g * GN)
                nc.vector.tensor_tensor(y[:], ps[:, 0:GN, :], m.x[:, group_tiles(g), :], ALU.add).then_inc(taken, 1)
                dve.wait_ge(taken, g + 1)
                layer_norm(nc, dve, link, b, y, m.x[:, group_tiles(g), :])
                link.end()

        @block.sync
        def _(sp):
            sp.wait_ge(b.norm_ready, NG * GN)
            sp.dma_start(a["out"][0:(NT - 1) * P, :].rearrange("(j p) f -> p j f", p=P), m.x[:, 0:NT - 1, :]).then_inc(stored, 16)
            sp.dma_start(a["out"][(NT - 1) * P:NODES, :], m.x[0:TAIL, NT - 1, :]).then_inc(stored, 16)
            sp.wait_ge(stored, 32)


class Memory:
    pass


class EdgeSemaphores:
    def __init__(self, sem):
        self.passes, self.hots = 0, 0
        self.gathered = [sem(f"gathered{u}") for u in range(U)]
        self.half_used = [sem(f"half_used{h}") for h in range(2)]
        self.staged, self.carried, self.hot_ready, self.window_ready, self.window_used = sem(
            "staged", "carried", "hot_ready", "window_ready", "window_used")


def gnn_blocks(nc, a):
    with ExitStack() as ctx:
        sb, _, sem = place(nc, ctx, "all")
        m = Memory()
        m.steps, m.step = 0, sem("step")
        m.edge = EdgeSemaphores(sem)
        table = lambda name, *shape: nc.dram_tensor(name, shape, F32, kind="Internal").ap()
        m.t_x, m.t_f, m.t_p, m.t_q = table("t_x", ROWS, C), table("t_f", ROWS, C), table("t_p", ROWS, C), table("t_q", ACCW, C)
        m.t_s1, m.t_h, m.t_al = table("t_s1", ROWS, H), table("t_h", ROWS, 2 * H), table("t_al", ACCW, 4)
        m.t_rel4, m.t_rel8 = table("t_rel4", ROWS, R4 * C), table("t_rel8", ROWS, R8 * C)
        m.t_hidden, m.t_self = table("t_hidden", T * P, C), table("t_self", TP * P, 2)
        m.t_src, m.t_ea = table("t_src", TP * P), table("t_ea", 2, TP * P)
        m.scatter = [table(f"scatter{k}", SROWS, SW) for k in range(COPIES)]
        m.iota, m.ident, m.before, m.ones = (sb(n, [P, P]) for n in ("iota", "ident", "before", "ones"))
        m.column, m.epsilon = sb("column", [P, 1]), sb("epsilon", [P, 1])
        m.ones_i, m.carrier = sb("ones_i", [1, 1], I32), sb("carrier", [1, 1], I32)
        m.x = sb("x", [P, NT, C])
        m.src, m.src4, m.src8 = (sb(n, [P, TP], I32) for n in ("src", "src4", "src8"))
        m.rel, m.w_rgcn, m.w_edge, m.src_key = (sb(n, [P, TP]) for n in ("rel", "w_rgcn", "w_edge", "src_key"))
        m.base = sb("base", [1, TP], I32)
        m.last_edge_f, m.has_edges = sb("last_edge_f", [P, NT]), sb("has_edges", [P, NT])
        m.last_edge = sb("last_edge", [P, NT], I32)
        m.self_weight = sb("self_weight", [P, NT, 2])
        m.totals, m.norm_rows = sb("totals", [P, 2]), sb("norm_rows", [P, 2, C])

        with nc.cleanup_on_exit():
            constants(nc, m, a)
            edge_setup(nc, m, a)
        m.inv_degree = sb("inv_degree", [P, ROWS])
        with nc.cleanup_on_exit(), ExitStack() as scope:
            scoped, _, _ = place(nc, scope, "first")
            m.acc = scoped("acc", [P, 2, ACCW])
            aggregate(nc, m, "block0", a["x"], m.src, [], 1, degree=True)
            degrees(nc, m)
            after_block0(nc, m, a)
            aggregate(nc, m, "sage1", m.t_x, m.src, [], 1)
            after_sage1(nc, m, a)
            aggregate(nc, m, "sage2", m.t_s1, m.src, [], 2)
            after_sage2(nc, m, a)
        m.alpha = sb("alpha", [P, 2, TP])
        with nc.cleanup_on_exit(), ExitStack() as scope:
            scoped, _, _ = place(nc, scope, "attention")
            m.e, m.e_self = scoped("e", [P, 2, TP]), scoped("e_self", [P, 2, TP])
            attention_terms(nc, m)
            attention_softmax(nc, m, a)
        with nc.cleanup_on_exit(), ExitStack() as scope:
            scoped, _, _ = place(nc, scope, "second")
            m.acc = scoped("acc", [P, 2, ACCW])
            aggregate(nc, m, "gat", m.t_h, m.src, [m.alpha[:, 0], m.alpha[:, 1]], 2)
            after_gat(nc, m, a)
            aggregate(nc, m, "rgcn", m.t_rel4.rearrange("n (r f) -> (n r) f", f=C), m.src4, [m.w_rgcn], 1, clear=False)
            after_rgcn(nc, m, a)
        m.seen, m.target = m.alpha[:, 0], m.alpha[:, 1].bitcast(I32)
        with nc.cleanup_on_exit():
            edge_hidden(nc, m, a)
            batch_norm_rows(nc, m, a)
            scatter_by_source(nc, m, a)
        with ExitStack() as scope:
            scoped, _, _ = place(nc, scope, "third")
            m.acc = scoped("acc", [P, 1, ACCW])
            after_block2(nc, m, a)
            aggregate(nc, m, "block3", m.t_rel8.rearrange("n (r f) -> (n r) f", f=C), m.src8, [m.w_edge], 1, clear=False)
            after_block3(nc, m, a)


NAMES = ["x", "src", "dst", "edge_attr_2", "edge_type_4", "edge_type_8", "edge_weight", "L0_gnn_W_neigh", "L0_gnn_b_neigh",
         "L1_gnn_sage1_Wl", "L1_gnn_sage1_Wr", "L1_gnn_sage1_b", "L1_gnn_sage2_Wl", "L1_gnn_sage2_Wr", "L1_gnn_sage2_b", "L1_gnn_gat_W",
         "L1_gnn_gat_att_src", "L1_gnn_gat_att_dst", "L1_gnn_gat_b", "L1_gnn_rgcn_Wrel", "L1_gnn_rgcn_Wroot", "L1_gnn_rgcn_b",
         "L1_gnn_fusion_W", "L1_gnn_fusion_b", "L2_gnn_W1", "L2_gnn_b1", "L2_gnn_gamma", "L2_gnn_beta", "L2_gnn_W2", "L2_gnn_b2",
         "L3_gnn_W", "L3_gnn_W0"]


def kernel(**inputs):
    import concourse.bacc as bacc
    from concourse.bass_utils import run_bass_kernel_spmd

    nc = bacc.Bacc("TRN2", target_bir_lowering=False, num_devices=1)
    arrays, a = {}, {}
    for name in NAMES:
        arrays[f"in_{name}"] = np.ascontiguousarray(inputs[name])
        a[name] = nc.dram_tensor(f"in_{name}", arrays[f"in_{name}"].shape, mybir.dt.from_np(arrays[f"in_{name}"].dtype), kind="ExternalInput").ap()
    a["out"] = nc.dram_tensor("out", (NODES, C), F32, kind="ExternalOutput").ap()
    gnn_blocks(nc, a)
    return run_bass_kernel_spmd(nc, [arrays], core_ids=[0]).results[0]["out"]
```

```python
from contextlib import ExitStack

import numpy as np

import concourse.bass as bass
from concourse import mybir

F32 = mybir.dt.float32
I32 = mybir.dt.int32
BF16 = mybir.dt.bfloat16
ALU = mybir.AluOpType
ACT = mybir.ActivationFunctionType
AX = mybir.AxisListType
DVE = mybir.EngineType.DVE
SP = mybir.EngineType.SP

P = 128
NODES, EDGES = 6250, 106250
C = 128
H = 256
R4, R8 = 4, 8
NT = -(-NODES // P)
GN = 7
NG = NT // GN
GW = GN * P
ROWS = NT * P
TAIL = NODES - (NT - 1) * P
U = 16
HU = U // 2
QU = 4
QUADS = U // QU
ITERS = -(-EDGES // (P * U))
T = ITERS * U
EB = -(-T // P)
TP = EB * P
FULL = EDGES // P
REST = EDGES - FULL * P
ACCW = 6400
COPIES = 8
SW = C + 1
SROWS = ROWS + P
BIG = 1e30
EPS = 1e-5
ROUNDER = 1.5 * 2.0 ** 23
REL, LOW, HIGH = 0, 1, 2
assert NT == NG * GN and EB * P >= T + HU and NODES + P <= ACCW


def chain(engine, m):
    def link(instruction):
        m.steps += 1
        instruction.then_inc(m.step, 1)
        engine.wait_ge(m.step, m.steps)
    return link


class LoopChain:
    def __init__(self, engine, sem, g, per):
        self.engine, self.sem, self.g, self.per, self.n = engine, sem, g, per, 0

    def __call__(self, instruction):
        self.n += 1
        assert self.n <= self.per
        instruction.then_inc(self.sem, 1)
        self.engine.wait_ge(self.sem, self.g * self.per + self.n)

    def end(self):
        assert self.n == self.per, (self.n, self.per)


def place(nc, ctx, phase):
    def sb(name, shape, dt=F32):
        return ctx.enter_context(nc.sbuf_tensor(f"{phase}_{name}", shape, dt))

    def pb(name, shape):
        return ctx.enter_context(nc.psum_tensor(f"{phase}_{name}", shape, F32))

    def sem(*names):
        made = [nc.alloc_semaphore(f"{phase}_{n}") for n in names]
        return made if len(made) > 1 else made[0]
    return sb, pb, sem


def node_rows(table, g, width):
    return table[bass.ds(g * GW, GW), 0:width].rearrange("(j p) f -> p j f", p=P)


def edge_blocks(array, b0, b1):
    return array[b0 * P * P:b1 * P * P].rearrange("(b t p) -> t b p", t=P, p=P)


def load_edge_rows(engine, tile, array, sem):
    last = FULL - (EB - 1) * P
    engine.dma_start(tile[:, 0:EB - 1, :], edge_blocks(array, 0, EB - 1)).then_inc(sem, 16)
    engine.dma_start(tile[0:last, EB - 1, :], array[(EB - 1) * P * P:FULL * P].rearrange("(t p) -> t p", p=P)).then_inc(sem, 16)
    engine.dma_start(tile[last:last + 1, EB - 1, 0:REST], array[FULL * P:EDGES].rearrange("(t p) -> t p", t=1)).then_inc(sem, 16)


def constants(nc, m, a):
    with ExitStack() as ctx:
        sb, _, sem = place(nc, ctx, "constants")
        ioted, loaded, cleared, zeros_ready = sem("ioted", "loaded", "cleared", "zeros_ready")
        iota_i, col_i = sb("iota_i", [P, P], I32), sb("col_i", [P, 1], I32)
        zeros = sb("zeros", [P, (SROWS // P) * SW])
        block = ctx.enter_context(nc.Block())

        @block.gpsimd
        def _(pool):
            nc.gpsimd.iota(iota_i[:], pattern=[[1, P]], base=0, channel_multiplier=0).then_inc(ioted, 1)
            nc.gpsimd.iota(col_i[:], pattern=[[1, 1]], base=0, channel_multiplier=1).then_inc(ioted, 1)

        @block.vector
        def _(dve):
            nc.vector.memset(zeros[:], 0.0).then_inc(zeros_ready, 1)
            nc.vector.memset(m.x[:], 0.0).then_inc(zeros_ready, 1)
            dve.wait_ge(ioted, 2)
            link = chain(dve, m)
            link(nc.vector.tensor_copy(m.iota[:], iota_i[:]))
            link(nc.vector.tensor_copy(m.column[:], col_i[:]))
            link(nc.vector.tensor_scalar(m.ident[:], m.iota[:], m.column[:], None, ALU.is_equal))
            link(nc.vector.tensor_scalar(m.before[:], m.iota[:], m.column[:], None, ALU.is_lt))
            link(nc.vector.memset(m.ones[:], 1.0))
            link(nc.vector.memset(m.ones_i[:], 1))
            link(nc.vector.memset(m.epsilon[:], EPS))
            link(nc.vector.tensor_scalar(m.minus_column[:], m.column[:], -1.0, None, ALU.mult))
            link(nc.vector.memset(m.spread_one[:], 1.0))
            link(nc.vector.tensor_scalar(m.spread_src[:], m.column[0:2, 0:1].to_broadcast([2, P]), float(P - 1), 1.0, ALU.mult, ALU.add))

        @block.sync
        def _(sp):
            sp.wait_ge(zeros_ready, 2)
            sp.dma_start(m.x[:, 0:NT - 1, :], a["x"][0:(NT - 1) * P, :].rearrange("(j p) f -> p j f", p=P)).then_inc(loaded, 16)
            sp.dma_start(m.x[0:TAIL, NT - 1, :], a["x"][(NT - 1) * P:NODES, :]).then_inc(loaded, 16)
            for k in range(COPIES):
                sp.dma_start(m.scatter[k].rearrange("(p r) w -> p (r w)", p=P), zeros[:]).then_inc(cleared, 16)
            sp.dma_start(m.t_q[ROWS:ACCW, :], zeros[:, 0:C]).then_inc(cleared, 16)
            sp.dma_start(m.t_last.rearrange("(p r) w -> p (r w)", p=P), zeros[:, 0:TP * 4]).then_inc(cleared, 16)
            sp.wait_ge(loaded, 32)
            sp.wait_ge(cleared, 16 * (COPIES + 2))


class Segments:
    def __init__(self, nc, ctx, phase, q):
        sb, _, _ = place(nc, ctx, phase)
        self.dst_i, self.dst = sb("dst_i", [P, EB, P], I32), sb("dst_rows", [P, EB, P])
        self.same_prev, self.same_next = sb("same_prev", [P, EB, P]), sb("same_next", [P, EB, P])
        self.in_first, self.in_last = sb("in_first", [P, EB, P]), sb("in_last", [P, EB, P])
        self.ends = sb("ends", [P, EB, 2, q])
        self.first, self.last = sb("first_row", [q, TP]), sb("last_row", [q, TP])
        self.cont, self.whole = sb("cont", [q, TP]), sb("whole", [q, TP])
        self.run_in, self.run_out = sb("run_in", [q, TP]), sb("run_out", [q, TP])


def segment_masks(nc, m, a, s, phase, q):
    with ExitStack() as ctx:
        _, pb, sem = place(nc, ctx, phase)
        padded, loaded, turned, ends_ready = sem("padded", "loaded", "turned", "ends_ready")
        rows = pb("ends_rows", [q, 2, 1024])
        block = ctx.enter_context(nc.Block())

        @block.sync
        def _(sp):
            sp.wait_ge(padded, 1)
            load_edge_rows(sp, s.dst_i, a["dst"], loaded)
            sp.wait_ge(loaded, 48)

        @block.vector
        def _(dve):
            nc.vector.memset(s.dst_i[:], NODES).then_inc(padded, 1)
            link = chain(dve, m)
            dve.wait_ge(padded, 1)
            dve.wait_ge(loaded, 48)
            link(nc.vector.tensor_copy(s.dst[:], s.dst_i[:]))
            d = s.dst
            link(nc.vector.memset(s.same_prev[:], 0.0))
            link(nc.vector.memset(s.same_next[:], 0.0))
            link(nc.vector.tensor_tensor(s.same_prev[:, :, 1:P], d[:, :, 1:P], d[:, :, 0:P - 1], ALU.is_equal))
            link(nc.vector.tensor_tensor(s.same_next[:, :, 0:P - 1], d[:, :, 1:P], d[:, :, 0:P - 1], ALU.is_equal))
            link(nc.vector.tensor_tensor(s.in_first[:], d[:], d[:, :, 0:1].to_broadcast([P, EB, P]), ALU.is_equal))
            link(nc.vector.tensor_tensor(s.in_last[:], d[:], d[:, :, P - 1:P].to_broadcast([P, EB, P]), ALU.is_equal))
            nc.vector.tensor_copy(s.ends[:, :, 0, :], d[:, :, 0:1].to_broadcast([P, EB, q])).then_inc(ends_ready, 1)
            nc.vector.tensor_copy(s.ends[:, :, 1, :], d[:, :, P - 1:P].to_broadcast([P, EB, q])).then_inc(ends_ready, 1)
            link(nc.vector.memset(s.cont[:], 0.0))
            link(nc.vector.memset(s.run_in[:], 0.0))
            dve.wait_ge(turned, 2 * EB)
            link(nc.vector.tensor_copy(s.first[:], rows[:, 0, 0:TP]))
            link(nc.vector.tensor_copy(s.last[:], rows[:, 1, 0:TP]))
            link(nc.vector.tensor_tensor(s.cont[:, 1:TP], s.first[:, 1:TP], s.last[:, 0:TP - 1], ALU.is_equal))
            link(nc.vector.tensor_tensor(s.whole[:], s.first[:], s.last[:], ALU.is_equal))
            link(nc.vector.tensor_tensor(s.run_in[:, 1:TP], s.cont[:, 1:TP], s.whole[:, 0:TP - 1], ALU.mult))
            link(nc.vector.memset(s.run_out[:], 0.0))
            link(nc.vector.tensor_tensor(s.run_out[:, 0:TP - 1], s.cont[:, 1:TP], s.whole[:, 1:TP], ALU.mult))

        @block.tensor
        def _(pe):
            pe.wait_ge(ends_ready, 2)
            for b in range(EB):
                for k in range(2):
                    nc.tensor.transpose(rows[:, k, b * P:(b + 1) * P], s.ends[:, b, k, :], m.ident[:]).then_inc(turned, 1)


def segment_totals(nc, m, s, phase, values, total, q, maximum=False):
    with ExitStack() as ctx:
        sb, pb, sem = place(nc, ctx, phase)
        tips_ready, turned, carries_ready, returned = sem("tips_ready", "turned", "carries_ready", "returned")
        back = sb("back", [P, q, EB, P])
        mask = sb("mask", [P, EB, P])
        carry = sb("carry", [q, 2, TP])
        gate, inflow = s.first[0:q], s.last[0:q]
        cont, run_in, run_out = s.cont[0:q], s.run_in[0:q], s.run_out[0:q]
        tips, carried = sb("tips", [P, EB, 2, q]), sb("carried", [P, EB, 2, q])
        rows = pb("tip_rows", [q, 2, 1024])
        cols = pb("carry_cols", [P, EB, 2, q])
        block = ctx.enter_context(nc.Block())
        join = ALU.max if maximum else ALU.add
        decay = ALU.add if maximum else ALU.mult
        flat = lambda t: t.rearrange("p b e -> p (b e)")

        @block.vector
        def _(dve):
            link = chain(dve, m)

            def gates(out, keep):
                if maximum:
                    link(nc.vector.tensor_scalar(out, keep, 1.0, BIG, ALU.subtract, ALU.mult))
                else:
                    link(nc.vector.tensor_copy(out, keep))

            gates(mask[:], s.same_prev[:])
            for k in range(q):
                link(nc.vector.tensor_tensor_scan(flat(total[:, k]), flat(mask[:]), flat(values[:, k]),
                                                  -BIG if maximum else 0.0, decay, join))
            gates(mask[:], s.same_next[:])
            for k in range(q):
                link(nc.vector.tensor_tensor_scan(flat(back[:, k])[:, ::-1], flat(mask[:])[:, ::-1], flat(values[:, k])[:, ::-1],
                                                  -BIG if maximum else 0.0, decay, join))
            link(nc.vector.tensor_copy(tips[:, :, 0, :].rearrange("p b q -> p q b"), total[:, :, :, P - 1]))
            nc.vector.tensor_copy(tips[:, :, 1, :].rearrange("p b q -> p q b"), back[:, :, :, 0]).then_inc(tips_ready, 1)
            if maximum:
                link(nc.vector.tensor_tensor(total[:], total[:], back[:], ALU.max))
            else:
                dve.wait_ge(tips_ready, 1)
                link(nc.vector.tensor_tensor(back[:], back[:], values[:], ALU.subtract))
                link(nc.vector.tensor_tensor(total[:], total[:], back[:], ALU.add))
            dve.wait_ge(turned, 2 * EB)
            link(nc.vector.memset(inflow[:], -BIG if maximum else 0.0))
            if maximum:
                gates(gate[:], cont[:])
                link(nc.vector.tensor_tensor(inflow[:, 1:TP], rows[:, 0, 0:TP - 1], gate[:, 1:TP], ALU.add))
            else:
                link(nc.vector.tensor_tensor(inflow[:, 1:TP], rows[:, 0, 0:TP - 1], cont[:, 1:TP], ALU.mult))
            gates(gate[:], run_in[:])
            link(nc.vector.tensor_tensor_scan(carry[:, 0], gate[:], inflow[:], -BIG if maximum else 0.0, decay, join))
            link(nc.vector.memset(inflow[:], -BIG if maximum else 0.0))
            if maximum:
                gates(gate[:], cont[:])
                link(nc.vector.tensor_tensor(inflow[:, 0:TP - 1], rows[:, 1, 1:TP], gate[:, 1:TP], ALU.add))
            else:
                link(nc.vector.tensor_tensor(inflow[:, 0:TP - 1], rows[:, 1, 1:TP], cont[:, 1:TP], ALU.mult))
            gates(gate[:], run_out[:])
            nc.vector.tensor_tensor_scan(carry[:, 1, ::-1], gate[:, ::-1], inflow[:, ::-1],
                                         -BIG if maximum else 0.0, decay, join).then_inc(carries_ready, 1)
            dve.wait_ge(returned, 2 * EB)
            link(nc.vector.tensor_copy(carried[:], cols[:]))
            for k in range(2):
                inside = s.in_first if k == 0 else s.in_last
                gates(mask[:], inside[:])
                for j in range(q):
                    per_tile = carried[:, :, k, j:j + 1].to_broadcast([P, EB, P])
                    link(nc.vector.tensor_tensor(back[:, j], mask[:], per_tile, ALU.add if maximum else ALU.mult))
                    link(nc.vector.tensor_tensor(total[:, j], total[:, j], back[:, j], join))

        @block.tensor
        def _(pe):
            pe.wait_ge(tips_ready, 1)
            for b in range(EB):
                for k in range(2):
                    nc.tensor.transpose(rows[:, k, b * P:(b + 1) * P], tips[:, b, k, :], m.ident[:]).then_inc(turned, 1)
            pe.wait_ge(carries_ready, 1)
            for b in range(EB):
                for k in range(2):
                    nc.tensor.transpose(cols[:, b, k, :], carry[:, k, b * P:(b + 1) * P], m.ident[0:q, 0:q]).then_inc(returned, 1)


def turn_edges(nc, m, phase, pairs):
    with ExitStack() as ctx:
        _, pb, sem = place(nc, ctx, phase)
        turned, kept = sem("turned", "kept")
        ps = [pb(f"turn{k}", [P, 4, P]) for k in range(4)]
        block = ctx.enter_context(nc.Block())
        work = [(source, target, b, min(4, EB - b)) for source, target in pairs for b in range(0, EB, 4)]

        @block.tensor
        def _(pe):
            for n, (source, _, b, count) in enumerate(work):
                if n >= 4:
                    pe.wait_ge(kept, n - 3)
                for k in range(count):
                    last = nc.tensor.transpose(ps[n % 4][:, k, :], source[:, b + k, :], m.ident[:])
                last.then_inc(turned, 1)

        @block.vector
        def _(dve):
            for n, (_, target, b, count) in enumerate(work):
                dve.wait_ge(turned, n + 1)
                nc.vector.tensor_copy(target[:, b:b + count, :], ps[n % 4][:, 0:count, :]).then_inc(kept, 1)


def by_block(t):
    return t.rearrange("p (b t) -> p b t", t=P)


def edge_setup(nc, m, a):
    with ExitStack() as ctx:
        sb, _, _ = place(nc, ctx, "setup")
        s = Segments(nc, ctx, "setup_masks", R4)
        segment_masks(nc, m, a, s, "setup_masks", R4)
        kind = sb("kind", [P, R4, EB, P])
        count = sb("count", [P, R4, EB, P])
        ints = sb("ints", [P, 3, EB, P])
        src_key = sb("src_key", [P, EB, P])
        high = sb("high", [P, EB, P])
        rel = sb("rel", [P, EB, P])
        weight = sb("weight", [P, EB, P])
        with ExitStack() as inner:
            sb, _, sem = place(nc, inner, "setup_load")
            padded, loaded, split, keyed, kept = sem("padded", "loaded", "split", "keyed", "kept")
            low, keys = sb("low", [P, EB, P]), sb("keys", [P, 3, EB, P], BF16)
            raw = sb("raw", [P, 3, EB, P], I32)
            ea = sb("ea", [P, EB, 2 * P])
            ea2 = sb("ea2", [P, 2, EB, P])
            block = inner.enter_context(nc.Block())

            @block.sync
            def _(sp):
                sp.wait_ge(padded, 3)
                load_edge_rows(sp, raw[:, 0], a["src"], loaded)
                load_edge_rows(sp, raw[:, 1], a["edge_type_4"], loaded)
                load_edge_rows(sp, raw[:, 2], a["edge_type_8"], loaded)
                load_edge_rows(sp, weight, a["edge_weight"], loaded)
                flat = a["edge_attr_2"].rearrange("e k -> (e k)")
                last = FULL - (EB - 1) * P
                full, most = FULL * P * 2, (EB - 1) * P * P * 2
                sp.dma_start(ea[:, 0:EB - 1, :], flat[0:most].rearrange("(b t p) -> t b p", t=P, p=2 * P)).then_inc(loaded, 16)
                sp.dma_start(ea[0:last, EB - 1, :], flat[most:full].rearrange("(t p) -> t p", p=2 * P)).then_inc(loaded, 16)
                sp.dma_start(ea[last:last + 1, EB - 1, 0:2 * REST], flat[full:2 * EDGES].rearrange("(t p) -> t p", t=1)).then_inc(loaded, 16)
                sp.wait_ge(split, 3)
                for k in range(2):
                    sp.dma_start(m.t_ea[k].rearrange("(b t p) -> t b p", t=P, p=P), ea2[:, k]).then_inc(kept, 16)
                sp.wait_ge(keyed, 3)
                for k in range(3):
                    sp.dma_start(m.t_keys[k].rearrange("(b t p) -> t b p", t=P, p=P), keys[:, k]).then_inc(kept, 16)
                sp.wait_ge(kept, 5 * 16)

            @block.vector
            def _(dve):
                nc.vector.memset(raw[:], 0).then_inc(padded, 1)
                nc.vector.memset(weight[:], 0.0).then_inc(padded, 1)
                nc.vector.memset(ea[:], 0.0).then_inc(padded, 1)
                dve.wait_ge(padded, 3)
                dve.wait_ge(loaded, 16 * 15)
                link = chain(dve, m)
                nc.vector.tensor_copy(ints[:], raw[:]).then_inc(split, 1)
                for k in range(2):
                    nc.vector.tensor_copy(ea2[:, k], ea[:].rearrange("t b (p k) -> t k b p", k=2)[:, k]).then_inc(split, 1)
                dve.wait_ge(split, 3)
                for r in range(R4):
                    link(nc.vector.tensor_scalar(kind[:, r], ints[:, 1], float(r), None, ALU.is_equal))
                valid = count[:, 0]
                link(nc.vector.tensor_scalar(valid, s.dst[:], float(NODES), None, ALU.is_lt))
                link(nc.vector.tensor_tensor(rel[:], s.dst[:], s.dst[:, :, 0:1].to_broadcast([P, EB, P]), ALU.subtract))
                link(nc.vector.scalar_tensor_tensor(rel[:], rel[:], 1.0, valid, ALU.add, ALU.mult))
                link(nc.vector.tensor_scalar(rel[:], rel[:], 1.0, None, ALU.subtract))
                link(nc.vector.scalar_tensor_tensor(src_key[:], ints[:, 0], 1.0, valid, ALU.add, ALU.mult))
                link(nc.vector.tensor_scalar(src_key[:], src_key[:], 1.0, None, ALU.subtract))
                link(nc.vector.tensor_scalar(high[:], src_key[:], 63.5, 1.0 / P, ALU.subtract, ALU.mult))
                link(nc.vector.tensor_scalar(high[:], high[:], ROUNDER, None, ALU.add))
                link(nc.vector.tensor_scalar(high[:], high[:], ROUNDER, None, ALU.subtract))
                link(nc.vector.scalar_tensor_tensor(low[:], high[:], -float(P), src_key[:], ALU.mult, ALU.add))
                for k, part in ((REL, rel), (LOW, low), (HIGH, high)):
                    nc.vector.tensor_copy(keys[:, k], part[:]).then_inc(keyed, 1)
        segment_totals(nc, m, s, "setup_count", kind, count, R4)
        with ExitStack() as inner:
            _, pb, sem = place(nc, inner, "setup_index")
            turned = sem("turned")
            row = pb("base_row", [1, 1024])
            block = inner.enter_context(nc.Block())

            @block.vector
            def _(dve):
                link = chain(dve, m)
                link(nc.vector.tensor_tensor(kind[:], kind[:], count[:], ALU.mult))
                link(nc.vector.tensor_tensor(kind[:, 0:2], kind[:, 0:2], kind[:, 2:4], ALU.add))
                link(nc.vector.tensor_tensor(kind[:, 0], kind[:, 0], kind[:, 1], ALU.add))
                link(nc.vector.tensor_scalar(kind[:, 0], kind[:, 0], 1.0, None, ALU.max))
                link(nc.vector.reciprocal(kind[:, 3], kind[:, 0]))
                link(nc.vector.scalar_tensor_tensor(ints[:, 1], ints[:, 0], float(R4), ints[:, 1], ALU.mult, ALU.add))
                link(nc.vector.scalar_tensor_tensor(ints[:, 2], ints[:, 0], float(R8), ints[:, 2], ALU.mult, ALU.add))
                dve.wait_ge(turned, EB)
                link(nc.vector.tensor_copy(m.base[:], row[:, 0:TP]))

            @block.tensor
            def _(pe):
                for b in range(EB):
                    nc.tensor.transpose(row[:, b * P:(b + 1) * P], s.dst[:, b, 0:1], m.ident[:]).then_inc(turned, 1)
        turn_edges(nc, m, "setup_turn", [
            (ints[:, 0], by_block(m.src)), (src_key, by_block(m.src_key)), (high, by_block(m.src_high)), (ints[:, 1], by_block(m.src4)),
            (ints[:, 2], by_block(m.src8)), (rel, by_block(m.rel)), (kind[:, 3], by_block(m.w_rgcn)),
            (weight, by_block(m.w_edge))])


def bases(nc, m, t, engine):
    return nc.values_load_multi_w_load_instructions(
        m.base[0:1, bass.ds(t, HU)], engines=[engine], min_val=0, max_val=NODES,
        skip_runtime_bounds_check_because="a first destination is a node, or NODES in the padding")[1]


def aggregate(nc, m, phase, table, index, weights, blocks, clear=True, degree=False):
    e = m.edge
    heads = max(1, len(weights))
    row = heads * blocks * P
    outs = 2 if degree else blocks
    n = e.passes
    e.passes += 1
    hots0, e.hots = e.hots, e.hots + (T + HU) * heads
    half0, done0, used0, staged0 = n * ITERS, n * ITERS * (U - 2), n * T, n * 2 * ITERS
    with ExitStack() as ctx:
        sb, pb, sem = place(nc, ctx, phase)
        message = [sb(f"message{u}", [P, row]) for u in range(U)]
        hot = sb("hot", [P, U, heads * P])
        stage = [sb(f"index_stage{h}", [P, HU], I32) for h in range(2)]
        ps = [pb(f"window{k}", [P, outs, P]) for k in range(HU)]
        cleared = sem("cleared")
        block = ctx.enter_context(nc.Block())

        @block.scalar
        def _(act):
            with act.Fori(0, ITERS, 1) as it:
                for h in range(2):
                    act.wait_ge(e.half_used[h], half0 + it)
                    nc.scalar.copy(stage[h][:], index[:, bass.ds(it * U + h * HU, HU)]).then_inc(e.staged, 1)

        @block.gpsimd
        def _(pool):
            with pool.Fori(0, ITERS, 1) as it:
                for u in range(U):
                    h, k = divmod(u, HU)
                    if k == 0:
                        pool.wait_ge(e.carried, staged0 + it * 2 + h)
                        pool.wait_ge(e.staged, staged0 + it * 2 + h + 1)
                        nc.gpsimd.tensor_tensor(m.carrier[:], m.ones_i[:], m.ones_i[:], ALU.add).then_inc(e.carried, 1)
                    pool.indirect_dma_start(message[u][:], None, table,
                                            bass.IndirectOffsetOnAxis(ap=stage[h][:, k:k + 1], axis=0)).then_inc(e.gathered[u], 16)

        @block.vector
        def _(dve):
            def one_hot(t, u):
                for k in range(heads):
                    if weights:
                        ins = nc.vector.tensor_scalar(hot[:, u, k * P:(k + 1) * P], m.iota[:], m.rel[:, t], weights[k][:, t],
                                                      ALU.is_equal, ALU.mult)
                    else:
                        ins = nc.vector.tensor_scalar(hot[:, u, :], m.iota[:], m.rel[:, t], None, ALU.is_equal)
                    ins.then_inc(e.hot_ready, 1)

            if clear:
                nc.vector.memset(m.acc[:, 0:outs, :], 0.0).then_inc(cleared, 1)
                dve.wait_ge(cleared, 1)
            for u in range(HU):
                one_hot(slice(u, u + 1), u)
            with dve.Fori(0, ITERS, 1) as it:
                for u in range(U):
                    h, k = divmod(u, HU)
                    if k == 0:
                        dve.wait_ge(e.half_used[1 - h], half0 + it + h)
                        base = bases(nc, m, it * U + u, DVE)
                    one_hot(bass.ds(it * U + u + HU, 1), (u + HU) % U)
                    if k == HU - 1:
                        dve.wait_ge(e.half_used[h], half0 + it + 1)
                    else:
                        dve.wait_ge(e.window_ready, done0 + it * (U - 2) + u + 1 - h)
                    dve.wait_ge(e.window_used, used0 + it * U + u)
                    window = m.acc[:, 0:outs, bass.ds(base[k], P)]
                    nc.vector.tensor_tensor(window, window, ps[k][:], ALU.add).then_inc(e.window_used, 1)

        @block.tensor
        def _(pe):
            with pe.Fori(0, ITERS, 1) as it:
                for u in range(U):
                    h, k = divmod(u, HU)
                    if k == 0:
                        pe.wait_ge(e.window_used, used0 + it * U + u)
                    pe.wait_ge(e.hot_ready, hots0 + (it * U + u + 1) * heads)
                    pe.wait_ge(e.gathered[u], 16 * (half0 + it + 1))
                    for b in range(blocks):
                        for j in range(heads):
                            f = (j * blocks + b) * P
                            last = nc.tensor.matmul(ps[k][:, b, :], message[u][:, f:f + P], hot[:, u, j * P:(j + 1) * P],
                                                    start=(j == 0), stop=(j == heads - 1))
                    if degree:
                        last = nc.tensor.matmul(ps[k][:, 1, :], m.ones[:], hot[:, u, :], start=True, stop=True)
                    last.then_inc(e.half_used[h] if k == HU - 1 else e.window_ready, 1)


def load_weights(nc, m, phase, loads):
    with ExitStack() as ctx:
        _, _, sem = place(nc, ctx, phase)
        loaded = sem("weights")
        block = ctx.enter_context(nc.Block())

        @block.sync
        def _(sp):
            for tile, source in loads:
                sp.dma_start(tile, source).then_inc(loaded, 16)
            sp.wait_ge(loaded, 16 * len(loads))


def row_of(vector):
    return vector.rearrange("(a n) -> a n", a=1)


def layer_norm(nc, dve, link, b, y, out):
    for j in range(GN):
        ins = nc.vector.bn_stats(b.stats[:, j, :], y[:, j, :])
        if j == GN - 1:
            link(ins)
        else:
            ins.then_inc(b.stat_ready, 1)
    dve.wait_ge(b.stat_ready, b.g * (GN - 1) + GN - 1)
    nc.vector.memset(b.spare[:], 0.0)
    for j in range(GN):
        ins = nc.vector.bn_aggr(b.moments[:, j, :], b.stats[:, j, :])
        ins.then_inc(b.var_ready, 1)
    dve.wait_ge(b.root_ready, b.g + 1)
    link(nc.vector.reciprocal(b.rstd[:], b.root[:]))
    for j in range(GN):
        ins = nc.vector.tensor_scalar(out[:, j, :], y[:, j, :], b.moments[:, j, 0:1], b.rstd[:, j:j + 1], ALU.subtract, ALU.mult)
        ins.then_inc(b.norm_ready, 1)


def layer_norm_root(nc, act, m, b):
    act.wait_ge(b.var_ready, (b.g + 1) * GN)
    nc.scalar.activation(b.root[:], b.moments[:, :, 1], ACT.Sqrt, bias=m.epsilon[:], scale=1.0).then_inc(b.root_ready, 1)


class NormBuffers:
    def __init__(self, sb, sem):
        self.g = None
        self.stats, self.moments = sb("stats", [P, GN, 6]), sb("moments", [P, GN, 2])
        self.root, self.rstd, self.spare = sb("root", [P, GN]), sb("rstd", [P, GN]), sb("spare", [P, 1])
        self.stat_ready, self.var_ready, self.root_ready, self.norm_ready = sem("stat_ready", "var_ready", "root_ready", "norm_ready")


def degrees(nc, m):
    with ExitStack() as ctx:
        sb, _, _ = place(nc, ctx, "degrees")
        ends = sb("ends", [P, NT, P])
        block = ctx.enter_context(nc.Block())
        degree = m.acc[:, 1, 0:ROWS]

        @block.vector
        def _(dve):
            link = chain(dve, m)
            flat = ends[:].rearrange("p j n -> p (j n)")
            diagonal = m.ident[:].rearrange("p (j n) -> p j n", j=1).to_broadcast([P, NT, P])
            link(nc.vector.tensor_tensor_scan(flat, degree, degree, 0.0, ALU.add, ALU.max))
            link(nc.vector.tensor_tensor(ends[:], ends[:], diagonal, ALU.mult))
            link(nc.vector.tensor_reduce(m.last_edge_f[:], ends[:], AX.X, ALU.add))
            link(nc.vector.tensor_scalar(m.last_edge_f[:], m.last_edge_f[:], 1.0, 0.0, ALU.subtract, ALU.max))
            link(nc.vector.tensor_copy(m.last_edge[:], m.last_edge_f[:]))
            link(nc.vector.tensor_tensor(ends[:], degree.rearrange("p (j n) -> p j n", n=P), diagonal, ALU.mult))
            link(nc.vector.tensor_reduce(m.has_edges[:], ends[:], AX.X, ALU.add))
            link(nc.vector.tensor_scalar(m.has_edges[:], m.has_edges[:], 1.0, None, ALU.min))
            link(nc.vector.tensor_scalar(m.inv_degree[:], degree, 1.0, None, ALU.max))
            link(nc.vector.reciprocal(m.inv_degree[:], m.inv_degree[:]))


def group_cols(g):
    return bass.ds(g * GW, GW)


def group_tiles(g):
    return bass.ds(g * GN, GN)


def after_block0(nc, m, a):
    with ExitStack() as ctx:
        sb, pb, sem = place(nc, ctx, "n0")
        w_in, w_t = sb("w_in", [P, C]), sb("w_t", [P, C])
        bias = sb("bias", [1, C])
        load_weights(nc, m, "n0_load", [(w_in[:], a["L0_gnn_W_neigh"]), (bias[:], row_of(a["L0_gnn_b_neigh"]))])
        mean = sb("mean", [P, GN, P])
        y = sb("y", [P, GN, C])
        ps_w, ps = pb("ps_w", [P, C]), pb("ps", [P, 8, C])
        b = NormBuffers(sb, sem)
        w_turned, w_ready, staged, made, taken, steps, stored = sem("w_turned", "w_ready", "staged", "made", "taken", "steps", "stored")
        block = ctx.enter_context(nc.Block())

        @block.tensor
        def _(pe):
            nc.tensor.transpose(ps_w[:], w_in[:], m.ident[:]).then_inc(w_turned, 1)
            pe.wait_ge(w_ready, 1)
            with pe.Fori(0, NG, 1) as g:
                pe.wait_ge(staged, g + 1)
                pe.wait_ge(taken, g)
                for j in range(GN):
                    nc.tensor.matmul(ps[:, j, :], m.ones[0:1, :], bias[:], start=True, stop=False)
                    last = nc.tensor.matmul(ps[:, j, :], mean[:, j, :], w_t[:], start=False, stop=True)
                last.then_inc(made, 1)

        @block.scalar
        def _(act):
            with act.Fori(0, NG, 1) as g:
                b.g = g
                layer_norm_root(nc, act, m, b)

        @block.vector
        def _(dve):
            dve.wait_ge(w_turned, 1)
            nc.vector.tensor_copy(w_t[:], ps_w[:]).then_inc(w_ready, 1)
            with dve.Fori(0, NG, 1) as g:
                b.g = g
                link = LoopChain(dve, steps, g, 2)
                dve.wait_ge(made, g)
                nc.vector.tensor_tensor(mean[:].rearrange("p j n -> p (j n)"), m.acc[:, 0, group_cols(g)],
                                        m.inv_degree[:, group_cols(g)], ALU.mult).then_inc(staged, 1)
                dve.wait_ge(made, g + 1)
                dve.wait_ge(b.norm_ready, g * GN)
                nc.vector.tensor_tensor(y[:], ps[:, 0:GN, :], m.x[:, group_tiles(g), :], ALU.add).then_inc(taken, 1)
                dve.wait_ge(taken, g + 1)
                layer_norm(nc, dve, link, b, y, m.x[:, group_tiles(g), :])
                link.end()

        @block.sync
        def _(sp):
            with sp.Fori(0, NG, 1) as g:
                sp.wait_ge(b.norm_ready, (g + 1) * GN)
                sp.dma_start(node_rows(m.t_x, g, C), m.x[:, group_tiles(g), :]).then_inc(stored, 16)
            sp.wait_ge(stored, 16 * NG)


def after_sage1(nc, m, a):
    with ExitStack() as ctx:
        sb, pb, sem = place(nc, ctx, "n1")
        wl, wr, bias = sb("wl", [P, H]), sb("wr", [P, H]), sb("bias", [1, H])
        load_weights(nc, m, "n1_load", [(wl[:], a["L1_gnn_sage1_Wl"]), (wr[:], a["L1_gnn_sage1_Wr"]), (bias[:], row_of(a["L1_gnn_sage1_b"]))])
        mean, x, x_t = sb("mean", [P, GN, P]), sb("x", [P, GN, P]), sb("x_t", [P, GN, P])
        out = sb("out", [P, GN, H])
        ps_t, ps = pb("ps_t", [P, 8, P]), pb("ps", [P, 8, H])
        staged, copied, turned, kept, made, taken, stored = sem("staged", "copied", "turned", "kept", "made", "taken", "stored")
        block = ctx.enter_context(nc.Block())

        @block.scalar
        def _(act):
            with act.Fori(0, NG, 1) as g:
                act.wait_ge(turned, g)
                nc.scalar.copy(x[:], m.x[:, group_tiles(g), :]).then_inc(copied, 1)
                act.wait_ge(made, g + 1)
                act.wait_ge(stored, 16 * g)
                nc.scalar.activation(out[:], ps[:, 0:GN, :], ACT.Relu).then_inc(taken, 1)

        @block.vector
        def _(dve):
            with dve.Fori(0, NG, 1) as g:
                dve.wait_ge(made, g)
                nc.vector.tensor_tensor(mean[:].rearrange("p j n -> p (j n)"), m.acc[:, 0, group_cols(g)],
                                        m.inv_degree[:, group_cols(g)], ALU.mult).then_inc(staged, 1)
                dve.wait_ge(turned, g + 1)
                nc.vector.tensor_copy(x_t[:], ps_t[:, 0:GN, :]).then_inc(kept, 1)

        @block.tensor
        def _(pe):
            with pe.Fori(0, NG, 1) as g:
                pe.wait_ge(copied, g + 1)
                for j in range(GN):
                    last = nc.tensor.transpose(ps_t[:, j, :], x[:, j, :], m.ident[:])
                last.then_inc(turned, 1)
                pe.wait_ge(staged, g + 1)
                pe.wait_ge(kept, g + 1)
                pe.wait_ge(taken, g)
                for j in range(GN):
                    nc.tensor.matmul(ps[:, j, :], m.ones[0:1, :], bias[:], start=True, stop=False)
                    nc.tensor.matmul(ps[:, j, :], mean[:, j, :], wl[:], start=False, stop=False)
                    last = nc.tensor.matmul(ps[:, j, :], x_t[:, j, :], wr[:], start=False, stop=True)
                last.then_inc(made, 1)

        @block.sync
        def _(sp):
            with sp.Fori(0, NG, 1) as g:
                sp.wait_ge(taken, g + 1)
                sp.dma_start(node_rows(m.t_s1, g, H), out[:]).then_inc(stored, 16)
            sp.wait_ge(stored, 16 * NG)


def attention_weights(nc, m, a, phase, w, w_al):
    with ExitStack() as ctx:
        sb, _, sem = place(nc, ctx, phase)
        att = sb("att", [P, 2, 2 * H])
        product = sb("product", [P, 2, H])
        loaded = sem("loaded")
        block = ctx.enter_context(nc.Block())

        @block.sync
        def _(sp):
            for k, vectors in enumerate((a["L1_gnn_gat_att_src"], a["L1_gnn_gat_att_dst"])):
                row = vectors.rearrange("(a h) c -> a (h c)", a=1)
                sp.dma_start(att[:, k, :], row.to_broadcast([P, 2 * H])).then_inc(loaded, 16)
            sp.wait_ge(loaded, 32)

        @block.vector
        def _(dve):
            link = chain(dve, m)
            dve.wait_ge(loaded, 32)
            for k in range(2):
                for b in range(2):
                    link(nc.vector.tensor_tensor(product[:].rearrange("p h c -> p (h c)"), w[:, b, :], att[:, k, :], ALU.mult))
                    link(nc.vector.tensor_reduce(w_al[:, b, 2 * k:2 * k + 2], product[:], AX.X, ALU.add))


def by_half(weights):
    return weights.rearrange("(b k) n -> k b n", k=P)


def after_sage2(nc, m, a):
    FA = C + 4
    with ExitStack() as ctx:
        sb, pb, sem = place(nc, ctx, "n2")
        wl, wr, wg = sb("wl", [P, 2, H]), sb("wr", [P, 2, H]), sb("wg", [P, 2, 2 * H])
        wf, w_al = sb("wf", [P, 2, C]), sb("w_al", [P, 2, 4])
        bias, bias_f = sb("bias", [1, H]), sb("bias_f", [1, C])
        load_weights(nc, m, "n2_load", [
            (wl[:], by_half(a["L1_gnn_sage2_Wl"])), (wr[:], by_half(a["L1_gnn_sage2_Wr"])), (wg[:], by_half(a["L1_gnn_gat_W"])),
            (wf[:], by_half(a["L1_gnn_fusion_W"][0:H, :])), (bias[:], row_of(a["L1_gnn_sage2_b"])), (bias_f[:], row_of(a["L1_gnn_fusion_b"]))])
        attention_weights(nc, m, a, "n2_att", wg, w_al)
        mean = sb("mean", [P, 2, GN, P])
        s1, s2 = sb("s1", [P, GN, H]), sb("s2", [P, GN, H])
        turned_rows = sb("turned_rows", [P, 2, GN, P])
        h_out, fa_out = sb("h_out", [P, GN, 2 * H]), sb("fa_out", [P, GN, FA])
        ps_t, ps = pb("ps_t", [P, 4, 512]), pb("ps", [P, 4, 512])
        loaded, staged, turned1, kept1, made, relued, turned2, kept2, fa_made, fa_taken, h_made, h_taken, stored = sem(
            "loaded", "staged", "turned1", "kept1", "made", "relued", "turned2", "kept2", "fa_made", "fa_taken", "h_made", "h_taken", "stored")
        block = ctx.enter_context(nc.Block())
        tile = lambda k, j: ps_t[:].rearrange("p b (s n) -> p (b s) n", n=P)[:, k * 8 + j, :]
        halves = ps_t[:].rearrange("p (k b) (s n) -> p k (b s) n", k=2, n=P)
        wide = ps[:].rearrange("p b (s n) -> p (b s) n", n=H)
        fa = ps_t[:].rearrange("p b (s n) -> p (b s) n", n=H)

        @block.sync
        def _(sp):
            with sp.Fori(0, NG, 1) as g:
                sp.wait_ge(turned1, g)
                sp.dma_start(s1[:], node_rows(m.t_s1, g, H)).then_inc(loaded, 16)
                sp.wait_ge(fa_taken, g + 1)
                sp.dma_start(node_rows(m.t_f, g, C), fa_out[:, :, 0:C]).then_inc(stored, 16)
                sp.dma_start(node_rows(m.t_al, g, 4), fa_out[:, :, C:FA]).then_inc(stored, 16)
                sp.wait_ge(h_taken, (g + 1) * GN)
                sp.dma_start(node_rows(m.t_h, g, 2 * H), h_out[:]).then_inc(stored, 16)
            sp.wait_ge(stored, 48 * NG)

        @block.vector
        def _(dve):
            with dve.Fori(0, NG, 1) as g:
                dve.wait_ge(made, g)
                for k in range(2):
                    nc.vector.tensor_tensor(mean[:, k].rearrange("p j n -> p (j n)"), m.acc[:, k, group_cols(g)],
                                            m.inv_degree[:, group_cols(g)], ALU.mult).then_inc(staged, 1)
                dve.wait_ge(fa_made, g + 1)
                dve.wait_ge(stored, 48 * g)
                nc.vector.tensor_copy(fa_out[:], fa[:, 0:GN, 0:FA]).then_inc(fa_taken, 1)
                for j in range(GN):
                    dve.wait_ge(h_made, g * GN + j + 1)
                    nc.vector.tensor_copy(h_out[:, j, :], ps[:, j % 4, :]).then_inc(h_taken, 1)

        @block.scalar
        def _(act):
            with act.Fori(0, NG, 1) as g:
                act.wait_ge(turned1, g + 1)
                act.wait_ge(h_made, g * GN)
                nc.scalar.copy(turned_rows[:], halves[:, :, 0:GN, :]).then_inc(kept1, 1)
                act.wait_ge(made, g + 1)
                nc.scalar.activation(s2[:], wide[:, 0:GN, :], ACT.Relu).then_inc(relued, 1)
                act.wait_ge(turned2, g + 1)
                nc.scalar.copy(turned_rows[:], halves[:, :, 0:GN, :]).then_inc(kept2, 1)

        @block.tensor
        def _(pe):
            with pe.Fori(0, NG, 1) as g:
                pe.wait_ge(loaded, 16 * (g + 1))
                pe.wait_ge(fa_taken, g)
                for j in range(GN):
                    for k in range(2):
                        last = nc.tensor.transpose(tile(k, j), s1[:, j, k * P:(k + 1) * P], m.ident[:])
                last.then_inc(turned1, 1)
                pe.wait_ge(staged, 2 * (g + 1))
                pe.wait_ge(kept1, g + 1)
                pe.wait_ge(h_taken, g * GN)
                for j in range(GN):
                    nc.tensor.matmul(wide[:, j, :], m.ones[0:1, :], bias[:], start=True, stop=False)
                    for k in range(2):
                        nc.tensor.matmul(wide[:, j, :], mean[:, k, j, :], wl[:, k, :], start=False, stop=False)
                        last = nc.tensor.matmul(wide[:, j, :], turned_rows[:, k, j, :], wr[:, k, :], start=False, stop=(k == 1))
                last.then_inc(made, 1)
                pe.wait_ge(relued, g + 1)
                for j in range(GN):
                    for k in range(2):
                        last = nc.tensor.transpose(tile(k, j), s2[:, j, k * P:(k + 1) * P], m.ident[:])
                last.then_inc(turned2, 1)
                pe.wait_ge(kept2, g + 1)
                for j in range(GN):
                    nc.tensor.matmul(fa[:, j, 0:C], m.ones[0:1, :], bias_f[:], start=True, stop=False)
                    for k in range(2):
                        nc.tensor.matmul(fa[:, j, 0:C], turned_rows[:, k, j, :], wf[:, k, :], start=False, stop=(k == 1))
                    for k in range(2):
                        last = nc.tensor.matmul(fa[:, j, C:FA], turned_rows[:, k, j, :], w_al[:, k, :], start=(k == 0), stop=(k == 1))
                last.then_inc(fa_made, 1)
                for j in range(GN):
                    if j >= 4:
                        pe.wait_ge(h_taken, g * GN + j - 3)
                    for k in range(2):
                        last = nc.tensor.matmul(ps[:, j % 4, :], turned_rows[:, k, j, :], wg[:, k, :], start=(k == 0), stop=(k == 1))
                    last.then_inc(h_made, 1)


def bank_before(sem, it, q):
    return (sem[q - 2], it + 1) if q >= 2 else (sem[q + 2], it)


def window_load(nc, m, sp, rows, table, width, it, h, loaded):
    base = bases(nc, m, it * U + h * HU, SP)
    for k in range(HU):
        u = h * HU + k
        sp.dma_start(rows[:, u, :], table[bass.ds(base[k], P), 0:width]).then_inc(loaded[u // QU], 16)


def turned_one_hot(nc, m, act, spread, distance, out, ready, ready_n, done):
    nc.scalar.activation(distance, spread, ACT.Abs, bias=m.minus_column[:], scale=1.0).then_inc(ready, 1)
    act.wait_ge(ready, ready_n)
    nc.scalar.activation(out, distance, ACT.Relu, bias=m.ones[:, 0:1], scale=-1.0).then_inc(done, 1)


def attention_terms(nc, m):
    with ExitStack() as ctx:
        sb, pb, sem = place(nc, ctx, "al")
        table, columns = sb("table", [P, NT, 4]), sb("columns", [P, 2, NT])
        keys = sb("keys", [1, QUADS, QU * P], BF16)
        low_hot, distance = sb("low_hot", [P, 2, QU * P]), sb("distance", [P, 2, QU * P])
        high_hot, product = sb("high_hot", [P, 2, QU, NT]), sb("product", [P, 2, QU, 2, NT])
        picked = sb("picked", [P, 2, QU, 2])
        ps_low = [pb(f"ps_low{k}", [P, QU * P]) for k in range(2)]
        ps = [pb(f"ps{k}", [P, QU, P]) for k in range(2)]
        keys_in, spread, low_ready, looked, high_ready, product_ready, reduced, kept = (
            [sem(f"{n}{q}") for q in range(QUADS)]
            for n in ("keys_in", "spread", "low_ready", "looked", "high_ready", "product_ready", "reduced", "kept"))
        table_in, table_ready, distance_ready, zeroed, placed = sem("table_in", "table_ready", "distance_ready", "zeroed", "placed")
        block = ctx.enter_context(nc.Block())

        @block.sync
        def _(sp):
            sp.dma_start(table[:], m.t_al[0:ROWS, :].rearrange("(j p) f -> p j f", p=P)).then_inc(table_in, 16)
            with sp.Fori(0, ITERS, 1) as it:
                for q in range(QUADS):
                    sp.wait_ge(spread[q], it)
                    sp.dma_start(keys[:, q], m.t_keys[LOW:LOW + 1, bass.ds((it * U + q * QU) * P, QU * P)]).then_inc(keys_in[q], 16)

        @block.gpsimd
        def _(pool):
            pool.wait_ge(table_in, 16)
            for j in range(NT):
                rows = P if j < NT - 1 else TAIL
                pool.indirect_dma_start(m.t_last, bass.IndirectOffsetOnAxis(ap=m.last_edge[0:rows, j:j + 1], axis=0), table[0:rows, j, :],
                                        None).then_inc(placed, 16)
            pool.wait_ge(placed, 16 * NT)

        @block.scalar
        def _(act):
            def keep(it, q):
                act.wait_ge(zeroed, 1)
                act.wait_ge(reduced[q], it + 1)
                tiles = bass.ds(it * U + q * QU, QU)
                nc.scalar.copy(m.e[:, :, tiles].rearrange("p k t -> p t k"), picked[:, q % 2]).then_inc(kept[q], 1)

            with act.Fori(0, ITERS, 1) as it:
                for q in range(QUADS):
                    act.wait_ge(spread[q], it + 1)
                    act.wait_ge(*bank_before(looked, it, q))
                    turned_one_hot(nc, m, act, ps_low[q % 2][:], distance[:, q % 2, :], low_hot[:, q % 2, :],
                                   distance_ready, it * QUADS + q + 1, low_ready[q])
                    if q >= 2:
                        keep(it, q - 2)
                for q in range(QUADS - 2, QUADS):
                    keep(it, q)

        @block.vector
        def _(dve):
            dve.wait_ge(table_in, 16)
            nc.vector.tensor_copy(columns[:].rearrange("p k j -> p j k"), table[:, :, 0:2]).then_inc(table_ready, 1)
            nc.vector.memset(m.e[:], 0.0).then_inc(zeroed, 1)

            def reduce(it, q):
                dve.wait_ge(product_ready[q], it + 1)
                dve.wait_ge(*bank_before(kept, it, q))
                nc.vector.tensor_reduce(picked[:, q % 2], product[:, q % 2], AX.X, ALU.add).then_inc(reduced[q], 1)

            with dve.Fori(0, ITERS, 1) as it:
                for q in range(QUADS):
                    p = q % 2
                    dve.wait_ge(*bank_before(product_ready, it, q))
                    high = m.src_high[:, bass.ds(it * U + q * QU, QU)].rearrange("p (t a) -> p t a", a=1).to_broadcast([P, QU, NT])
                    places = m.iota[:, 0:NT].rearrange("p (a j) -> p a j", a=1).to_broadcast([P, QU, NT])
                    nc.vector.tensor_tensor(high_hot[:, p], places, high, ALU.is_equal).then_inc(high_ready[q], 1)
                    if q >= 1:
                        reduce(it, q - 1)
                    dve.wait_ge(high_ready[q], it + 1)
                    dve.wait_ge(looked[q], it + 1)
                    dve.wait_ge(*bank_before(reduced, it, q))
                    nc.vector.tensor_tensor(product[:, p], ps[p][:, :, 0:2 * NT].rearrange("p t (k j) -> p t k j", k=2),
                                            high_hot[:, p].rearrange("p t (a j) -> p t a j", a=1).to_broadcast([P, QU, 2, NT]),
                                            ALU.mult).then_inc(product_ready[q], 1)
                reduce(it, QUADS - 1)

        @block.tensor
        def _(pe):
            def look_up(it, q):
                pe.wait_ge(low_ready[q], it + 1)
                pe.wait_ge(*bank_before(product_ready, it, q))
                for k in range(QU):
                    last = nc.tensor.matmul(ps[q % 2][:, k, 0:2 * NT], low_hot[:, q % 2, k * P:(k + 1) * P],
                                            columns[:].rearrange("p k j -> p (k j)"), start=True, stop=True)
                last.then_inc(looked[q], 1)

            pe.wait_ge(table_ready, 1)
            with pe.Fori(0, ITERS, 1) as it:
                for q in range(QUADS):
                    pe.wait_ge(keys_in[q], 16 * (it + 1))
                    pe.wait_ge(*bank_before(low_ready, it, q))
                    nc.tensor.matmul(ps_low[q % 2][:], m.spread_one[:], keys[:, q], start=True, stop=True).then_inc(spread[q], 1)
                    if q >= 1:
                        look_up(it, q - 1)
                look_up(it, QUADS - 1)


def attention_softmax(nc, m, a):
    with ExitStack() as ctx:
        sb, _, _ = place(nc, ctx, "softmax")
        s = Segments(nc, ctx, "softmax_masks", 4)
        segment_masks(nc, m, a, s, "softmax_masks", 4)
        at_dst = sb("at_dst", [P, 4, EB, P])
        top, total = at_dst[:, 0:2], at_dst[:, 2:4]
        with ExitStack() as inner:
            sb_in, _, sem = place(nc, inner, "softmax_dst")
            last_in = sem("last_in")
            last = sb_in("last", [P, EB, P, 4])
            with nc.Block() as block:
                @block.sync
                def _(sp):
                    sp.dma_start(last[:].rearrange("t b p k -> t b (p k)"), m.t_last.rearrange("(b t p) k -> t b (p k)", t=P, p=P)).then_inc(last_in, 16)
                    sp.wait_ge(last_in, 16)
            segment_totals(nc, m, s, "softmax_dst", last[:].rearrange("t b p k -> t k b p"), at_dst, 4)
        e, own = sb("e", [P, 2, EB, P]), sb("own", [P, 2, EB, P])
        self_weight = sb("self_weight", [P, EB, P, 2])
        turn_edges(nc, m, "softmax_turn", [(by_block(m.e[:, k]), e[:, k]) for k in range(2)])
        with ExitStack() as inner:
            block = inner.enter_context(nc.Block())

            @block.vector
            def _(dve):
                link = chain(dve, m)
                link(nc.vector.tensor_tensor(e[:], e[:], at_dst[:, 2:4], ALU.add))
                link(nc.vector.tensor_tensor(own[:], at_dst[:, 0:2], at_dst[:, 2:4], ALU.add))
                for t in (e, own):
                    link(nc.vector.tensor_scalar(total, t[:], 0.2, None, ALU.mult))
                    link(nc.vector.tensor_tensor(t[:], t[:], total, ALU.max))
        segment_totals(nc, m, s, "softmax_top", e, top, 2, maximum=True)
        with ExitStack() as inner:
            _, _, sem = place(nc, inner, "softmax_exp")
            shifted, raised = sem("shifted", "raised")
            block = inner.enter_context(nc.Block())

            @block.vector
            def _(dve):
                link = chain(dve, m)
                link(nc.vector.tensor_tensor(top, top, own[:], ALU.max))
                nc.vector.tensor_tensor(e[:], e[:], top, ALU.subtract).then_inc(shifted, 1)
                nc.vector.tensor_tensor(own[:], own[:], top, ALU.subtract).then_inc(shifted, 1)

            @block.scalar
            def _(act):
                for n, t in enumerate((e, own)):
                    act.wait_ge(shifted, n + 1)
                    nc.scalar.activation(t[:], t[:], ACT.Exp).then_inc(raised, 1)
                act.wait_ge(raised, 2)
        segment_totals(nc, m, s, "softmax_sum", e, total, 2)
        with ExitStack() as inner:
            sb, _, sem = place(nc, inner, "softmax_self")
            weighed, kept = sem("weighed", "kept")
            block = inner.enter_context(nc.Block())

            @block.vector
            def _(dve):
                link = chain(dve, m)
                link(nc.vector.tensor_tensor(total, total, own[:], ALU.add))
                link(nc.vector.tensor_scalar(total, total, 1e-16, None, ALU.max))
                link(nc.vector.reciprocal(top, total))
                link(nc.vector.tensor_scalar(top, top, 0.5, None, ALU.mult))
                link(nc.vector.tensor_tensor(e[:], e[:], top, ALU.mult))
                nc.vector.tensor_tensor(self_weight[:].rearrange("p b t k -> p k b t"), own[:], top, ALU.mult).then_inc(weighed, 1)

            @block.sync
            def _(sp):
                sp.wait_ge(weighed, 1)
                sp.dma_start(m.t_self.rearrange("(b t p) k -> t b (p k)", t=P, p=P),
                             self_weight[:].rearrange("t b p k -> t b (p k)")).then_inc(kept, 16)
                sp.wait_ge(kept, 16)
        turn_edges(nc, m, "softmax_back", [(e[:, k], by_block(m.alpha[:, k])) for k in range(2)])
        with ExitStack() as inner:
            sb, _, sem = place(nc, inner, "softmax_nodes")
            got = sem("got")
            rows = sb("rows", [P, NT, 2])
            block = inner.enter_context(nc.Block())

            @block.gpsimd
            def _(pool):
                for j in range(NT):
                    pool.indirect_dma_start(rows[:, j, :], None, m.t_self,
                                            bass.IndirectOffsetOnAxis(ap=m.last_edge[:, j:j + 1], axis=0)).then_inc(got, 16)

            @block.vector
            def _(dve):
                link = chain(dve, m)
                dve.wait_ge(got, 16 * NT)
                link(nc.vector.tensor_scalar(rows[:], rows[:], 0.5, None, ALU.subtract))
                link(nc.vector.tensor_tensor(rows[:], rows[:], m.has_edges[:].rearrange("p (j k) -> p j k", k=1).to_broadcast([P, NT, 2]), ALU.mult))
                link(nc.vector.tensor_scalar(m.self_weight[:], rows[:], 0.5, None, ALU.add))


def after_gat(nc, m, a):
    with ExitStack() as ctx:
        sb, pb, sem = place(nc, ctx, "n3")
        wrel, wroot, wf = sb("wrel", [P, 2, R4, C]), sb("wroot", [P, 2, C]), sb("wf", [P, 2, C])
        bias, bias_root = sb("bias", [1, H]), sb("bias_root", [P, 1])
        load_weights(nc, m, "n3_load", [
            *[(wrel[:, k], a["L1_gnn_rgcn_Wrel"].rearrange("r (b k) n -> b k r n", k=P)[k]) for k in range(2)],
            (wroot[:], by_half(a["L1_gnn_rgcn_Wroot"])), (wf[:], by_half(a["L1_gnn_fusion_W"][H:2 * H, :])),
            (bias[:], row_of(a["L1_gnn_gat_b"])), (bias_root[:], a["L1_gnn_rgcn_b"].rearrange("(n a) -> n a", a=1))])
        sums = sb("sums", [P, 2, GN, P])
        h, f = sb("h", [P, GN, 2 * H]), sb("f", [P, GN, C])
        y = sb("y", [P, GN, H])
        y_t = sb("y_t", [P, 2, GN, P])
        ps_t, ps = pb("ps_t", [P, 4, 512]), pb("ps", [P, 4, 512])
        loaded, staged, made, partly, summed, relued, turned, kept, f_made, f_taken, root_made, root_taken, x_made, x_taken, stored = sem(
            "loaded", "staged", "made", "partly", "summed", "relued", "turned", "kept", "f_made", "f_taken", "root_made", "root_taken",
            "x_made", "x_taken", "stored")
        block = ctx.enter_context(nc.Block())
        tile = lambda k, j: ps_t[:].rearrange("p b (s n) -> p (b s) n", n=P)[:, k * 8 + j, :]
        halves = ps_t[:].rearrange("p (k b) (s n) -> p k (b s) n", k=2, n=P)
        quarter = ps_t[:].rearrange("p b (s n) -> p (b s) n", n=P)
        root = ps_t[:, 2:4, 0:GW // 2]
        wide = ps[:].rearrange("p b (s n) -> p (b s) n", n=H)

        @block.sync
        def _(sp):
            with sp.Fori(0, NG, 1) as g:
                sp.wait_ge(stored, 32 * g)
                sp.dma_start(h[:], node_rows(m.t_h, g, 2 * H)).then_inc(loaded, 16)
                sp.dma_start(f[:], node_rows(m.t_f, g, C)).then_inc(loaded, 16)
                sp.wait_ge(f_taken, g + 1)
                sp.dma_start(node_rows(m.t_f, g, C), f[:]).then_inc(stored, 16)
                sp.wait_ge(x_taken, (g + 1) * GN)
                sp.dma_start(node_rows(m.t_rel4, g, R4 * C), h[:]).then_inc(stored, 16)
            sp.wait_ge(stored, 32 * NG)

        @block.scalar
        def _(act):
            with act.Fori(0, NG, 1) as g:
                act.wait_ge(made, g)
                nc.scalar.copy(sums[:].rearrange("p k j n -> p k (j n)"), m.acc[:, 0:2, group_cols(g)]).then_inc(staged, 1)
                act.wait_ge(summed, (g + 1) * GN)
                nc.scalar.activation(y[:], y[:], ACT.Relu).then_inc(relued, 1)
                act.wait_ge(turned, g + 1)
                act.wait_ge(x_made, g * GN)
                nc.scalar.copy(y_t[:], halves[:, :, 0:GN, :]).then_inc(kept, 1)

        @block.vector
        def _(dve):
            with dve.Fori(0, NG, 1) as g:
                dve.wait_ge(loaded, 32 * (g + 1))
                dve.wait_ge(made, g + 1)
                dve.wait_ge(turned, g)
                for j in range(GN):
                    nc.vector.scalar_tensor_tensor(y[:, j, :], h[:, j, 0:H], m.self_weight[:, bass.ds(g * GN + j, 1), 0], wide[:, j, :],
                                                   ALU.mult, ALU.add).then_inc(partly, 1)
                dve.wait_ge(partly, (g + 1) * GN)
                for j in range(GN):
                    nc.vector.scalar_tensor_tensor(y[:, j, :], h[:, j, H:2 * H], m.self_weight[:, bass.ds(g * GN + j, 1), 1], y[:, j, :],
                                                   ALU.mult, ALU.add).then_inc(summed, 1)
                dve.wait_ge(f_made, g + 1)
                nc.vector.tensor_tensor(f[:], f[:], quarter[:, 0:GN, :], ALU.add).then_inc(f_taken, 1)
                dve.wait_ge(root_made, g + 1)
                nc.vector.tensor_scalar(m.acc[:, 0, group_cols(g)].rearrange("p (b n) -> p b n", b=2), root, bias_root[:], None,
                                        ALU.add).then_inc(root_taken, 1)
                dve.wait_ge(summed, (g + 1) * GN)
                for j in range(GN):
                    dve.wait_ge(x_made, g * GN + j + 1)
                    nc.vector.tensor_copy(h[:, j, :], ps[:, j % 4, :]).then_inc(x_taken, 1)

        @block.tensor
        def _(pe):
            with pe.Fori(0, NG, 1) as g:
                pe.wait_ge(staged, g + 1)
                pe.wait_ge(x_taken, g * GN)
                for j in range(GN):
                    nc.tensor.matmul(wide[:, j, :], m.ones[0:1, :], bias[:], start=True, stop=False, skip_group_check=True)
                    for k in range(2):
                        last = nc.tensor.matmul(wide[:, j, k * P:(k + 1) * P], sums[:, k, j, :], m.ident[:], start=False, stop=True,
                                                skip_group_check=True)
                last.then_inc(made, 1)
                pe.wait_ge(relued, g + 1)
                pe.wait_ge(root_taken, g)
                for j in range(GN):
                    for k in range(2):
                        last = nc.tensor.transpose(tile(k, j), y[:, j, k * P:(k + 1) * P], m.ident[:])
                last.then_inc(turned, 1)
                pe.wait_ge(kept, g + 1)
                for j in range(GN):
                    for k in range(2):
                        last = nc.tensor.matmul(quarter[:, j, :], y_t[:, k, j, :], wf[:, k, :], start=(k == 0), stop=(k == 1))
                last.then_inc(f_made, 1)
                for b in range(2):
                    for k in range(2):
                        nodes = y_t[:, k].rearrange("p j n -> p (j n)")[:, b * (GW // 2):(b + 1) * (GW // 2)]
                        last = nc.tensor.matmul(root[:, b, :], wroot[:, k, :], nodes, start=(k == 0), stop=(k == 1))
                last.then_inc(root_made, 1)
                for j in range(GN):
                    if j >= 4:
                        pe.wait_ge(x_taken, g * GN + j - 3)
                    for k in range(2):
                        last = nc.tensor.matmul(ps[:, j % 4, :], y_t[:, k, j, :], wrel[:, k].rearrange("p r n -> p (r n)"), start=(k == 0), stop=(k == 1))
                    last.then_inc(x_made, 1)


def after_rgcn(nc, m, a):
    with ExitStack() as ctx:
        sb, pb, sem = place(nc, ctx, "n4")
        wf, w1 = sb("wf", [P, C]), sb("w1", [P, 2, C])
        bias = sb("bias", [1, C])
        load_weights(nc, m, "n4_load", [(wf[:], a["L1_gnn_fusion_W"][2 * H:2 * H + C, :]), (w1[:], by_half(a["L2_gnn_W1"][0:2 * C, :])),
                                        (bias[:], row_of(a["L2_gnn_b1"]))])
        rgcn, f = sb("rgcn", [P, GN, P]), sb("f", [P, GN, C])
        out, square = sb("out", [P, GN, C]), sb("square", [P, GN, C])
        length = sb("length", [P, 3, GN])
        x, x_t = sb("x", [P, GN, C]), sb("x_t", [P, GN, P])
        pq = sb("pq", [P, GN, 2 * C])
        ps_f, ps_t, ps = pb("ps_f", [P, 8, C]), pb("ps_t", [P, 8, P]), pb("ps", [P, 8, 2 * C])
        b = NormBuffers(sb, sem)
        loaded, staged, made, fused, squared, length_ready, length_root, steps, joined, turned, kept, pq_made, pq_taken, stored = sem(
            "loaded", "staged", "made", "fused", "squared", "length_ready", "length_root", "steps", "joined", "turned", "kept", "pq_made",
            "pq_taken", "stored")
        x_kept = sem("x_kept")
        block = ctx.enter_context(nc.Block())

        @block.sync
        def _(sp):
            with sp.Fori(0, NG, 1) as g:
                sp.wait_ge(fused, g)
                sp.dma_start(f[:], node_rows(m.t_f, g, C)).then_inc(loaded, 16)
                sp.wait_ge(pq_taken, g + 1)
                sp.dma_start(node_rows(m.t_p, g, C), pq[:, :, 0:C]).then_inc(stored, 16)
                sp.dma_start(node_rows(m.t_q, g, C), pq[:, :, C:2 * C]).then_inc(stored, 16)
            sp.wait_ge(stored, 32 * NG)

        @block.scalar
        def _(act):
            with act.Fori(0, NG, 1) as g:
                b.g = g
                act.wait_ge(made, g)
                nc.scalar.copy(rgcn[:].rearrange("p j n -> p (j n)"), m.acc[:, 0, group_cols(g)]).then_inc(staged, 1)
                act.wait_ge(length_ready, g + 1)
                nc.scalar.activation(length[:, 1, :], length[:, 0, :], ACT.Sqrt).then_inc(length_root, 1)
                layer_norm_root(nc, act, m, b)
                act.wait_ge(turned, g + 1)
                nc.scalar.copy(x_t[:], ps_t[:, 0:GN, :]).then_inc(kept, 1)
                nc.scalar.copy(m.x[:, group_tiles(g), :], x[:]).then_inc(x_kept, 1)
                act.wait_ge(pq_made, g + 1)
                act.wait_ge(stored, 32 * g)
                nc.scalar.copy(pq[:], ps[:, 0:GN, :]).then_inc(pq_taken, 1)

        @block.vector
        def _(dve):
            with dve.Fori(0, NG, 1) as g:
                b.g = g
                link = LoopChain(dve, steps, g, 3 + 2)
                dve.wait_ge(loaded, 16 * (g + 1))
                dve.wait_ge(made, g + 1)
                nc.vector.tensor_tensor(out[:], ps_f[:, 0:GN, :], f[:], ALU.add).then_inc(fused, 1)
                dve.wait_ge(fused, g + 1)
                link(nc.vector.tensor_tensor(square[:], out[:], out[:], ALU.mult))
                nc.vector.tensor_reduce(length[:, 0, :], square[:], AX.X, ALU.add).then_inc(length_ready, 1)
                dve.wait_ge(length_root, g + 1)
                link(nc.vector.tensor_scalar(length[:, 1, :], length[:, 1, :], 1e-12, None, ALU.max))
                link(nc.vector.reciprocal(length[:, 2, :], length[:, 1, :]))
                for j in range(GN):
                    nc.vector.scalar_tensor_tensor(out[:, j, :], out[:, j, :], length[:, 2, j:j + 1], m.x[:, bass.ds(g * GN + j, 1), :],
                                                   ALU.mult, ALU.add).then_inc(joined, 1)
                dve.wait_ge(joined, (g + 1) * GN)
                dve.wait_ge(x_kept, g)
                layer_norm(nc, dve, link, b, out, x)
                link.end()

        @block.tensor
        def _(pe):
            with pe.Fori(0, NG, 1) as g:
                pe.wait_ge(staged, g + 1)
                pe.wait_ge(fused, g)
                for j in range(GN):
                    last = nc.tensor.matmul(ps_f[:, j, :], rgcn[:, j, :], wf[:], start=True, stop=True)
                last.then_inc(made, 1)
                pe.wait_ge(b.norm_ready, (g + 1) * GN)
                for j in range(GN):
                    last = nc.tensor.transpose(ps_t[:, j, :], x[:, j, :], m.ident[:])
                last.then_inc(turned, 1)
                pe.wait_ge(kept, g + 1)
                pe.wait_ge(pq_taken, g)
                for j in range(GN):
                    nc.tensor.matmul(ps[:, j, :], x_t[:, j, :], w1[:].rearrange("p b n -> p (b n)"), start=True, stop=False, skip_group_check=True)
                    last = nc.tensor.matmul(ps[:, j, 0:C], m.ones[0:1, :], bias[:], start=False, stop=True, skip_group_check=True)
                last.then_inc(pq_made, 1)


def edge_hidden(nc, m, a):
    with ExitStack() as ctx:
        sb, pb, sem = place(nc, ctx, "eh")
        w1c = sb("w1c", [2, C])
        load_weights(nc, m, "eh_load", [(w1c[:], a["L2_gnn_W1"][2 * C:2 * C + 2, :])])
        window = sb("window", [P, U, C])
        message = sb("message", [P, U, C])
        stage = [sb(f"stage{h}", [P, HU], I32) for h in range(2)]
        rel_keys, src_keys = sb("rel_keys", [1, U * P], BF16), sb("src_keys", [2, U * P], BF16)
        attr = sb("attr", [2, U * P])
        distance, hot_t = sb("distance", [P, QUADS, QU * P]), sb("hot_t", [P, QUADS, QU * P])
        both = sb("both", [P, U, 2, C])
        hidden, square = both[:, :, 0, :], both[:, :, 1, :]
        junk, seen = sb("junk", [P, 2, QU, P]), sb("seen", [P, 2, QU])
        valid = sb("valid", [P, TP])
        ps = pb("ps", [P, U, C])
        ps_rel = pb("ps_rel", [P, QU * P])
        ps_src = [pb(f"ps_src{k}", [P, QU, P]) for k in range(2)]
        ps_sum = pb("ps_sum", [1, 2 * C])
        gathered, made, spread, rel_ready, added, squared, summed, counted = (
            [sem(f"{n}{q}") for q in range(QUADS)] for n in ("gathered", "made", "spread", "rel_ready", "added", "squared", "summed", "counted"))
        keys_in, stored, staged = ([sem(f"{n}{h}") for h in range(2)] for n in ("keys_in", "stored", "staged"))
        window_in = [sem(f"window_in{q}") for q in range(QUADS)]
        carried, distance_ready, counts, zeroed, cleared = sem("carried", "distance_ready", "counts", "zeroed", "cleared")
        masked = [sem(f"masked{q}") for q in range(QUADS)]
        mask = sb("mask", [P, U])
        block = ctx.enter_context(nc.Block())
        quad = lambda q: slice(q * QU, (q + 1) * QU)
        edges_of = lambda q: slice(q * QU * P, (q + 1) * QU * P)

        @block.sync
        def _(sp):
            def load(it, h):
                edges, slot = bass.ds((it * U + h * HU) * P, HU * P), slice(h * HU * P, (h + 1) * HU * P)
                sp.dma_start(rel_keys[:, slot], m.t_keys[REL:REL + 1, edges]).then_inc(keys_in[h], 16)
                sp.dma_start(src_keys[:, slot], m.t_keys[LOW:HIGH + 1, edges]).then_inc(keys_in[h], 16)
                sp.dma_start(attr[:, slot], m.t_ea[:, edges]).then_inc(keys_in[h], 16)
                window_load(nc, m, sp, window, m.t_q, C, it, h, window_in)

            def store(it, h):
                for q in (2 * h, 2 * h + 1):
                    sp.wait_ge(added[q], it + 1)
                sp.dma_start(m.t_hidden[bass.ds((it * U + h * HU) * P, HU * P), :].rearrange("(t p) f -> p t f", p=P),
                             hidden[:, h * HU:(h + 1) * HU, :]).then_inc(stored[h], 16)

            for h in range(2):
                load(0, h)
            with sp.Fori(0, ITERS - 1, 1) as it:
                for h in range(2):
                    for q in (2 * h, 2 * h + 1):
                        sp.wait_ge(made[q], it + 1)
                    load(it + 1, h)
                    store(it, h)
            for h in range(2):
                store(ITERS - 1, h)
            for h in range(2):
                sp.wait_ge(stored[h], 16 * ITERS)

        @block.gpsimd
        def _(pool):
            with pool.Fori(0, ITERS, 1) as it:
                for u in range(U):
                    h, k = divmod(u, HU)
                    if k == 0:
                        pool.wait_ge(carried, it * 2 + h)
                        pool.wait_ge(staged[h], it + 1)
                        nc.gpsimd.tensor_tensor(m.carrier[:], m.ones_i[:], m.ones_i[:], ALU.add).then_inc(carried, 1)
                    pool.indirect_dma_start(message[:, u, :], None, m.t_p,
                                            bass.IndirectOffsetOnAxis(ap=stage[h][:, k:k + 1], axis=0)).then_inc(gathered[u // QU], 16)

        @block.scalar
        def _(act):
            def stage_indices(it, h):
                nc.scalar.copy(stage[h][:], m.src[:, bass.ds(it * U + h * HU, HU)]).then_inc(staged[h], 1)

            def one_hot(it, q):
                act.wait_ge(spread[q], it + 1)
                turned_one_hot(nc, m, act, ps_rel[:], distance[:, q], hot_t[:, q], distance_ready, it * QUADS + q + 1, rel_ready[q])

            for h in range(2):
                stage_indices(0, h)
            for q in range(QUADS):
                one_hot(0, q)
            with act.Fori(0, ITERS - 1, 1) as it:
                for q in range(QUADS):
                    act.wait_ge(added[q], it + 1)
                    if q % 2 == 1:
                        stage_indices(it + 1, q // 2)
                    act.wait_ge(summed[q], it)
                    nc.scalar.copy(mask[:, quad(q)], valid[:, bass.ds(it * U + q * QU, QU)]).then_inc(masked[q], 1)
                    nc.scalar.activation(square[:, quad(q), :], hidden[:, quad(q), :], ACT.Square).then_inc(squared[q], 1)
                    act.wait_ge(made[q], it + 1)
                    one_hot(it + 1, q)
            for q in range(QUADS):
                act.wait_ge(added[q], ITERS)
                act.wait_ge(summed[q], ITERS - 1)
                nc.scalar.copy(mask[:, quad(q)], valid[:, (ITERS - 1) * U + q * QU:(ITERS - 1) * U + (q + 1) * QU]).then_inc(masked[q], 1)
                nc.scalar.activation(square[:, quad(q), :], hidden[:, quad(q), :], ACT.Square).then_inc(squared[q], 1)

        @block.vector
        def _(dve):
            nc.vector.memset(both[:, 0], 0.0).then_inc(zeroed, 1)
            nc.vector.tensor_scalar(valid[:], m.rel[:], 0.0, None, ALU.is_ge).then_inc(zeroed, 1)

            def count_seen(it, q):
                dve.wait_ge(spread[q], it + 1)
                for k in range(QU):
                    t = it * U + q * QU + k
                    nc.vector.scalar_tensor_tensor(junk[:, q % 2, k, :], ps_src[q % 2][:, k, :], m.src_key[:, bass.ds(t, 1)], m.before[:],
                                                   ALU.is_equal, ALU.mult, accum_out=seen[:, q % 2, k:k + 1]).then_inc(counts, 1)
                dve.wait_ge(counts, (it * QUADS + q + 1) * QU)
                nc.vector.tensor_copy(m.seen[:, bass.ds(it * U + q * QU, QU)], seen[:, q % 2, :]).then_inc(counted[q], 1)

            def add(it, q):
                dve.wait_ge(stored[q // 2], 16 * it)
                dve.wait_ge(summed[q], it)
                dve.wait_ge(cleared, 1)
                dve.wait_ge(gathered[q], 16 * QU * (it + 1))
                dve.wait_ge(made[q], it + 1)
                nc.vector.tensor_tensor(hidden[:, quad(q), :], ps[:, quad(q), :], message[:, quad(q), :], ALU.add).then_inc(added[q], 1)

            for q in range(QUADS):
                if q >= 2:
                    dve.wait_ge(counted[q - 2], 1)
                count_seen(0, q)
            with dve.Fori(0, ITERS - 1, 1) as it:
                for q in range(QUADS):
                    add(it, q)
                    dve.wait_ge(*bank_before(counted, it + 1, q))
                    count_seen(it + 1, q)
            for q in range(QUADS):
                add(ITERS - 1, q)
            for q in range(QUADS):
                dve.wait_ge(summed[q], ITERS)
            nc.vector.tensor_copy(m.totals[:], ps_sum[:]).then_inc(zeroed, 1)

        @block.tensor
        def _(pe):
            def spread_keys(it, q, waits):
                pe.wait_ge(keys_in[q // 2], 48 * (it + 1))
                for sem_, count in waits:
                    pe.wait_ge(sem_, count)
                nc.tensor.matmul(ps_rel[:], m.spread_one[:], rel_keys[:, edges_of(q)], start=True, stop=True)
                nc.tensor.matmul(ps_src[q % 2][:].rearrange("p k e -> p (k e)"), m.spread_src[:], src_keys[:, edges_of(q)],
                                 start=True, stop=True).then_inc(spread[q], 1)

            def look_up(it, q):
                pe.wait_ge(rel_ready[q], it + 1)
                pe.wait_ge(window_in[q], 16 * QU * (it + 1))
                for k in range(QU):
                    u = q * QU + k
                    nc.tensor.matmul(ps[:, u, :], hot_t[:, q, k * P:(k + 1) * P], window[:, u, :], start=True, stop=False)
                    last = nc.tensor.matmul(ps[:, u, :], attr[:, u * P:(u + 1) * P], w1c[:], start=False, stop=True)
                last.then_inc(made[q], 1)

            def add_up(it, q):
                pe.wait_ge(squared[q], it + 1)
                pe.wait_ge(masked[q], it + 1)
                for k in range(QU):
                    u = q * QU + k
                    last = nc.tensor.matmul(ps_sum[:], mask[:, u:u + 1], both[:, u].rearrange("p c f -> p (c f)"), start=False, stop=True,
                                            skip_group_check=True)
                last.then_inc(summed[q], 1)

            pe.wait_ge(zeroed, 2)
            nc.tensor.matmul(ps_sum[:], m.ones[:, 0:1], both[:, 0].rearrange("p c f -> p (c f)"), start=True, stop=False,
                             skip_group_check=True).then_inc(cleared, 1)
            for q in range(QUADS):
                spread_keys(0, q, ([(rel_ready[q - 1], 1)] if q >= 1 else []) + ([(counted[q - 2], 1)] if q >= 2 else []))
                look_up(0, q)
            with pe.Fori(0, ITERS - 1, 1) as it:
                for q in range(QUADS):
                    before = (rel_ready[q - 1], it + 2) if q >= 1 else (rel_ready[QUADS - 1], it + 1)
                    spread_keys(it + 1, q, [before, bank_before(counted, it + 1, q)])
                    add_up(it, q)
                    pe.wait_ge(added[q], it + 1)
                    look_up(it + 1, q)
            for q in range(QUADS):
                add_up(ITERS - 1, q)


def batch_norm_rows(nc, m, a):
    with ExitStack() as ctx:
        sb, pb, sem = place(nc, ctx, "bn")
        gamma, beta = sb("gamma", [P, 1]), sb("beta", [P, 1])
        load_weights(nc, m, "bn_load", [(gamma[:], a["L2_gnn_gamma"].rearrange("(n a) -> n a", a=1)), (beta[:], a["L2_gnn_beta"].rearrange("(n a) -> n a", a=1))])
        v = sb("v", [P, 6])
        diag = sb("diag", [P, 2, C])
        first, target = sb("first", [P, TP]), sb("target", [P, TP])
        ps_v = pb("ps_v", [P, 2])
        columned = sem("columned")
        ps = pb("ps", [P, 2, C])
        var_ready, root_ready, diag_ready, spread = sem("var_ready", "root_ready", "diag_ready", "spread")
        block = ctx.enter_context(nc.Block())

        @block.vector
        def _(dve):
            link = chain(dve, m)
            ts, stt = nc.vector.tensor_scalar, nc.vector.scalar_tensor_tensor
            dve.wait_ge(columned, 2)
            link(ts(v[:, 0:2], ps_v[:], 1.0 / EDGES, None, ALU.mult))
            link(stt(v[:, 2:3], v[:, 0:1], v[:, 0:1], v[:, 1:2], ALU.mult, ALU.subtract))
            ts(v[:, 3:4], v[:, 2:3], -1.0, 0.0, ALU.mult, ALU.max).then_inc(var_ready, 1)
            dve.wait_ge(root_ready, 1)
            link(nc.vector.reciprocal(v[:, 5:6], v[:, 4:5]))
            link(nc.vector.tensor_tensor(v[:, 5:6], v[:, 5:6], gamma[:], ALU.mult))
            link(nc.vector.tensor_tensor(v[:, 4:5], v[:, 0:1], v[:, 5:6], ALU.mult))
            link(nc.vector.tensor_tensor(v[:, 4:5], beta[:], v[:, 4:5], ALU.subtract))
            ts(diag[:, 0], m.ident[:], v[:, 5:6], None, ALU.mult).then_inc(diag_ready, 1)
            ts(diag[:, 1], m.ident[:], v[:, 4:5], None, ALU.mult).then_inc(diag_ready, 1)
            link(ts(first[:], m.seen[:], 0.5, None, ALU.is_lt))
            link(ts(target[:], m.rel[:], 0.0, None, ALU.is_ge))
            link(nc.vector.tensor_tensor(first[:], first[:], target[:], ALU.mult))
            link(ts(m.column[:], m.column[:], float(ROWS), None, ALU.add))
            link(ts(target[:], m.src_key[:], m.column[:], None, ALU.subtract))
            link(nc.vector.tensor_tensor(target[:], target[:], first[:], ALU.mult))
            link(ts(target[:], target[:], m.column[:], None, ALU.add))
            link(nc.vector.tensor_copy(m.target[:], target[:]))
            dve.wait_ge(spread, 2)
            link(nc.vector.tensor_copy(m.norm_rows[:], ps[:]))

        @block.scalar
        def _(act):
            act.wait_ge(var_ready, 1)
            nc.scalar.activation(v[:, 4:5], v[:, 3:4], ACT.Sqrt, bias=m.epsilon[:], scale=1.0).then_inc(root_ready, 1)

        @block.tensor
        def _(pe):
            for k in range(2):
                nc.tensor.matmul(ps_v[:, k:k + 1], m.totals[:, k * C:(k + 1) * C], m.ones[0:1, 0:1], start=True, stop=True).then_inc(columned, 1)
            pe.wait_ge(diag_ready, 2)
            for k in range(2):
                nc.tensor.matmul(ps[:, k, :], m.ones[:], diag[:, k], start=True, stop=True).then_inc(spread, 1)


def scatter_by_source(nc, m, a):
    assert COPIES == 2 * QU
    with ExitStack() as ctx:
        sb, pb, sem = place(nc, ctx, "sc")
        rows = sb("rows", [P, 2, HU, C])
        message = sb("message", [P, 2, HU, SW])
        src_keys = sb("src_keys", [2, 2, HU * P], BF16)
        same = sb("same", [P, U, P])
        total = sb("total", [P, U, SW])
        stage = [sb(f"stage{q}", [P, QU], I32) for q in range(QUADS)]
        ps_src = [pb(f"ps_src{k}", [P, QU, P]) for k in range(2)]
        ps = [pb(f"ps{k}", [P, QU, 256]) for k in range(2)]
        rows_in, keys_in, scaled, shifted, relued = ([sem(f"{n}{h}") for h in range(2)] for n in ("rows_in", "keys_in", "scaled", "shifted", "relued"))
        spread, matched, summed, taken, staged = (
            [sem(f"{n}{q}") for q in range(QUADS)] for n in ("spread", "matched", "summed", "taken", "staged"))
        scattered = [sem(f"scattered{k}") for k in range(COPIES)]
        carried, counts_set = sem("carried", "counts_set")
        block = ctx.enter_context(nc.Block())

        @block.sync
        def _(sp):
            with sp.Fori(0, ITERS, 1) as it:
                for h in range(2):
                    edges = bass.ds((it * U + h * HU) * P, HU * P)
                    sp.wait_ge(spread[2 * h + 1], it)
                    sp.dma_start(src_keys[:, h], m.t_keys[LOW:HIGH + 1, edges]).then_inc(keys_in[h], 16)
                    sp.wait_ge(relued[h], it)
                    sp.dma_start(rows[:, h], m.t_hidden[edges, :].rearrange("(t p) f -> p t f", p=P)).then_inc(rows_in[h], 16)

        @block.vector
        def _(dve):
            nc.vector.memset(message[:], 1.0).then_inc(counts_set, 1)

            def normalise(it, h):
                wide = lambda k: m.norm_rows[:, k:k + 1, :].to_broadcast([P, HU, C])
                dve.wait_ge(rows_in[h], 16 * (it + 1))
                nc.vector.tensor_tensor(rows[:, h], rows[:, h], wide(0), ALU.mult).then_inc(scaled[h], 1)
                dve.wait_ge(scaled[h], it + 1)
                nc.vector.tensor_tensor(rows[:, h], rows[:, h], wide(1), ALU.add).then_inc(shifted[h], 1)

            def match(it, q):
                dve.wait_ge(spread[q], it + 1)
                dve.wait_ge(summed[q], it)
                for k in range(QU):
                    u = q * QU + k
                    nc.vector.tensor_scalar(same[:, u, :], ps_src[q % 2][:, k, :], m.src_key[:, bass.ds(it * U + u, 1)], None,
                                            ALU.is_equal).then_inc(matched[q], 1)

            def take(it, q):
                dve.wait_ge(staged[q], it + 1)
                dve.wait_ge(summed[q], it + 1)
                nc.vector.tensor_copy(total[:, q * QU:(q + 1) * QU, :], ps[q % 2][:, :, 0:SW]).then_inc(taken[q], 1)

            with dve.Fori(0, ITERS, 1) as it:
                for q in range(QUADS):
                    if q % 2 == 0:
                        normalise(it, q // 2)
                    match(it, q)
                    if q >= 1:
                        take(it, q - 1)
                take(it, QUADS - 1)

        @block.scalar
        def _(act):
            act.wait_ge(counts_set, 1)
            with act.Fori(0, ITERS, 1) as it:
                for q in range(QUADS):
                    h, even = divmod(q, 2)
                    if even == 0:
                        for r in (q, q + 1):
                            act.wait_ge(summed[r], it)
                        act.wait_ge(shifted[h], it + 1)
                        nc.scalar.activation(message[:, h, :, 0:C], rows[:, h], ACT.Relu).then_inc(relued[h], 1)
                    for k in range(QU):
                        act.wait_ge(scattered[(q % 2) * QU + k], 32 * it)
                    nc.scalar.copy(stage[q][:], m.target[:, bass.ds(it * U + q * QU, QU)]).then_inc(staged[q], 1)

        @block.tensor
        def _(pe):
            def add_up(it, q):
                pe.wait_ge(relued[q // 2], it + 1)
                pe.wait_ge(matched[q], QU * (it + 1))
                pe.wait_ge(*bank_before(taken, it, q))
                for k in range(QU):
                    u = q * QU + k
                    last = nc.tensor.matmul(ps[q % 2][:, k, 0:SW], same[:, u, :], message[:, u // HU, u % HU, :], start=True, stop=True)
                last.then_inc(summed[q], 1)

            with pe.Fori(0, ITERS, 1) as it:
                for q in range(QUADS):
                    h = q // 2
                    pe.wait_ge(keys_in[h], 16 * (it + 1))
                    earlier, count = bank_before(matched, it, q)
                    pe.wait_ge(earlier, QU * count)
                    nc.tensor.matmul(ps_src[q % 2][:].rearrange("p k e -> p (k e)"), m.spread_src[:],
                                     src_keys[:, h, (q % 2) * QU * P:(q % 2 + 1) * QU * P], start=True, stop=True).then_inc(spread[q], 1)
                    if q >= 1:
                        add_up(it, q - 1)
                add_up(it, QUADS - 1)

        @block.gpsimd
        def _(pool):
            with pool.Fori(0, ITERS, 1) as it:
                for q in range(QUADS):
                    pool.wait_ge(carried, it * QUADS + q)
                    pool.wait_ge(taken[q], it + 1)
                    for k in range(QU):
                        pool.wait_ge(scattered[(q % 2) * QU + k], 16 * (it * 2 + q // 2))
                    nc.gpsimd.tensor_tensor(m.carrier[:], m.ones_i[:], m.ones_i[:], ALU.add).then_inc(carried, 1)
                    for k in range(QU):
                        copy = (q % 2) * QU + k
                        pool.indirect_dma_start(m.scatter[copy], bass.IndirectOffsetOnAxis(ap=stage[q][:, k:k + 1], axis=0), total[:, q * QU + k, :],
                                                None, compute_op=ALU.add).then_inc(scattered[copy], 16)
            for c in range(COPIES):
                pool.wait_ge(scattered[c], 16 * 2 * ITERS)


def after_block2(nc, m, a):
    with ExitStack() as ctx:
        sb, pb, sem = place(nc, ctx, "n5")
        w2, w0, w8 = sb("w2", [P, C]), sb("w0", [P, C]), sb("w8", [P, R8, C])
        b2 = sb("b2", [P, C])
        load_weights(nc, m, "n5_load", [(w2[:], a["L2_gnn_W2"]), (w0[:], a["L3_gnn_W0"]), (w8[:], a["L3_gnn_W"].rearrange("r k n -> k r n")),
                                        (b2[:], row_of(a["L2_gnn_b2"]).to_broadcast([P, C]))])
        copies = sb("copies", [P, COPIES, GN, SW])
        sums_t = sb("sums_t", [P, GN, P])
        count = sb("count", [P, 2, GN])
        y = sb("y", [P, GN, C])
        x, x_t = sb("x", [P, GN, C]), sb("x_t", [P, GN, P])
        h = sb("h", [P, GN, R8, C])
        ps_t, ps, ps_h = pb("ps_t", [P, 8, P]), pb("ps", [P, 8, C]), pb("ps_h", [P, 4, 512])
        b = NormBuffers(sb, sem)
        loaded, steps, summed, turned, kept, made, joined, taken, turned2, kept2, root_made, root_taken, h_made, h_even, h_odd, stored, x_kept = sem(
            "loaded", "steps", "summed", "turned", "kept", "made", "joined", "taken", "turned2", "kept2", "root_made", "root_taken", "h_made",
            "h_even", "h_odd", "stored", "x_kept")
        tail_cleared = sem("tail_cleared")
        block = ctx.enter_context(nc.Block())
        root = ps[:].rearrange("p (b j) n -> p b (j n)", b=2)[:, :, 0:GW // 2]

        @block.sync
        def _(sp):
            with sp.Fori(0, NG, 1) as g:
                sp.wait_ge(joined, g * GN)
                for c in range(COPIES):
                    sp.dma_start(copies[:, c], node_rows(m.scatter[c], g, SW)).then_inc(loaded, 16)
                sp.wait_ge(h_even, (g + 1) * GN)
                sp.wait_ge(h_odd, (g + 1) * GN)
                sp.dma_start(node_rows(m.t_rel8, g, R8 * C), h[:].rearrange("p j r n -> p j (r n)")).then_inc(stored, 16)
            sp.wait_ge(stored, 16 * NG)

        @block.vector
        def _(dve):
            nc.vector.memset(m.acc[:, :, ROWS:ACCW], 0.0).then_inc(tail_cleared, 1)
            with dve.Fori(0, NG, 1) as g:
                b.g = g
                link = LoopChain(dve, steps, g, 2 + 2 + 1 + 2)
                dve.wait_ge(loaded, 16 * COPIES * (g + 1))
                span = COPIES
                while span > 2:
                    span //= 2
                    link(nc.vector.tensor_tensor(copies[:, 0:span], copies[:, 0:span], copies[:, span:2 * span], ALU.add))
                nc.vector.tensor_tensor(copies[:, 0], copies[:, 0], copies[:, 1], ALU.add).then_inc(summed, 1)
                dve.wait_ge(summed, g + 1)
                link(nc.vector.tensor_scalar(count[:, 0], copies[:, 0, :, C], 1.0, None, ALU.add))
                link(nc.vector.reciprocal(count[:, 1], count[:, 0]))
                dve.wait_ge(made, g + 1)
                for j in range(GN):
                    nc.vector.scalar_tensor_tensor(y[:, j, :], b2[:], copies[:, 0, j, C:C + 1], ps[:, j, :], ALU.mult, ALU.add).then_inc(joined, 1)
                dve.wait_ge(joined, (g + 1) * GN)
                for j in range(GN):
                    nc.vector.scalar_tensor_tensor(y[:, j, :], y[:, j, :], count[:, 1, j:j + 1], m.x[:, bass.ds(g * GN + j, 1), :],
                                                   ALU.mult, ALU.add).then_inc(taken, 1)
                dve.wait_ge(taken, (g + 1) * GN)
                link(nc.vector.tensor_tensor(y[:], y[:], m.x[:, group_tiles(g), :], ALU.add))
                dve.wait_ge(x_kept, g)
                dve.wait_ge(turned2, g)
                layer_norm(nc, dve, link, b, y, x)
                link.end()
                dve.wait_ge(stored, 16 * g)
                for j in range(GN):
                    dve.wait_ge(h_made, (g * GN + j + 1) * 2 - 1)
                    nc.vector.tensor_copy(h[:, j, 0:R8 // 2].rearrange("p r n -> p (r n)"), ps_h[:, (2 * j) % 4, :]).then_inc(h_even, 1)

        @block.scalar
        def _(act):
            with act.Fori(0, NG, 1) as g:
                b.g = g
                act.wait_ge(turned, g + 1)
                act.wait_ge(made, g)
                nc.scalar.copy(sums_t[:], ps_t[:, 0:GN, :]).then_inc(kept, 1)
                layer_norm_root(nc, act, m, b)
                act.wait_ge(b.norm_ready, (g + 1) * GN)
                nc.scalar.copy(m.x[:, group_tiles(g), :], x[:]).then_inc(x_kept, 1)
                act.wait_ge(turned2, g + 1)
                act.wait_ge(h_made, 2 * GN * g)
                nc.scalar.copy(x_t[:], ps_t[:, 0:GN, :]).then_inc(kept2, 1)
                act.wait_ge(root_made, g + 1)
                nc.scalar.copy(m.acc[:, 0, group_cols(g)].rearrange("p (b n) -> p b n", b=2), root).then_inc(root_taken, 1)
                act.wait_ge(stored, 16 * g)
                for j in range(GN):
                    act.wait_ge(h_made, (g * GN + j + 1) * 2)
                    nc.scalar.copy(h[:, j, R8 // 2:R8].rearrange("p r n -> p (r n)"), ps_h[:, (2 * j + 1) % 4, :]).then_inc(h_odd, 1)

        @block.tensor
        def _(pe):
            with pe.Fori(0, NG, 1) as g:
                pe.wait_ge(summed, g + 1)
                pe.wait_ge(kept2, g)
                for j in range(GN):
                    last = nc.tensor.transpose(ps_t[:, j, :], copies[:, 0, j, 0:C], m.ident[:])
                last.then_inc(turned, 1)
                pe.wait_ge(kept, g + 1)
                pe.wait_ge(root_taken, g)
                for j in range(GN):
                    last = nc.tensor.matmul(ps[:, j, :], sums_t[:, j, :], w2[:], start=True, stop=True)
                last.then_inc(made, 1)
                pe.wait_ge(b.norm_ready, (g + 1) * GN)
                for j in range(GN):
                    last = nc.tensor.transpose(ps_t[:, j, :], x[:, j, :], m.ident[:])
                last.then_inc(turned2, 1)
                pe.wait_ge(kept2, g + 1)
                for c in range(2):
                    nodes = x_t[:].rearrange("p j n -> p (j n)")[:, c * (GW // 2):(c + 1) * (GW // 2)]
                    last = nc.tensor.matmul(root[:, c, :], w0[:], nodes, start=True, stop=True)
                last.then_inc(root_made, 1)
                for j in range(GN):
                    if j >= 2:
                        pe.wait_ge(h_even, g * GN + j - 1)
                        pe.wait_ge(h_odd, g * GN + j - 1)
                    else:
                        pe.wait_ge(h_even, g * GN)
                        pe.wait_ge(h_odd, g * GN)
                    for c in range(2):
                        last = nc.tensor.matmul(ps_h[:, (2 * j + c) % 4, :], x_t[:, j, :], w8[:, c * 4:c * 4 + 4].rearrange("p r n -> p (r n)"),
                                                start=True, stop=True)
                        last.then_inc(h_made, 1)


def after_block3(nc, m, a):
    with ExitStack() as ctx:
        sb, pb, sem = place(nc, ctx, "n6")
        scaled = sb("scaled", [P, GN, P])
        y = sb("y", [P, GN, C])
        ps = pb("ps", [P, 8, C])
        b = NormBuffers(sb, sem)
        staged, made, taken, steps, stored = sem("staged", "made", "taken", "steps", "stored")
        block = ctx.enter_context(nc.Block())

        @block.tensor
        def _(pe):
            with pe.Fori(0, NG, 1) as g:
                pe.wait_ge(staged, g + 1)
                pe.wait_ge(taken, g)
                for j in range(GN):
                    last = nc.tensor.transpose(ps[:, j, :], scaled[:, j, :], m.ident[:])
                last.then_inc(made, 1)

        @block.scalar
        def _(act):
            with act.Fori(0, NG, 1) as g:
                b.g = g
                layer_norm_root(nc, act, m, b)

        @block.vector
        def _(dve):
            with dve.Fori(0, NG, 1) as g:
                b.g = g
                link = LoopChain(dve, steps, g, 2)
                dve.wait_ge(made, g)
                nc.vector.tensor_tensor(scaled[:].rearrange("p j n -> p (j n)"), m.acc[:, 0, group_cols(g)],
                                        m.inv_degree[:, group_cols(g)], ALU.mult).then_inc(staged, 1)
                dve.wait_ge(made, g + 1)
                dve.wait_ge(b.norm_ready, g * GN)
                nc.vector.tensor_tensor(y[:], ps[:, 0:GN, :], m.x[:, group_tiles(g), :], ALU.add).then_inc(taken, 1)
                dve.wait_ge(taken, g + 1)
                layer_norm(nc, dve, link, b, y, m.x[:, group_tiles(g), :])
                link.end()

        @block.sync
        def _(sp):
            sp.wait_ge(b.norm_ready, NG * GN)
            sp.dma_start(a["out"][0:(NT - 1) * P, :].rearrange("(j p) f -> p j f", p=P), m.x[:, 0:NT - 1, :]).then_inc(stored, 16)
            sp.dma_start(a["out"][(NT - 1) * P:NODES, :], m.x[0:TAIL, NT - 1, :]).then_inc(stored, 16)
            sp.wait_ge(stored, 32)


class Memory:
    pass


class EdgeSemaphores:
    def __init__(self, sem):
        self.passes, self.hots = 0, 0
        self.gathered = [sem(f"gathered{u}") for u in range(U)]
        self.half_used = [sem(f"half_used{h}") for h in range(2)]
        self.staged, self.carried, self.hot_ready, self.window_ready, self.window_used = sem(
            "staged", "carried", "hot_ready", "window_ready", "window_used")


def gnn_blocks(nc, a):
    with ExitStack() as ctx:
        sb, _, sem = place(nc, ctx, "all")
        m = Memory()
        m.steps, m.step = 0, sem("step")
        m.edge = EdgeSemaphores(sem)
        table = lambda name, *shape: nc.dram_tensor(name, shape, F32, kind="Internal").ap()
        m.t_x, m.t_f, m.t_p, m.t_q = table("t_x", ROWS, C), table("t_f", ROWS, C), table("t_p", ROWS, C), table("t_q", ACCW, C)
        m.t_s1, m.t_h, m.t_al = table("t_s1", ROWS, H), table("t_h", ROWS, 2 * H), table("t_al", ROWS, 4)
        m.t_rel4, m.t_rel8 = table("t_rel4", ROWS, R4 * C), table("t_rel8", ROWS, R8 * C)
        m.t_hidden, m.t_self = table("t_hidden", T * P, C), table("t_self", TP * P, 2)
        m.t_ea, m.t_last = table("t_ea", 2, TP * P), table("t_last", TP * P, 4)
        m.t_keys = nc.dram_tensor("t_keys", (3, TP * P), BF16, kind="Internal").ap()
        m.scatter = [table(f"scatter{k}", SROWS, SW) for k in range(COPIES)]
        m.iota, m.ident, m.before, m.ones = (sb(n, [P, P]) for n in ("iota", "ident", "before", "ones"))
        m.column, m.minus_column, m.epsilon = (sb(n, [P, 1]) for n in ("column", "minus_column", "epsilon"))
        m.spread_one, m.spread_src = sb("spread_one", [1, P], BF16), sb("spread_src", [2, P], BF16)
        m.ones_i, m.carrier = sb("ones_i", [1, 1], I32), sb("carrier", [1, 1], I32)
        m.x = sb("x", [P, NT, C])
        m.src, m.src4, m.src8 = (sb(n, [P, TP], I32) for n in ("src", "src4", "src8"))
        m.rel, m.w_rgcn, m.w_edge, m.src_key, m.src_high = (sb(n, [P, TP]) for n in ("rel", "w_rgcn", "w_edge", "src_key", "src_high"))
        m.base = sb("base", [1, TP], I32)
        m.last_edge_f, m.has_edges = sb("last_edge_f", [P, NT]), sb("has_edges", [P, NT])
        m.last_edge = sb("last_edge", [P, NT], I32)
        m.self_weight = sb("self_weight", [P, NT, 2])
        m.totals, m.norm_rows = sb("totals", [1, 2 * C]), sb("norm_rows", [P, 2, C])

        with nc.cleanup_on_exit():
            constants(nc, m, a)
            edge_setup(nc, m, a)
        m.inv_degree = sb("inv_degree", [P, ROWS])
        with nc.cleanup_on_exit(), ExitStack() as scope:
            scoped, _, _ = place(nc, scope, "first")
            m.acc = scoped("acc", [P, 2, ACCW])
            aggregate(nc, m, "block0", a["x"], m.src, [], 1, degree=True)
            degrees(nc, m)
            after_block0(nc, m, a)
            aggregate(nc, m, "sage1", m.t_x, m.src, [], 1)
            after_sage1(nc, m, a)
            aggregate(nc, m, "sage2", m.t_s1, m.src, [], 2)
            after_sage2(nc, m, a)
        m.alpha = sb("alpha", [P, 2, TP])
        with nc.cleanup_on_exit(), ExitStack() as scope:
            scoped, _, _ = place(nc, scope, "attention")
            m.e = scoped("e", [P, 2, TP])
            attention_terms(nc, m)
            attention_softmax(nc, m, a)
        with nc.cleanup_on_exit(), ExitStack() as scope:
            scoped, _, _ = place(nc, scope, "second")
            m.acc = scoped("acc", [P, 2, ACCW])
            aggregate(nc, m, "gat", m.t_h, m.src, [m.alpha[:, 0], m.alpha[:, 1]], 2)
            after_gat(nc, m, a)
            aggregate(nc, m, "rgcn", m.t_rel4.rearrange("n (r f) -> (n r) f", f=C), m.src4, [m.w_rgcn], 1, clear=False)
            after_rgcn(nc, m, a)
        m.seen, m.target = m.alpha[:, 0], m.alpha[:, 1].bitcast(I32)
        with nc.cleanup_on_exit():
            edge_hidden(nc, m, a)
            batch_norm_rows(nc, m, a)
            scatter_by_source(nc, m, a)
        with ExitStack() as scope:
            scoped, _, _ = place(nc, scope, "third")
            m.acc = scoped("acc", [P, 1, ACCW])
            after_block2(nc, m, a)
            aggregate(nc, m, "block3", m.t_rel8.rearrange("n (r f) -> (n r) f", f=C), m.src8, [m.w_edge], 1, clear=False)
            after_block3(nc, m, a)


NAMES = ["x", "src", "dst", "edge_attr_2", "edge_type_4", "edge_type_8", "edge_weight", "L0_gnn_W_neigh", "L0_gnn_b_neigh",
         "L1_gnn_sage1_Wl", "L1_gnn_sage1_Wr", "L1_gnn_sage1_b", "L1_gnn_sage2_Wl", "L1_gnn_sage2_Wr", "L1_gnn_sage2_b", "L1_gnn_gat_W",
         "L1_gnn_gat_att_src", "L1_gnn_gat_att_dst", "L1_gnn_gat_b", "L1_gnn_rgcn_Wrel", "L1_gnn_rgcn_Wroot", "L1_gnn_rgcn_b",
         "L1_gnn_fusion_W", "L1_gnn_fusion_b", "L2_gnn_W1", "L2_gnn_b1", "L2_gnn_gamma", "L2_gnn_beta", "L2_gnn_W2", "L2_gnn_b2",
         "L3_gnn_W", "L3_gnn_W0"]


def kernel(**inputs):
    import concourse.bacc as bacc
    from concourse.bass_utils import run_bass_kernel_spmd

    nc = bacc.Bacc("TRN2", target_bir_lowering=False, num_devices=1)
    arrays, a = {}, {}
    for name in NAMES:
        arrays[f"in_{name}"] = np.ascontiguousarray(inputs[name])
        a[name] = nc.dram_tensor(f"in_{name}", arrays[f"in_{name}"].shape, mybir.dt.from_np(arrays[f"in_{name}"].dtype), kind="ExternalInput").ap()
    a["out"] = nc.dram_tensor("out", (NODES, C), F32, kind="ExternalOutput").ap()
    gnn_blocks(nc, a)
    return run_bass_kernel_spmd(nc, [arrays], core_ids=[0]).results[0]["out"]
```

```python
from contextlib import ExitStack

import numpy as np

import concourse.bass as bass
from concourse import mybir

F32 = mybir.dt.float32
I32 = mybir.dt.int32
BF16 = mybir.dt.bfloat16
ALU = mybir.AluOpType
ACT = mybir.ActivationFunctionType
AX = mybir.AxisListType
DVE = mybir.EngineType.DVE
SP = mybir.EngineType.SP

P = 128
NODES, EDGES = 6250, 106250
C = 128
H = 256
R4, R8 = 4, 8
NT = -(-NODES // P)
GN = 7
NG = NT // GN
GW = GN * P
ROWS = NT * P
TAIL = NODES - (NT - 1) * P
U = 16
HU = U // 2
QU = 4
QUADS = U // QU
ITERS = -(-EDGES // (P * U))
T = ITERS * U
EB = -(-T // P)
TP = EB * P
FULL = EDGES // P
REST = EDGES - FULL * P
ACCW = 6400
COPIES = 8
SW = C + 1
SROWS = ROWS + P
BIG = 1e30
EPS = 1e-5
ROUNDER = 1.5 * 2.0 ** 23
REL, LOW, HIGH = 0, 1, 2
assert NT == NG * GN and EB * P >= T + HU and NODES + P <= ACCW


def chain(engine, m):
    def link(instruction):
        m.steps += 1
        instruction.then_inc(m.step, 1)
        engine.wait_ge(m.step, m.steps)
    return link


class LoopChain:
    def __init__(self, engine, sem, g, per):
        self.engine, self.sem, self.g, self.per, self.n = engine, sem, g, per, 0

    def __call__(self, instruction):
        self.n += 1
        assert self.n <= self.per
        instruction.then_inc(self.sem, 1)
        self.engine.wait_ge(self.sem, self.g * self.per + self.n)

    def end(self):
        assert self.n == self.per, (self.n, self.per)


def place(nc, ctx, phase):
    def sb(name, shape, dt=F32):
        return ctx.enter_context(nc.sbuf_tensor(f"{phase}_{name}", shape, dt))

    def pb(name, shape):
        return ctx.enter_context(nc.psum_tensor(f"{phase}_{name}", shape, F32))

    def sem(*names):
        made = [nc.alloc_semaphore(f"{phase}_{n}") for n in names]
        return made if len(made) > 1 else made[0]
    return sb, pb, sem


def node_rows(table, g, width):
    return table[bass.ds(g * GW, GW), 0:width].rearrange("(j p) f -> p j f", p=P)


def edge_blocks(array, b0, b1):
    return array[b0 * P * P:b1 * P * P].rearrange("(b t p) -> t b p", t=P, p=P)


def load_edge_rows(engine, tile, array, sem):
    last = FULL - (EB - 1) * P
    engine.dma_start(tile[:, 0:EB - 1, :], edge_blocks(array, 0, EB - 1)).then_inc(sem, 16)
    engine.dma_start(tile[0:last, EB - 1, :], array[(EB - 1) * P * P:FULL * P].rearrange("(t p) -> t p", p=P)).then_inc(sem, 16)
    engine.dma_start(tile[last:last + 1, EB - 1, 0:REST], array[FULL * P:EDGES].rearrange("(t p) -> t p", t=1)).then_inc(sem, 16)


def constants(nc, m, a):
    with ExitStack() as ctx:
        sb, _, sem = place(nc, ctx, "constants")
        ioted, loaded, zeros_ready = sem("ioted", "loaded", "zeros_ready")
        iota_i, col_i = sb("iota_i", [P, P], I32), sb("col_i", [P, 1], I32)
        block = ctx.enter_context(nc.Block())

        @block.gpsimd
        def _(pool):
            nc.gpsimd.iota(iota_i[:], pattern=[[1, P]], base=0, channel_multiplier=0).then_inc(ioted, 1)
            nc.gpsimd.iota(col_i[:], pattern=[[1, 1]], base=0, channel_multiplier=1).then_inc(ioted, 1)

        @block.vector
        def _(dve):
            nc.vector.memset(m.x[:], 0.0).then_inc(zeros_ready, 1)
            dve.wait_ge(ioted, 2)
            link = chain(dve, m)
            link(nc.vector.tensor_copy(m.iota[:], iota_i[:]))
            link(nc.vector.tensor_copy(m.column[:], col_i[:]))
            link(nc.vector.tensor_scalar(m.ident[:], m.iota[:], m.column[:], None, ALU.is_equal))
            link(nc.vector.tensor_scalar(m.before[:], m.iota[:], m.column[:], None, ALU.is_lt))
            link(nc.vector.memset(m.ones[:], 1.0))
            link(nc.vector.memset(m.ones_i[:], 1))
            link(nc.vector.memset(m.epsilon[:], EPS))
            link(nc.vector.tensor_scalar(m.minus_column[:], m.column[:], -1.0, None, ALU.mult))
            link(nc.vector.memset(m.spread_one[:], 1.0))
            link(nc.vector.tensor_scalar(m.spread_src[:], m.column[0:2, 0:1].to_broadcast([2, P]), float(P - 1), 1.0, ALU.mult, ALU.add))

        @block.sync
        def _(sp):
            sp.wait_ge(zeros_ready, 1)
            sp.dma_start(m.x[:, 0:NT - 1, :], a["x"][0:(NT - 1) * P, :].rearrange("(j p) f -> p j f", p=P)).then_inc(loaded, 16)
            sp.dma_start(m.x[0:TAIL, NT - 1, :], a["x"][(NT - 1) * P:NODES, :]).then_inc(loaded, 16)
            sp.wait_ge(loaded, 32)


class Segments:
    def __init__(self, nc, ctx, phase, q):
        sb, _, _ = place(nc, ctx, phase)
        self.dst_i, self.dst = sb("dst_i", [P, EB, P], I32), sb("dst_rows", [P, EB, P])
        self.same_prev, self.same_next = sb("same_prev", [P, EB, P]), sb("same_next", [P, EB, P])
        self.in_first, self.in_last = sb("in_first", [P, EB, P]), sb("in_last", [P, EB, P])
        self.ends = sb("ends", [P, EB, 2, q])
        self.first, self.last = sb("first_row", [q, TP]), sb("last_row", [q, TP])
        self.cont, self.whole = sb("cont", [q, TP]), sb("whole", [q, TP])
        self.run_in, self.run_out = sb("run_in", [q, TP]), sb("run_out", [q, TP])


def segment_masks(nc, m, a, s, phase, q):
    with ExitStack() as ctx:
        _, pb, sem = place(nc, ctx, phase)
        padded, loaded, turned, ends_ready = sem("padded", "loaded", "turned", "ends_ready")
        rows = pb("ends_rows", [q, 2, 1024])
        block = ctx.enter_context(nc.Block())

        @block.sync
        def _(sp):
            sp.wait_ge(padded, 1)
            load_edge_rows(sp, s.dst_i, a["dst"], loaded)
            sp.wait_ge(loaded, 48)

        @block.vector
        def _(dve):
            nc.vector.memset(s.dst_i[:], NODES).then_inc(padded, 1)
            link = chain(dve, m)
            dve.wait_ge(padded, 1)
            dve.wait_ge(loaded, 48)
            link(nc.vector.tensor_copy(s.dst[:], s.dst_i[:]))
            d = s.dst
            link(nc.vector.memset(s.same_prev[:], 0.0))
            link(nc.vector.memset(s.same_next[:], 0.0))
            link(nc.vector.tensor_tensor(s.same_prev[:, :, 1:P], d[:, :, 1:P], d[:, :, 0:P - 1], ALU.is_equal))
            link(nc.vector.tensor_tensor(s.same_next[:, :, 0:P - 1], d[:, :, 1:P], d[:, :, 0:P - 1], ALU.is_equal))
            link(nc.vector.tensor_tensor(s.in_first[:], d[:], d[:, :, 0:1].to_broadcast([P, EB, P]), ALU.is_equal))
            link(nc.vector.tensor_tensor(s.in_last[:], d[:], d[:, :, P - 1:P].to_broadcast([P, EB, P]), ALU.is_equal))
            nc.vector.tensor_copy(s.ends[:, :, 0, :], d[:, :, 0:1].to_broadcast([P, EB, q])).then_inc(ends_ready, 1)
            nc.vector.tensor_copy(s.ends[:, :, 1, :], d[:, :, P - 1:P].to_broadcast([P, EB, q])).then_inc(ends_ready, 1)
            link(nc.vector.memset(s.cont[:], 0.0))
            link(nc.vector.memset(s.run_in[:], 0.0))
            dve.wait_ge(turned, 2 * EB)
            link(nc.vector.tensor_copy(s.first[:], rows[:, 0, 0:TP]))
            link(nc.vector.tensor_copy(s.last[:], rows[:, 1, 0:TP]))
            link(nc.vector.tensor_tensor(s.cont[:, 1:TP], s.first[:, 1:TP], s.last[:, 0:TP - 1], ALU.is_equal))
            link(nc.vector.tensor_tensor(s.whole[:], s.first[:], s.last[:], ALU.is_equal))
            link(nc.vector.tensor_tensor(s.run_in[:, 1:TP], s.cont[:, 1:TP], s.whole[:, 0:TP - 1], ALU.mult))
            link(nc.vector.memset(s.run_out[:], 0.0))
            link(nc.vector.tensor_tensor(s.run_out[:, 0:TP - 1], s.cont[:, 1:TP], s.whole[:, 1:TP], ALU.mult))

        @block.tensor
        def _(pe):
            pe.wait_ge(ends_ready, 2)
            for b in range(EB):
                for k in range(2):
                    nc.tensor.transpose(rows[:, k, b * P:(b + 1) * P], s.ends[:, b, k, :], m.ident[:]).then_inc(turned, 1)


def segment_totals(nc, m, s, phase, values, total, q, maximum=False):
    with ExitStack() as ctx:
        sb, pb, sem = place(nc, ctx, phase)
        tips_ready, turned, carries_ready, returned = sem("tips_ready", "turned", "carries_ready", "returned")
        back = sb("back", [P, q, EB, P])
        mask = sb("mask", [P, EB, P])
        carry = sb("carry", [q, 2, TP])
        gate, inflow = s.first[0:q], s.last[0:q]
        cont, run_in, run_out = s.cont[0:q], s.run_in[0:q], s.run_out[0:q]
        tips, carried = sb("tips", [P, EB, 2, q]), sb("carried", [P, EB, 2, q])
        rows = pb("tip_rows", [q, 2, 1024])
        cols = pb("carry_cols", [P, EB, 2, q])
        block = ctx.enter_context(nc.Block())
        join = ALU.max if maximum else ALU.add
        decay = ALU.add if maximum else ALU.mult
        flat = lambda t: t.rearrange("p b e -> p (b e)")

        @block.vector
        def _(dve):
            link = chain(dve, m)

            def gates(out, keep):
                if maximum:
                    link(nc.vector.tensor_scalar(out, keep, 1.0, BIG, ALU.subtract, ALU.mult))
                else:
                    link(nc.vector.tensor_copy(out, keep))

            gates(mask[:], s.same_prev[:])
            for k in range(q):
                link(nc.vector.tensor_tensor_scan(flat(total[:, k]), flat(mask[:]), flat(values[:, k]),
                                                  -BIG if maximum else 0.0, decay, join))
            gates(mask[:], s.same_next[:])
            for k in range(q):
                link(nc.vector.tensor_tensor_scan(flat(back[:, k])[:, ::-1], flat(mask[:])[:, ::-1], flat(values[:, k])[:, ::-1],
                                                  -BIG if maximum else 0.0, decay, join))
            link(nc.vector.tensor_copy(tips[:, :, 0, :].rearrange("p b q -> p q b"), total[:, :, :, P - 1]))
            nc.vector.tensor_copy(tips[:, :, 1, :].rearrange("p b q -> p q b"), back[:, :, :, 0]).then_inc(tips_ready, 1)
            if maximum:
                link(nc.vector.tensor_tensor(total[:], total[:], back[:], ALU.max))
            else:
                dve.wait_ge(tips_ready, 1)
                link(nc.vector.tensor_tensor(back[:], back[:], values[:], ALU.subtract))
                link(nc.vector.tensor_tensor(total[:], total[:], back[:], ALU.add))
            dve.wait_ge(turned, 2 * EB)
            link(nc.vector.memset(inflow[:], -BIG if maximum else 0.0))
            if maximum:
                gates(gate[:], cont[:])
                link(nc.vector.tensor_tensor(inflow[:, 1:TP], rows[:, 0, 0:TP - 1], gate[:, 1:TP], ALU.add))
            else:
                link(nc.vector.tensor_tensor(inflow[:, 1:TP], rows[:, 0, 0:TP - 1], cont[:, 1:TP], ALU.mult))
            gates(gate[:], run_in[:])
            link(nc.vector.tensor_tensor_scan(carry[:, 0], gate[:], inflow[:], -BIG if maximum else 0.0, decay, join))
            link(nc.vector.memset(inflow[:], -BIG if maximum else 0.0))
            if maximum:
                gates(gate[:], cont[:])
                link(nc.vector.tensor_tensor(inflow[:, 0:TP - 1], rows[:, 1, 1:TP], gate[:, 1:TP], ALU.add))
            else:
                link(nc.vector.tensor_tensor(inflow[:, 0:TP - 1], rows[:, 1, 1:TP], cont[:, 1:TP], ALU.mult))
            gates(gate[:], run_out[:])
            nc.vector.tensor_tensor_scan(carry[:, 1, ::-1], gate[:, ::-1], inflow[:, ::-1],
                                         -BIG if maximum else 0.0, decay, join).then_inc(carries_ready, 1)
            dve.wait_ge(returned, 2 * EB)
            link(nc.vector.tensor_copy(carried[:], cols[:]))
            for k in range(2):
                inside = s.in_first if k == 0 else s.in_last
                gates(mask[:], inside[:])
                for j in range(q):
                    per_tile = carried[:, :, k, j:j + 1].to_broadcast([P, EB, P])
                    link(nc.vector.tensor_tensor(back[:, j], mask[:], per_tile, ALU.add if maximum else ALU.mult))
                    link(nc.vector.tensor_tensor(total[:, j], total[:, j], back[:, j], join))

        @block.tensor
        def _(pe):
            pe.wait_ge(tips_ready, 1)
            for b in range(EB):
                for k in range(2):
                    nc.tensor.transpose(rows[:, k, b * P:(b + 1) * P], tips[:, b, k, :], m.ident[:]).then_inc(turned, 1)
            pe.wait_ge(carries_ready, 1)
            for b in range(EB):
                for k in range(2):
                    nc.tensor.transpose(cols[:, b, k, :], carry[:, k, b * P:(b + 1) * P], m.ident[0:q, 0:q]).then_inc(returned, 1)


def turn_edges(nc, m, phase, pairs):
    with ExitStack() as ctx:
        _, pb, sem = place(nc, ctx, phase)
        turned, kept = sem("turned", "kept")
        ps = [pb(f"turn{k}", [P, 4, P]) for k in range(4)]
        block = ctx.enter_context(nc.Block())
        work = [(source, target, b, min(4, EB - b)) for source, target in pairs for b in range(0, EB, 4)]

        @block.tensor
        def _(pe):
            for n, (source, _, b, count) in enumerate(work):
                if n >= 4:
                    pe.wait_ge(kept, n - 3)
                for k in range(count):
                    last = nc.tensor.transpose(ps[n % 4][:, k, :], source[:, b + k, :], m.ident[:])
                last.then_inc(turned, 1)

        @block.vector
        def _(dve):
            for n, (_, target, b, count) in enumerate(work):
                dve.wait_ge(turned, n + 1)
                nc.vector.tensor_copy(target[:, b:b + count, :], ps[n % 4][:, 0:count, :]).then_inc(kept, 1)


def by_block(t):
    return t.rearrange("p (b t) -> p b t", t=P)


def edge_setup(nc, m, a):
    with ExitStack() as ctx:
        sb, _, _ = place(nc, ctx, "setup")
        s = Segments(nc, ctx, "setup_masks", R4)
        segment_masks(nc, m, a, s, "setup_masks", R4)
        kind = sb("kind", [P, R4, EB, P])
        count = sb("count", [P, R4, EB, P])
        ints = sb("ints", [P, 3, EB, P])
        src_key = sb("src_key", [P, EB, P])
        high = sb("high", [P, EB, P])
        rel = sb("rel", [P, EB, P])
        weight = sb("weight", [P, EB, P])
        with ExitStack() as inner:
            sb, _, sem = place(nc, inner, "setup_load")
            padded, loaded, split, keyed, kept = sem("padded", "loaded", "split", "keyed", "kept")
            low, keys = sb("low", [P, EB, P]), sb("keys", [P, 3, EB, P], BF16)
            raw = sb("raw", [P, 3, EB, P], I32)
            ea = sb("ea", [P, EB, 2 * P])
            ea2 = sb("ea2", [P, 2, EB, P])
            block = inner.enter_context(nc.Block())

            @block.sync
            def _(sp):
                sp.wait_ge(padded, 3)
                load_edge_rows(sp, raw[:, 0], a["src"], loaded)
                load_edge_rows(sp, raw[:, 1], a["edge_type_4"], loaded)
                load_edge_rows(sp, raw[:, 2], a["edge_type_8"], loaded)
                load_edge_rows(sp, weight, a["edge_weight"], loaded)
                flat = a["edge_attr_2"].rearrange("e k -> (e k)")
                last = FULL - (EB - 1) * P
                full, most = FULL * P * 2, (EB - 1) * P * P * 2
                sp.dma_start(ea[:, 0:EB - 1, :], flat[0:most].rearrange("(b t p) -> t b p", t=P, p=2 * P)).then_inc(loaded, 16)
                sp.dma_start(ea[0:last, EB - 1, :], flat[most:full].rearrange("(t p) -> t p", p=2 * P)).then_inc(loaded, 16)
                sp.dma_start(ea[last:last + 1, EB - 1, 0:2 * REST], flat[full:2 * EDGES].rearrange("(t p) -> t p", t=1)).then_inc(loaded, 16)
                sp.wait_ge(split, 3)
                for k in range(2):
                    sp.dma_start(m.t_ea[k].rearrange("(b t p) -> t b p", t=P, p=P), ea2[:, k]).then_inc(kept, 16)
                sp.wait_ge(keyed, 3)
                for k in range(3):
                    sp.dma_start(m.t_keys[k].rearrange("(b t p) -> t b p", t=P, p=P), keys[:, k]).then_inc(kept, 16)
                sp.wait_ge(kept, 5 * 16)

            @block.vector
            def _(dve):
                nc.vector.memset(raw[:], 0).then_inc(padded, 1)
                nc.vector.memset(weight[:], 0.0).then_inc(padded, 1)
                nc.vector.memset(ea[:], 0.0).then_inc(padded, 1)
                dve.wait_ge(padded, 3)
                dve.wait_ge(loaded, 16 * 15)
                link = chain(dve, m)
                nc.vector.tensor_copy(ints[:], raw[:]).then_inc(split, 1)
                for k in range(2):
                    nc.vector.tensor_copy(ea2[:, k], ea[:].rearrange("t b (p k) -> t k b p", k=2)[:, k]).then_inc(split, 1)
                dve.wait_ge(split, 3)
                for r in range(R4):
                    link(nc.vector.tensor_scalar(kind[:, r], ints[:, 1], float(r), None, ALU.is_equal))
                valid = count[:, 0]
                link(nc.vector.tensor_scalar(valid, s.dst[:], float(NODES), None, ALU.is_lt))
                link(nc.vector.tensor_tensor(rel[:], s.dst[:], s.dst[:, :, 0:1].to_broadcast([P, EB, P]), ALU.subtract))
                link(nc.vector.scalar_tensor_tensor(rel[:], rel[:], 1.0, valid, ALU.add, ALU.mult))
                link(nc.vector.tensor_scalar(rel[:], rel[:], 1.0, None, ALU.subtract))
                link(nc.vector.scalar_tensor_tensor(src_key[:], ints[:, 0], 1.0, valid, ALU.add, ALU.mult))
                link(nc.vector.tensor_scalar(src_key[:], src_key[:], 1.0, None, ALU.subtract))
                link(nc.vector.tensor_scalar(high[:], src_key[:], 63.5, 1.0 / P, ALU.subtract, ALU.mult))
                link(nc.vector.tensor_scalar(high[:], high[:], ROUNDER, None, ALU.add))
                link(nc.vector.tensor_scalar(high[:], high[:], ROUNDER, None, ALU.subtract))
                link(nc.vector.scalar_tensor_tensor(low[:], high[:], -float(P), src_key[:], ALU.mult, ALU.add))
                for k, part in ((REL, rel), (LOW, low), (HIGH, high)):
                    nc.vector.tensor_copy(keys[:, k], part[:]).then_inc(keyed, 1)
        segment_totals(nc, m, s, "setup_count", kind, count, R4)
        with ExitStack() as inner:
            _, pb, sem = place(nc, inner, "setup_index")
            turned = sem("turned")
            row = pb("base_row", [1, 1024])
            block = inner.enter_context(nc.Block())

            @block.vector
            def _(dve):
                link = chain(dve, m)
                link(nc.vector.tensor_tensor(kind[:], kind[:], count[:], ALU.mult))
                link(nc.vector.tensor_tensor(kind[:, 0:2], kind[:, 0:2], kind[:, 2:4], ALU.add))
                link(nc.vector.tensor_tensor(kind[:, 0], kind[:, 0], kind[:, 1], ALU.add))
                link(nc.vector.tensor_scalar(kind[:, 0], kind[:, 0], 1.0, None, ALU.max))
                link(nc.vector.reciprocal(kind[:, 3], kind[:, 0]))
                link(nc.vector.scalar_tensor_tensor(ints[:, 1], ints[:, 0], float(R4), ints[:, 1], ALU.mult, ALU.add))
                link(nc.vector.scalar_tensor_tensor(ints[:, 2], ints[:, 0], float(R8), ints[:, 2], ALU.mult, ALU.add))
                dve.wait_ge(turned, EB)
                link(nc.vector.tensor_copy(m.base[:], row[:, 0:TP]))

            @block.tensor
            def _(pe):
                for b in range(EB):
                    nc.tensor.transpose(row[:, b * P:(b + 1) * P], s.dst[:, b, 0:1], m.ident[:]).then_inc(turned, 1)
        turn_edges(nc, m, "setup_turn", [
            (ints[:, 0], by_block(m.src)), (src_key, by_block(m.src_key)), (high, by_block(m.src_high)), (ints[:, 1], by_block(m.src4)),
            (ints[:, 2], by_block(m.src8)), (rel, by_block(m.rel)), (kind[:, 3], by_block(m.w_rgcn)),
            (weight, by_block(m.w_edge))])


def bases(nc, m, t, engine):
    return nc.values_load_multi_w_load_instructions(
        m.base[0:1, bass.ds(t, HU)], engines=[engine], min_val=0, max_val=NODES,
        skip_runtime_bounds_check_because="a first destination is a node, or NODES in the padding")[1]


def clear_tables(nc, m, sp, zeros, zeros_ready, written, rounds):
    sem, before = rounds
    sp.wait_ge(zeros_ready, 1)
    for k in range(COPIES):
        sp.wait_ge(sem, 16 * (before + (k + 1) * ITERS // (COPIES + 2)))
        sp.dma_start(m.scatter[k].rearrange("(p r) w -> p (r w)", p=P), zeros[:]).then_inc(written, 16)
    sp.dma_start(m.t_q[ROWS:ACCW, :], zeros[:, 0:C]).then_inc(written, 16)
    sp.dma_start(m.t_last.rearrange("(p r) w -> p (r w)", p=P), zeros[:, 0:TP * 4]).then_inc(written, 16)
    sp.wait_ge(written, 16 * (COPIES + 2))


def aggregate(nc, m, phase, table, index, weights, blocks, clear=True, degree=False, clears_tables=False):
    e = m.edge
    heads = max(1, len(weights))
    row = heads * blocks * P
    outs = 2 if degree else blocks
    n = e.passes
    e.passes += 1
    hots0, e.hots = e.hots, e.hots + (T + HU) * heads
    half0, done0, used0, staged0 = n * ITERS, n * ITERS * (U - 2), n * T, n * 2 * ITERS
    with ExitStack() as ctx:
        sb, pb, sem = place(nc, ctx, phase)
        message = [sb(f"message{u}", [P, row]) for u in range(U)]
        hot = sb("hot", [P, U, heads * P])
        stage = [sb(f"index_stage{h}", [P, HU], I32) for h in range(2)]
        ps = [pb(f"window{k}", [P, outs, P]) for k in range(HU)]
        cleared, zeros_ready, written = sem("cleared", "zeros_ready", "written")
        zeros = sb("zeros", [P, (SROWS // P) * SW]) if clears_tables else None
        block = ctx.enter_context(nc.Block())

        if clears_tables:
            @block.sync
            def _(sp):
                clear_tables(nc, m, sp, zeros, zeros_ready, written, (e.gathered[0], half0))

        @block.scalar
        def _(act):
            with act.Fori(0, ITERS, 1) as it:
                for h in range(2):
                    act.wait_ge(e.half_used[h], half0 + it)
                    nc.scalar.copy(stage[h][:], index[:, bass.ds(it * U + h * HU, HU)]).then_inc(e.staged, 1)

        @block.gpsimd
        def _(pool):
            with pool.Fori(0, ITERS, 1) as it:
                for u in range(U):
                    h, k = divmod(u, HU)
                    if k == 0:
                        pool.wait_ge(e.carried, staged0 + it * 2 + h)
                        pool.wait_ge(e.staged, staged0 + it * 2 + h + 1)
                        nc.gpsimd.tensor_tensor(m.carrier[:], m.ones_i[:], m.ones_i[:], ALU.add).then_inc(e.carried, 1)
                    pool.indirect_dma_start(message[u][:], None, table,
                                            bass.IndirectOffsetOnAxis(ap=stage[h][:, k:k + 1], axis=0)).then_inc(e.gathered[u], 16)

        @block.vector
        def _(dve):
            def one_hot(t, u):
                for k in range(heads):
                    if weights:
                        ins = nc.vector.tensor_scalar(hot[:, u, k * P:(k + 1) * P], m.iota[:], m.rel[:, t], weights[k][:, t],
                                                      ALU.is_equal, ALU.mult)
                    else:
                        ins = nc.vector.tensor_scalar(hot[:, u, :], m.iota[:], m.rel[:, t], None, ALU.is_equal)
                    ins.then_inc(e.hot_ready, 1)

            if clears_tables:
                nc.vector.memset(zeros[:], 0.0).then_inc(zeros_ready, 1)
            if clear:
                nc.vector.memset(m.acc[:, 0:outs, :], 0.0).then_inc(cleared, 1)
                dve.wait_ge(cleared, 1)
            for u in range(HU):
                one_hot(slice(u, u + 1), u)
            with dve.Fori(0, ITERS, 1) as it:
                for u in range(U):
                    h, k = divmod(u, HU)
                    if k == 0:
                        dve.wait_ge(e.half_used[1 - h], half0 + it + h)
                        base = bases(nc, m, it * U + u, DVE)
                    one_hot(bass.ds(it * U + u + HU, 1), (u + HU) % U)
                    if k == HU - 1:
                        dve.wait_ge(e.half_used[h], half0 + it + 1)
                    else:
                        dve.wait_ge(e.window_ready, done0 + it * (U - 2) + u + 1 - h)
                    dve.wait_ge(e.window_used, used0 + it * U + u)
                    window = m.acc[:, 0:outs, bass.ds(base[k], P)]
                    nc.vector.tensor_tensor(window, window, ps[k][:], ALU.add).then_inc(e.window_used, 1)

        @block.tensor
        def _(pe):
            with pe.Fori(0, ITERS, 1) as it:
                for u in range(U):
                    h, k = divmod(u, HU)
                    if k == 0:
                        pe.wait_ge(e.window_used, used0 + it * U + u)
                    pe.wait_ge(e.hot_ready, hots0 + (it * U + u + 1) * heads)
                    pe.wait_ge(e.gathered[u], 16 * (half0 + it + 1))
                    for b in range(blocks):
                        for j in range(heads):
                            f = (j * blocks + b) * P
                            last = nc.tensor.matmul(ps[k][:, b, :], message[u][:, f:f + P], hot[:, u, j * P:(j + 1) * P],
                                                    start=(j == 0), stop=(j == heads - 1))
                    if degree:
                        last = nc.tensor.matmul(ps[k][:, 1, :], m.ones[:], hot[:, u, :], start=True, stop=True)
                    last.then_inc(e.half_used[h] if k == HU - 1 else e.window_ready, 1)


def load_weights(nc, m, phase, loads):
    with ExitStack() as ctx:
        _, _, sem = place(nc, ctx, phase)
        loaded = sem("weights")
        block = ctx.enter_context(nc.Block())

        @block.sync
        def _(sp):
            for tile, source in loads:
                sp.dma_start(tile, source).then_inc(loaded, 16)
            sp.wait_ge(loaded, 16 * len(loads))


def row_of(vector):
    return vector.rearrange("(a n) -> a n", a=1)


def layer_norm(nc, dve, link, b, y, out):
    for j in range(GN):
        ins = nc.vector.bn_stats(b.stats[:, j, :], y[:, j, :])
        if j == GN - 1:
            link(ins)
        else:
            ins.then_inc(b.stat_ready, 1)
    dve.wait_ge(b.stat_ready, b.g * (GN - 1) + GN - 1)
    nc.vector.memset(b.spare[:], 0.0)
    for j in range(GN):
        ins = nc.vector.bn_aggr(b.moments[:, j, :], b.stats[:, j, :])
        ins.then_inc(b.var_ready, 1)
    dve.wait_ge(b.root_ready, b.g + 1)
    link(nc.vector.reciprocal(b.rstd[:], b.root[:]))
    for j in range(GN):
        ins = nc.vector.tensor_scalar(out[:, j, :], y[:, j, :], b.moments[:, j, 0:1], b.rstd[:, j:j + 1], ALU.subtract, ALU.mult)
        ins.then_inc(b.norm_ready, 1)


def layer_norm_root(nc, act, m, b):
    act.wait_ge(b.var_ready, (b.g + 1) * GN)
    nc.scalar.activation(b.root[:], b.moments[:, :, 1], ACT.Sqrt, bias=m.epsilon[:], scale=1.0).then_inc(b.root_ready, 1)


class NormBuffers:
    def __init__(self, sb, sem):
        self.g = None
        self.stats, self.moments = sb("stats", [P, GN, 6]), sb("moments", [P, GN, 2])
        self.root, self.rstd, self.spare = sb("root", [P, GN]), sb("rstd", [P, GN]), sb("spare", [P, 1])
        self.stat_ready, self.var_ready, self.root_ready, self.norm_ready = sem("stat_ready", "var_ready", "root_ready", "norm_ready")


def degrees(nc, m):
    with ExitStack() as ctx:
        sb, pb, sem = place(nc, ctx, "degrees")
        ends, diag = sb("ends", [P, NT, P]), sb("diag", [P, NT, P])
        inverse = sb("inverse", [P, NT])
        ps = [pb(f"ps{k}", [P, 4 * P]) for k in range(4)]
        diag_ready, spread, kept = sem("diag_ready", "spread", "kept")
        block = ctx.enter_context(nc.Block())
        degree = m.acc[:, 1, 0:ROWS]
        parts = [(n, min(4 * P, ROWS - n)) for n in range(0, ROWS, 4 * P)]

        @block.vector
        def _(dve):
            link = chain(dve, m)
            flat = ends[:].rearrange("p j n -> p (j n)")
            diagonal = m.ident[:].rearrange("p (j n) -> p j n", j=1).to_broadcast([P, NT, P])
            link(nc.vector.tensor_tensor(diag[:], degree.rearrange("p (j n) -> p j n", n=P), diagonal, ALU.mult))
            link(nc.vector.tensor_reduce(m.has_edges[:], diag[:], AX.X, ALU.add))
            link(nc.vector.tensor_scalar(inverse[:], m.has_edges[:], 1.0, None, ALU.max))
            link(nc.vector.reciprocal(inverse[:], inverse[:]))
            link(nc.vector.tensor_scalar(m.has_edges[:], m.has_edges[:], 1.0, None, ALU.min))
            nc.vector.tensor_tensor(diag[:], diagonal, inverse[:].rearrange("p (j n) -> p j n", n=1).to_broadcast([P, NT, P]),
                                    ALU.mult).then_inc(diag_ready, 1)
            link(nc.vector.tensor_tensor_scan(flat, degree, degree, 0.0, ALU.add, ALU.max))
            link(nc.vector.tensor_tensor(ends[:], ends[:], diagonal, ALU.mult))
            link(nc.vector.tensor_reduce(m.last_edge_f[:], ends[:], AX.X, ALU.add))
            link(nc.vector.tensor_scalar(m.last_edge_f[:], m.last_edge_f[:], 1.0, 0.0, ALU.subtract, ALU.max))
            link(nc.vector.tensor_copy(m.last_edge[:], m.last_edge_f[:]))

        @block.tensor
        def _(pe):
            pe.wait_ge(diag_ready, 1)
            for k, (n, width) in enumerate(parts):
                if k >= 4:
                    pe.wait_ge(kept, k - 3)
                nc.tensor.matmul(ps[k % 4][:, 0:width], m.ones[:], diag[:].rearrange("p j n -> p (j n)")[:, n:n + width],
                                 start=True, stop=True).then_inc(spread, 1)

        @block.scalar
        def _(act):
            for k, (n, width) in enumerate(parts):
                act.wait_ge(spread, k + 1)
                nc.scalar.copy(m.inv_degree[:, n:n + width], ps[k % 4][:, 0:width]).then_inc(kept, 1)


def group_cols(g):
    return bass.ds(g * GW, GW)


def group_tiles(g):
    return bass.ds(g * GN, GN)


def after_block0(nc, m, a):
    with ExitStack() as ctx:
        sb, pb, sem = place(nc, ctx, "n0")
        w_in, w_t = sb("w_in", [P, C]), sb("w_t", [P, C])
        bias = sb("bias", [1, C])
        load_weights(nc, m, "n0_load", [(w_in[:], a["L0_gnn_W_neigh"]), (bias[:], row_of(a["L0_gnn_b_neigh"]))])
        mean = sb("mean", [P, GN, P])
        y = sb("y", [P, GN, C])
        ps_w, ps = pb("ps_w", [P, C]), pb("ps", [P, 8, C])
        b = NormBuffers(sb, sem)
        w_turned, w_ready, staged, made, taken, steps, stored = sem("w_turned", "w_ready", "staged", "made", "taken", "steps", "stored")
        block = ctx.enter_context(nc.Block())

        @block.tensor
        def _(pe):
            nc.tensor.transpose(ps_w[:], w_in[:], m.ident[:]).then_inc(w_turned, 1)
            pe.wait_ge(w_ready, 1)
            with pe.Fori(0, NG, 1) as g:
                pe.wait_ge(staged, g + 1)
                pe.wait_ge(taken, g)
                for j in range(GN):
                    nc.tensor.matmul(ps[:, j, :], m.ones[0:1, :], bias[:], start=True, stop=False)
                    last = nc.tensor.matmul(ps[:, j, :], mean[:, j, :], w_t[:], start=False, stop=True)
                last.then_inc(made, 1)

        @block.scalar
        def _(act):
            with act.Fori(0, NG, 1) as g:
                b.g = g
                layer_norm_root(nc, act, m, b)

        @block.vector
        def _(dve):
            dve.wait_ge(w_turned, 1)
            nc.vector.tensor_copy(w_t[:], ps_w[:]).then_inc(w_ready, 1)

            def scale(g):
                nc.vector.tensor_tensor(mean[:].rearrange("p j n -> p (j n)"), m.acc[:, 0, group_cols(g)],
                                        m.inv_degree[:, group_cols(g)], ALU.mult).then_inc(staged, 1)

            def join(g):
                dve.wait_ge(made, g + 1)
                dve.wait_ge(b.norm_ready, g * GN)
                nc.vector.tensor_tensor(y[:], ps[:, 0:GN, :], m.x[:, group_tiles(g), :], ALU.add).then_inc(taken, 1)

            def norm(g):
                b.g = g
                link = LoopChain(dve, steps, g, 2)
                dve.wait_ge(taken, g + 1)
                layer_norm(nc, dve, link, b, y, m.x[:, group_tiles(g), :])
                link.end()

            scale(0)
            with dve.Fori(0, NG - 1, 1) as g:
                join(g)
                scale(g + 1)
                norm(g)
            join(NG - 1)
            norm(NG - 1)

        @block.sync
        def _(sp):
            with sp.Fori(0, NG, 1) as g:
                sp.wait_ge(b.norm_ready, (g + 1) * GN)
                sp.dma_start(node_rows(m.t_x, g, C), m.x[:, group_tiles(g), :]).then_inc(stored, 16)
            sp.wait_ge(stored, 16 * NG)


def after_sage1(nc, m, a):
    with ExitStack() as ctx:
        sb, pb, sem = place(nc, ctx, "n1")
        wl, wr, bias = sb("wl", [P, H]), sb("wr", [P, H]), sb("bias", [1, H])
        load_weights(nc, m, "n1_load", [(wl[:], a["L1_gnn_sage1_Wl"]), (wr[:], a["L1_gnn_sage1_Wr"]), (bias[:], row_of(a["L1_gnn_sage1_b"]))])
        mean, x, x_t = sb("mean", [P, GN, P]), sb("x", [P, GN, P]), sb("x_t", [P, GN, P])
        out = sb("out", [P, GN, H])
        ps_t, ps = pb("ps_t", [P, 8, P]), pb("ps", [P, 8, H])
        staged, copied, turned, kept, made, taken, stored = sem("staged", "copied", "turned", "kept", "made", "taken", "stored")
        block = ctx.enter_context(nc.Block())

        @block.scalar
        def _(act):
            with act.Fori(0, NG, 1) as g:
                act.wait_ge(turned, g)
                nc.scalar.copy(x[:], m.x[:, group_tiles(g), :]).then_inc(copied, 1)
                act.wait_ge(made, g + 1)
                act.wait_ge(stored, 16 * g)
                nc.scalar.activation(out[:], ps[:, 0:GN, :], ACT.Relu).then_inc(taken, 1)

        @block.vector
        def _(dve):
            with dve.Fori(0, NG, 1) as g:
                dve.wait_ge(made, g)
                nc.vector.tensor_tensor(mean[:].rearrange("p j n -> p (j n)"), m.acc[:, 0, group_cols(g)],
                                        m.inv_degree[:, group_cols(g)], ALU.mult).then_inc(staged, 1)
                dve.wait_ge(turned, g + 1)
                nc.vector.tensor_copy(x_t[:], ps_t[:, 0:GN, :]).then_inc(kept, 1)

        @block.tensor
        def _(pe):
            with pe.Fori(0, NG, 1) as g:
                pe.wait_ge(copied, g + 1)
                for j in range(GN):
                    last = nc.tensor.transpose(ps_t[:, j, :], x[:, j, :], m.ident[:])
                last.then_inc(turned, 1)
                pe.wait_ge(staged, g + 1)
                pe.wait_ge(kept, g + 1)
                pe.wait_ge(taken, g)
                for j in range(GN):
                    nc.tensor.matmul(ps[:, j, :], m.ones[0:1, :], bias[:], start=True, stop=False)
                    nc.tensor.matmul(ps[:, j, :], mean[:, j, :], wl[:], start=False, stop=False)
                    last = nc.tensor.matmul(ps[:, j, :], x_t[:, j, :], wr[:], start=False, stop=True)
                last.then_inc(made, 1)

        @block.sync
        def _(sp):
            with sp.Fori(0, NG, 1) as g:
                sp.wait_ge(taken, g + 1)
                sp.dma_start(node_rows(m.t_s1, g, H), out[:]).then_inc(stored, 16)
            sp.wait_ge(stored, 16 * NG)


def attention_weights(nc, m, a, phase, w, w_al, no_bias):
    with ExitStack() as ctx:
        sb, _, sem = place(nc, ctx, phase)
        att = sb("att", [P, 2, 2 * H])
        product = sb("product", [P, 2, H])
        loaded = sem("loaded")
        block = ctx.enter_context(nc.Block())

        @block.sync
        def _(sp):
            for k, vectors in enumerate((a["L1_gnn_gat_att_src"], a["L1_gnn_gat_att_dst"])):
                row = vectors.rearrange("(a h) c -> a (h c)", a=1)
                sp.dma_start(att[:, k, :], row.to_broadcast([P, 2 * H])).then_inc(loaded, 16)
            sp.wait_ge(loaded, 32)

        @block.vector
        def _(dve):
            link = chain(dve, m)
            link(nc.vector.memset(no_bias, 0.0))
            dve.wait_ge(loaded, 32)
            for k in range(2):
                for b in range(2):
                    link(nc.vector.tensor_tensor(product[:].rearrange("p h c -> p (h c)"), w[:, b, :], att[:, k, :], ALU.mult))
                    link(nc.vector.tensor_reduce(w_al[:, b, 2 * k:2 * k + 2], product[:], AX.X, ALU.add))


def by_half(weights):
    return weights.rearrange("(b k) n -> k b n", k=P)


def after_sage2(nc, m, a):
    FA = C + 4
    with ExitStack() as ctx:
        sb, pb, sem = place(nc, ctx, "n2")
        wl, wr, wg = sb("wl", [P, 2, H]), sb("wr", [P, 2, H]), sb("wg", [P, 2, 2 * H])
        wfa = sb("wfa", [P, 2, FA])
        bias, bias_fa = sb("bias", [1, H]), sb("bias_fa", [1, FA])
        load_weights(nc, m, "n2_load", [
            (wl[:], by_half(a["L1_gnn_sage2_Wl"])), (wr[:], by_half(a["L1_gnn_sage2_Wr"])), (wg[:], by_half(a["L1_gnn_gat_W"])),
            (wfa[:, :, 0:C], by_half(a["L1_gnn_fusion_W"][0:H, :])), (bias[:], row_of(a["L1_gnn_sage2_b"])), (bias_fa[:, 0:C], row_of(a["L1_gnn_fusion_b"]))])
        attention_weights(nc, m, a, "n2_att", wg, wfa[:, :, C:FA], bias_fa[:, C:FA])
        mean = sb("mean", [P, 2, GN, P])
        s1, s2 = sb("s1", [P, GN, H]), sb("s2", [P, GN, H])
        turned_rows = sb("turned_rows", [P, 2, GN, P])
        h_out, fa_out = sb("h_out", [P, GN, 2 * H]), sb("fa_out", [P, GN, FA])
        ps_t, ps = pb("ps_t", [P, 4, 512]), pb("ps", [P, 4, 512])
        loaded, staged, turned1, kept1, made, relued, turned2, kept2, fa_made, fa_taken, h_made, h_taken, stored = sem(
            "loaded", "staged", "turned1", "kept1", "made", "relued", "turned2", "kept2", "fa_made", "fa_taken", "h_made", "h_taken", "stored")
        block = ctx.enter_context(nc.Block())
        tile = lambda k, j: ps_t[:].rearrange("p b (s n) -> p (b s) n", n=P)[:, k * 8 + j, :]
        halves = ps_t[:].rearrange("p (k b) (s n) -> p k (b s) n", k=2, n=P)
        wide = ps[:].rearrange("p b (s n) -> p (b s) n", n=H)
        fa = ps_t[:].rearrange("p b (s n) -> p (b s) n", n=H)

        @block.sync
        def _(sp):
            def load(g):
                sp.dma_start(s1[:], node_rows(m.t_s1, g, H)).then_inc(loaded, 16)

            def store(g):
                sp.wait_ge(fa_taken, g + 1)
                sp.dma_start(node_rows(m.t_f, g, C), fa_out[:, :, 0:C]).then_inc(stored, 16)
                sp.dma_start(node_rows(m.t_al, g, 4), fa_out[:, :, C:FA]).then_inc(stored, 16)
                sp.wait_ge(h_taken, (g + 1) * GN)
                sp.dma_start(node_rows(m.t_h, g, 2 * H), h_out[:]).then_inc(stored, 16)

            load(0)
            with sp.Fori(0, NG - 1, 1) as g:
                sp.wait_ge(turned1, g + 1)
                load(g + 1)
                store(g)
            store(NG - 1)
            sp.wait_ge(stored, 48 * NG)

        @block.vector
        def _(dve):
            with dve.Fori(0, NG, 1) as g:
                dve.wait_ge(made, g)
                for k in range(2):
                    nc.vector.tensor_tensor(mean[:, k].rearrange("p j n -> p (j n)"), m.acc[:, k, group_cols(g)],
                                            m.inv_degree[:, group_cols(g)], ALU.mult).then_inc(staged, 1)
                dve.wait_ge(fa_made, g + 1)
                dve.wait_ge(stored, 48 * g)
                nc.vector.tensor_copy(fa_out[:], fa[:, 0:GN, 0:FA]).then_inc(fa_taken, 1)
                for j in range(GN):
                    dve.wait_ge(h_made, g * GN + j + 1)
                    nc.vector.tensor_copy(h_out[:, j, :], ps[:, j % 4, :]).then_inc(h_taken, 1)

        @block.scalar
        def _(act):
            with act.Fori(0, NG, 1) as g:
                act.wait_ge(turned1, g + 1)
                act.wait_ge(h_made, g * GN)
                nc.scalar.copy(turned_rows[:], halves[:, :, 0:GN, :]).then_inc(kept1, 1)
                act.wait_ge(made, g + 1)
                nc.scalar.activation(s2[:], wide[:, 0:GN, :], ACT.Relu).then_inc(relued, 1)
                act.wait_ge(turned2, g + 1)
                nc.scalar.copy(turned_rows[:], halves[:, :, 0:GN, :]).then_inc(kept2, 1)

        @block.tensor
        def _(pe):
            with pe.Fori(0, NG, 1) as g:
                pe.wait_ge(loaded, 16 * (g + 1))
                pe.wait_ge(fa_taken, g)
                for j in range(GN):
                    for k in range(2):
                        last = nc.tensor.transpose(tile(k, j), s1[:, j, k * P:(k + 1) * P], m.ident[:])
                last.then_inc(turned1, 1)
                pe.wait_ge(staged, 2 * (g + 1))
                pe.wait_ge(kept1, g + 1)
                pe.wait_ge(h_taken, g * GN)
                for j in range(GN):
                    nc.tensor.matmul(wide[:, j, :], m.ones[0:1, :], bias[:], start=True, stop=False)
                    for k in range(2):
                        nc.tensor.matmul(wide[:, j, :], mean[:, k, j, :], wl[:, k, :], start=False, stop=False)
                        last = nc.tensor.matmul(wide[:, j, :], turned_rows[:, k, j, :], wr[:, k, :], start=False, stop=(k == 1))
                last.then_inc(made, 1)
                pe.wait_ge(relued, g + 1)
                for j in range(GN):
                    for k in range(2):
                        last = nc.tensor.transpose(tile(k, j), s2[:, j, k * P:(k + 1) * P], m.ident[:])
                last.then_inc(turned2, 1)
                pe.wait_ge(kept2, g + 1)
                for j in range(GN):
                    nc.tensor.matmul(fa[:, j, 0:FA], m.ones[0:1, :], bias_fa[:], start=True, stop=False)
                    for k in range(2):
                        last = nc.tensor.matmul(fa[:, j, 0:FA], turned_rows[:, k, j, :], wfa[:, k, :], start=False, stop=(k == 1))
                last.then_inc(fa_made, 1)
                for j in range(GN):
                    if j >= 4:
                        pe.wait_ge(h_taken, g * GN + j - 3)
                    for k in range(2):
                        last = nc.tensor.matmul(ps[:, j % 4, :], turned_rows[:, k, j, :], wg[:, k, :], start=(k == 0), stop=(k == 1))
                    last.then_inc(h_made, 1)


def bank_before(sem, it, q):
    return (sem[q - 2], it + 1) if q >= 2 else (sem[len(sem) + q - 2], it)


def window_load(nc, m, sp, rows, table, width, it, h, loaded):
    base = bases(nc, m, it * U + h * HU, SP)
    for k in range(HU):
        u = h * HU + k
        sp.dma_start(rows[:, u, :], table[bass.ds(base[k], P), 0:width]).then_inc(loaded[u // QU], 16)


def turned_one_hot(nc, m, act, spread, distance, out, ready, ready_n, done):
    nc.scalar.activation(distance, spread, ACT.Abs, bias=m.minus_column[:], scale=1.0).then_inc(ready, 1)
    act.wait_ge(ready, ready_n)
    nc.scalar.activation(out, distance, ACT.Relu, bias=m.ones[:, 0:1], scale=-1.0).then_inc(done, 1)


def attention_terms(nc, m):
    AQ = 8
    assert T % (AQ * QU) == 0
    with ExitStack() as ctx:
        sb, pb, sem = place(nc, ctx, "al")
        table, rest, part = sb("table", [P, NT, 4]), sb("rest", [P, 2, NT]), sb("part", [P, 2, NT])
        parts = sb("parts", [P, 3, 2, NT], BF16)
        keys = sb("keys", [1, AQ, QU * P], BF16)
        low_hot, distance = sb("low_hot", [P, 2, QU * P], BF16), sb("distance", [P, 2, QU * P])
        high_hot, product = sb("high_hot", [P, 2, QU, NT]), sb("product", [P, 2, QU, 2, NT])
        picked = sb("picked", [P, 2, QU, 2])
        ps_low = [pb(f"ps_low{k}", [P, QU * P]) for k in range(2)]
        ps = [pb(f"ps{k}", [P, QU, P]) for k in range(2)]
        keys_in, spread, low_ready, looked, high_ready, product_ready, reduced, kept = (
            [sem(f"{n}{q}") for q in range(AQ)]
            for n in ("keys_in", "spread", "low_ready", "looked", "high_ready", "product_ready", "reduced", "kept"))
        table_in, table_ready, distance_ready, zeroed, placed = sem("table_in", "table_ready", "distance_ready", "zeroed", "placed")
        block = ctx.enter_context(nc.Block())

        @block.sync
        def _(sp):
            sp.dma_start(table[:], m.t_al[0:ROWS, :].rearrange("(j p) f -> p j f", p=P)).then_inc(table_in, 16)
            with sp.Fori(0, T // (AQ * QU), 1) as it:
                for q in range(AQ):
                    sp.wait_ge(spread[q], it)
                    sp.dma_start(keys[:, q], m.t_keys[LOW:LOW + 1, bass.ds(((it * AQ + q) * QU) * P, QU * P)]).then_inc(keys_in[q], 16)

        @block.gpsimd
        def _(pool):
            pool.wait_ge(table_in, 16)
            for j in range(NT):
                rows = P if j < NT - 1 else TAIL
                pool.indirect_dma_start(m.t_last, bass.IndirectOffsetOnAxis(ap=m.last_edge[0:rows, j:j + 1], axis=0), table[0:rows, j, :],
                                        None).then_inc(placed, 16)
            pool.wait_ge(placed, 16 * NT)

        @block.scalar
        def _(act):
            def keep(it, q):
                act.wait_ge(zeroed, 1)
                act.wait_ge(reduced[q], it + 1)
                tiles = bass.ds((it * AQ + q) * QU, QU)
                nc.scalar.copy(m.e[:, :, tiles].rearrange("p k t -> p t k"), picked[:, q % 2]).then_inc(kept[q], 1)

            with act.Fori(0, T // (AQ * QU), 1) as it:
                for q in range(AQ):
                    act.wait_ge(spread[q], it + 1)
                    act.wait_ge(*bank_before(looked, it, q))
                    turned_one_hot(nc, m, act, ps_low[q % 2][:], distance[:, q % 2, :], low_hot[:, q % 2, :],
                                   distance_ready, it * AQ + q + 1, low_ready[q])
                    if q >= 2:
                        keep(it, q - 2)
                for q in range(AQ - 2, AQ):
                    keep(it, q)

        @block.vector
        def _(dve):
            dve.wait_ge(table_in, 16)
            nc.vector.memset(m.e[:], 0.0).then_inc(zeroed, 1)
            link = chain(dve, m)
            link(nc.vector.tensor_copy(rest[:].rearrange("p k j -> p j k"), table[:, :, 0:2]))
            for k in range(3):
                nc.vector.tensor_copy(parts[:, k], rest[:]).then_inc(table_ready, 1)
                dve.wait_ge(table_ready, k + 1)
                if k < 2:
                    link(nc.vector.tensor_copy(part[:], parts[:, k]))
                    link(nc.vector.tensor_tensor(rest[:], rest[:], part[:], ALU.subtract))

            def reduce(it, q):
                dve.wait_ge(product_ready[q], it + 1)
                dve.wait_ge(*bank_before(kept, it, q))
                nc.vector.tensor_reduce(picked[:, q % 2], product[:, q % 2], AX.X, ALU.add).then_inc(reduced[q], 1)

            with dve.Fori(0, T // (AQ * QU), 1) as it:
                for q in range(AQ):
                    p = q % 2
                    dve.wait_ge(*bank_before(product_ready, it, q))
                    high = m.src_high[:, bass.ds((it * AQ + q) * QU, QU)].rearrange("p (t a) -> p t a", a=1).to_broadcast([P, QU, NT])
                    places = m.iota[:, 0:NT].rearrange("p (a j) -> p a j", a=1).to_broadcast([P, QU, NT])
                    nc.vector.tensor_tensor(high_hot[:, p], places, high, ALU.is_equal).then_inc(high_ready[q], 1)
                    if q >= 1:
                        reduce(it, q - 1)
                    dve.wait_ge(high_ready[q], it + 1)
                    dve.wait_ge(looked[q], it + 1)
                    dve.wait_ge(*bank_before(reduced, it, q))
                    nc.vector.tensor_tensor(product[:, p], ps[p][:, :, 0:2 * NT].rearrange("p t (k j) -> p t k j", k=2),
                                            high_hot[:, p].rearrange("p t (a j) -> p t a j", a=1).to_broadcast([P, QU, 2, NT]),
                                            ALU.mult).then_inc(product_ready[q], 1)
                reduce(it, AQ - 1)

        @block.tensor
        def _(pe):
            def look_up(it, q):
                pe.wait_ge(low_ready[q], it + 1)
                pe.wait_ge(*bank_before(product_ready, it, q))
                for k in range(QU):
                    for n in range(3):
                        last = nc.tensor.matmul(ps[q % 2][:, k, 0:2 * NT], low_hot[:, q % 2, k * P:(k + 1) * P],
                                                parts[:, n].rearrange("p k j -> p (k j)"), start=(n == 0), stop=(n == 2))
                last.then_inc(looked[q], 1)

            pe.wait_ge(table_ready, 3)
            with pe.Fori(0, T // (AQ * QU), 1) as it:
                for q in range(AQ):
                    pe.wait_ge(keys_in[q], 16 * (it + 1))
                    pe.wait_ge(*bank_before(low_ready, it, q))
                    nc.tensor.matmul(ps_low[q % 2][:], m.spread_one[:], keys[:, q], start=True, stop=True).then_inc(spread[q], 1)
                    if q >= 1:
                        look_up(it, q - 1)
                look_up(it, AQ - 1)


def attention_softmax(nc, m, a):
    with ExitStack() as ctx:
        sb, _, _ = place(nc, ctx, "softmax")
        s = Segments(nc, ctx, "softmax_masks", 4)
        segment_masks(nc, m, a, s, "softmax_masks", 4)
        at_dst = sb("at_dst", [P, 4, EB, P])
        top, total = at_dst[:, 0:2], at_dst[:, 2:4]
        with ExitStack() as inner:
            sb_in, _, sem = place(nc, inner, "softmax_dst")
            last_in = sem("last_in")
            last = sb_in("last", [P, EB, P, 4])
            with nc.Block() as block:
                @block.sync
                def _(sp):
                    sp.dma_start(last[:].rearrange("t b p k -> t b (p k)"), m.t_last.rearrange("(b t p) k -> t b (p k)", t=P, p=P)).then_inc(last_in, 16)
                    sp.wait_ge(last_in, 16)
            segment_totals(nc, m, s, "softmax_dst", last[:].rearrange("t b p k -> t k b p"), at_dst, 4)
        e, own = sb("e", [P, 2, EB, P]), sb("own", [P, 2, EB, P])
        self_weight = sb("self_weight", [P, EB, P, 2])
        turn_edges(nc, m, "softmax_turn", [(by_block(m.e[:, k]), e[:, k]) for k in range(2)])
        with ExitStack() as inner:
            block = inner.enter_context(nc.Block())

            @block.vector
            def _(dve):
                link = chain(dve, m)
                link(nc.vector.tensor_tensor(e[:], e[:], at_dst[:, 2:4], ALU.add))
                link(nc.vector.tensor_tensor(own[:], at_dst[:, 0:2], at_dst[:, 2:4], ALU.add))
                for t in (e, own):
                    link(nc.vector.tensor_scalar(total, t[:], 0.2, None, ALU.mult))
                    link(nc.vector.tensor_tensor(t[:], t[:], total, ALU.max))
        segment_totals(nc, m, s, "softmax_top", e, top, 2, maximum=True)
        with ExitStack() as inner:
            _, _, sem = place(nc, inner, "softmax_exp")
            shifted, raised = sem("shifted", "raised")
            block = inner.enter_context(nc.Block())

            @block.vector
            def _(dve):
                link = chain(dve, m)
                link(nc.vector.tensor_tensor(top, top, own[:], ALU.max))
                nc.vector.tensor_tensor(e[:], e[:], top, ALU.subtract).then_inc(shifted, 1)
                nc.vector.tensor_tensor(own[:], own[:], top, ALU.subtract).then_inc(shifted, 1)

            @block.scalar
            def _(act):
                for n, t in enumerate((e, own)):
                    act.wait_ge(shifted, n + 1)
                    nc.scalar.activation(t[:], t[:], ACT.Exp).then_inc(raised, 1)
                act.wait_ge(raised, 2)
        segment_totals(nc, m, s, "softmax_sum", e, total, 2)
        with ExitStack() as inner:
            sb, _, sem = place(nc, inner, "softmax_self")
            weighed, kept = sem("weighed", "kept")
            block = inner.enter_context(nc.Block())

            @block.vector
            def _(dve):
                link = chain(dve, m)
                link(nc.vector.tensor_tensor(total, total, own[:], ALU.add))
                link(nc.vector.tensor_scalar(total, total, 1e-16, None, ALU.max))
                link(nc.vector.reciprocal(top, total))
                link(nc.vector.tensor_scalar(top, top, 0.5, None, ALU.mult))
                link(nc.vector.tensor_tensor(e[:], e[:], top, ALU.mult))
                nc.vector.tensor_tensor(self_weight[:].rearrange("p b t k -> p k b t"), own[:], top, ALU.mult).then_inc(weighed, 1)

            @block.sync
            def _(sp):
                sp.wait_ge(weighed, 1)
                sp.dma_start(m.t_self.rearrange("(b t p) k -> t b (p k)", t=P, p=P),
                             self_weight[:].rearrange("t b p k -> t b (p k)")).then_inc(kept, 16)
                sp.wait_ge(kept, 16)
        turn_edges(nc, m, "softmax_back", [(e[:, k], by_block(m.alpha[:, k])) for k in range(2)])
        with ExitStack() as inner:
            sb, _, sem = place(nc, inner, "softmax_nodes")
            got = sem("got")
            rows = sb("rows", [P, NT, 2])
            block = inner.enter_context(nc.Block())

            @block.gpsimd
            def _(pool):
                for j in range(NT):
                    pool.indirect_dma_start(rows[:, j, :], None, m.t_self,
                                            bass.IndirectOffsetOnAxis(ap=m.last_edge[:, j:j + 1], axis=0)).then_inc(got, 16)

            @block.vector
            def _(dve):
                link = chain(dve, m)
                dve.wait_ge(got, 16 * NT)
                link(nc.vector.tensor_scalar(rows[:], rows[:], 0.5, None, ALU.subtract))
                link(nc.vector.tensor_tensor(rows[:], rows[:], m.has_edges[:].rearrange("p (j k) -> p j k", k=1).to_broadcast([P, NT, 2]), ALU.mult))
                link(nc.vector.tensor_scalar(m.self_weight[:], rows[:], 0.5, None, ALU.add))


def after_gat(nc, m, a):
    with ExitStack() as ctx:
        sb, pb, sem = place(nc, ctx, "n3")
        wrel, wroot, wf = sb("wrel", [P, 2, R4, C]), sb("wroot", [P, 2, C]), sb("wf", [P, 2, C])
        bias, bias_root = sb("bias", [1, H]), sb("bias_root", [P, 1])
        load_weights(nc, m, "n3_load", [
            *[(wrel[:, k], a["L1_gnn_rgcn_Wrel"].rearrange("r (b k) n -> b k r n", k=P)[k]) for k in range(2)],
            (wroot[:], by_half(a["L1_gnn_rgcn_Wroot"])), (wf[:], by_half(a["L1_gnn_fusion_W"][H:2 * H, :])),
            (bias[:], row_of(a["L1_gnn_gat_b"])), (bias_root[:], a["L1_gnn_rgcn_b"].rearrange("(n a) -> n a", a=1))])
        sums = sb("sums", [P, 2, GN, P])
        h, f = sb("h", [P, GN, 2 * H]), sb("f", [P, GN, C])
        x_out, f_out = sb("x_out", [P, GN, 2 * H]), sb("f_out", [P, GN, C])
        y = sb("y", [P, GN, H])
        y_t = sb("y_t", [P, 2, GN, P])
        ps_t, ps = pb("ps_t", [P, 4, 512]), pb("ps", [P, 4, 512])
        loaded, staged, made, partly, summed, relued, turned, kept, f_made, f_taken, root_made, root_taken, x_made, x_taken, stored = sem(
            "loaded", "staged", "made", "partly", "summed", "relued", "turned", "kept", "f_made", "f_taken", "root_made", "root_taken",
            "x_made", "x_taken", "stored")
        block = ctx.enter_context(nc.Block())
        tile = lambda k, j: ps_t[:].rearrange("p b (s n) -> p (b s) n", n=P)[:, k * 8 + j, :]
        halves = ps_t[:].rearrange("p (k b) (s n) -> p k (b s) n", k=2, n=P)
        quarter = ps_t[:].rearrange("p b (s n) -> p (b s) n", n=P)
        root = ps_t[:, 2:4, 0:GW // 2]
        wide = ps[:].rearrange("p b (s n) -> p (b s) n", n=H)

        @block.sync
        def _(sp):
            def load(g):
                sp.dma_start(h[:], node_rows(m.t_h, g, 2 * H)).then_inc(loaded, 16)
                sp.dma_start(f[:], node_rows(m.t_f, g, C)).then_inc(loaded, 16)

            def store(g):
                sp.wait_ge(f_taken, g + 1)
                sp.dma_start(node_rows(m.t_f, g, C), f_out[:]).then_inc(stored, 16)
                sp.wait_ge(x_taken, (g + 1) * GN)
                sp.dma_start(node_rows(m.t_rel4, g, R4 * C), x_out[:]).then_inc(stored, 16)

            load(0)
            with sp.Fori(0, NG - 1, 1) as g:
                sp.wait_ge(summed, (g + 1) * GN)
                sp.wait_ge(f_taken, g + 1)
                load(g + 1)
                store(g)
            store(NG - 1)
            sp.wait_ge(stored, 32 * NG)

        @block.scalar
        def _(act):
            with act.Fori(0, NG, 1) as g:
                act.wait_ge(made, g)
                nc.scalar.copy(sums[:].rearrange("p k j n -> p k (j n)"), m.acc[:, 0:2, group_cols(g)]).then_inc(staged, 1)
                act.wait_ge(summed, (g + 1) * GN)
                nc.scalar.activation(y[:], y[:], ACT.Relu).then_inc(relued, 1)
                act.wait_ge(turned, g + 1)
                act.wait_ge(x_made, g * GN)
                nc.scalar.copy(y_t[:], halves[:, :, 0:GN, :]).then_inc(kept, 1)

        @block.vector
        def _(dve):
            with dve.Fori(0, NG, 1) as g:
                dve.wait_ge(loaded, 32 * (g + 1))
                dve.wait_ge(made, g + 1)
                dve.wait_ge(turned, g)
                for j in range(GN):
                    nc.vector.scalar_tensor_tensor(y[:, j, :], h[:, j, 0:H], m.self_weight[:, bass.ds(g * GN + j, 1), 0], wide[:, j, :],
                                                   ALU.mult, ALU.add).then_inc(partly, 1)
                dve.wait_ge(partly, (g + 1) * GN)
                for j in range(GN):
                    nc.vector.scalar_tensor_tensor(y[:, j, :], h[:, j, H:2 * H], m.self_weight[:, bass.ds(g * GN + j, 1), 1], y[:, j, :],
                                                   ALU.mult, ALU.add).then_inc(summed, 1)
                dve.wait_ge(f_made, g + 1)
                dve.wait_ge(stored, 32 * g)
                nc.vector.tensor_tensor(f_out[:], f[:], quarter[:, 0:GN, :], ALU.add).then_inc(f_taken, 1)
                dve.wait_ge(root_made, g + 1)
                nc.vector.tensor_scalar(m.acc[:, 0, group_cols(g)].rearrange("p (b n) -> p b n", b=2), root, bias_root[:], None,
                                        ALU.add).then_inc(root_taken, 1)
                for j in range(GN):
                    dve.wait_ge(x_made, g * GN + j + 1)
                    nc.vector.tensor_copy(x_out[:, j, :], ps[:, j % 4, :]).then_inc(x_taken, 1)

        @block.tensor
        def _(pe):
            with pe.Fori(0, NG, 1) as g:
                pe.wait_ge(staged, g + 1)
                pe.wait_ge(x_taken, g * GN)
                for j in range(GN):
                    nc.tensor.matmul(wide[:, j, :], m.ones[0:1, :], bias[:], start=True, stop=False, skip_group_check=True)
                    for k in range(2):
                        last = nc.tensor.matmul(wide[:, j, k * P:(k + 1) * P], sums[:, k, j, :], m.ident[:], start=False, stop=True,
                                                skip_group_check=True)
                last.then_inc(made, 1)
                pe.wait_ge(relued, g + 1)
                pe.wait_ge(root_taken, g)
                for j in range(GN):
                    for k in range(2):
                        last = nc.tensor.transpose(tile(k, j), y[:, j, k * P:(k + 1) * P], m.ident[:])
                last.then_inc(turned, 1)
                pe.wait_ge(kept, g + 1)
                for j in range(GN):
                    for k in range(2):
                        last = nc.tensor.matmul(quarter[:, j, :], y_t[:, k, j, :], wf[:, k, :], start=(k == 0), stop=(k == 1))
                last.then_inc(f_made, 1)
                for b in range(2):
                    for k in range(2):
                        nodes = y_t[:, k].rearrange("p j n -> p (j n)")[:, b * (GW // 2):(b + 1) * (GW // 2)]
                        last = nc.tensor.matmul(root[:, b, :], wroot[:, k, :], nodes, start=(k == 0), stop=(k == 1))
                last.then_inc(root_made, 1)
                for j in range(GN):
                    if j >= 4:
                        pe.wait_ge(x_taken, g * GN + j - 3)
                    for k in range(2):
                        last = nc.tensor.matmul(ps[:, j % 4, :], y_t[:, k, j, :], wrel[:, k].rearrange("p r n -> p (r n)"), start=(k == 0), stop=(k == 1))
                    last.then_inc(x_made, 1)


def after_rgcn(nc, m, a):
    with ExitStack() as ctx:
        sb, pb, sem = place(nc, ctx, "n4")
        wf, w1 = sb("wf", [P, C]), sb("w1", [P, 2, C])
        bias = sb("bias", [1, C])
        load_weights(nc, m, "n4_load", [(wf[:], a["L1_gnn_fusion_W"][2 * H:2 * H + C, :]), (w1[:], by_half(a["L2_gnn_W1"][0:2 * C, :])),
                                        (bias[:], row_of(a["L2_gnn_b1"]))])
        rgcn, f = sb("rgcn", [P, GN, P]), sb("f", [P, GN, C])
        out, square = sb("out", [P, GN, C]), sb("square", [P, GN, C])
        length = sb("length", [P, 3, GN])
        x, x_t = sb("x", [P, GN, C]), sb("x_t", [P, GN, P])
        pq = sb("pq", [P, GN, 2 * C])
        ps_f, ps_t, ps = pb("ps_f", [P, 8, C]), pb("ps_t", [P, 8, P]), pb("ps", [P, 8, 2 * C])
        b = NormBuffers(sb, sem)
        loaded, staged, made, fused, squared, length_ready, length_root, steps, joined, turned, kept, pq_made, pq_taken, stored = sem(
            "loaded", "staged", "made", "fused", "squared", "length_ready", "length_root", "steps", "joined", "turned", "kept", "pq_made",
            "pq_taken", "stored")
        x_kept = sem("x_kept")
        block = ctx.enter_context(nc.Block())

        @block.sync
        def _(sp):
            def load(g):
                sp.dma_start(f[:], node_rows(m.t_f, g, C)).then_inc(loaded, 16)

            def store(g):
                sp.wait_ge(pq_taken, g + 1)
                sp.dma_start(node_rows(m.t_p, g, C), pq[:, :, 0:C]).then_inc(stored, 16)
                sp.dma_start(node_rows(m.t_q, g, C), pq[:, :, C:2 * C]).then_inc(stored, 16)

            load(0)
            with sp.Fori(0, NG - 1, 1) as g:
                sp.wait_ge(fused, g + 1)
                load(g + 1)
                store(g)
            store(NG - 1)
            sp.wait_ge(stored, 32 * NG)

        @block.scalar
        def _(act):
            def before_norm(g):
                b.g = g
                act.wait_ge(made, g)
                nc.scalar.copy(rgcn[:].rearrange("p j n -> p (j n)"), m.acc[:, 0, group_cols(g)]).then_inc(staged, 1)
                act.wait_ge(length_ready, g + 1)
                nc.scalar.activation(length[:, 1, :], length[:, 0, :], ACT.Sqrt).then_inc(length_root, 1)
                layer_norm_root(nc, act, m, b)

            def after_norm(g):
                act.wait_ge(turned, g + 1)
                act.wait_ge(pq_made, g)
                nc.scalar.copy(x_t[:], ps_t[:, 0:GN, :]).then_inc(kept, 1)
                nc.scalar.copy(m.x[:, group_tiles(g), :], x[:]).then_inc(x_kept, 1)

            def take(g):
                act.wait_ge(pq_made, g + 1)
                act.wait_ge(stored, 32 * g)
                nc.scalar.copy(pq[:], ps[:, 0:GN, :]).then_inc(pq_taken, 1)

            before_norm(0)
            after_norm(0)
            with act.Fori(0, NG - 1, 1) as g:
                before_norm(g + 1)
                take(g)
                after_norm(g + 1)
            take(NG - 1)

        @block.vector
        def _(dve):
            with dve.Fori(0, NG, 1) as g:
                b.g = g
                link = LoopChain(dve, steps, g, 3 + 2)
                dve.wait_ge(loaded, 16 * (g + 1))
                dve.wait_ge(made, g + 1)
                nc.vector.tensor_tensor(out[:], ps_f[:, 0:GN, :], f[:], ALU.add).then_inc(fused, 1)
                dve.wait_ge(fused, g + 1)
                link(nc.vector.tensor_tensor(square[:], out[:], out[:], ALU.mult))
                nc.vector.tensor_reduce(length[:, 0, :], square[:], AX.X, ALU.add).then_inc(length_ready, 1)
                dve.wait_ge(length_root, g + 1)
                link(nc.vector.tensor_scalar(length[:, 1, :], length[:, 1, :], 1e-12, None, ALU.max))
                link(nc.vector.reciprocal(length[:, 2, :], length[:, 1, :]))
                for j in range(GN):
                    nc.vector.scalar_tensor_tensor(out[:, j, :], out[:, j, :], length[:, 2, j:j + 1], m.x[:, bass.ds(g * GN + j, 1), :],
                                                   ALU.mult, ALU.add).then_inc(joined, 1)
                dve.wait_ge(joined, (g + 1) * GN)
                dve.wait_ge(x_kept, g)
                layer_norm(nc, dve, link, b, out, x)
                link.end()

        @block.tensor
        def _(pe):
            def fuse(g):
                pe.wait_ge(staged, g + 1)
                pe.wait_ge(fused, g)
                for j in range(GN):
                    last = nc.tensor.matmul(ps_f[:, j, :], rgcn[:, j, :], wf[:], start=True, stop=True)
                last.then_inc(made, 1)

            def turn(g):
                pe.wait_ge(b.norm_ready, (g + 1) * GN)
                pe.wait_ge(kept, g)
                for j in range(GN):
                    last = nc.tensor.transpose(ps_t[:, j, :], x[:, j, :], m.ident[:])
                last.then_inc(turned, 1)

            def products(g):
                pe.wait_ge(kept, g + 1)
                pe.wait_ge(pq_taken, g)
                for j in range(GN):
                    nc.tensor.matmul(ps[:, j, :], x_t[:, j, :], w1[:].rearrange("p b n -> p (b n)"), start=True, stop=False, skip_group_check=True)
                    last = nc.tensor.matmul(ps[:, j, 0:C], m.ones[0:1, :], bias[:], start=False, stop=True, skip_group_check=True)
                last.then_inc(pq_made, 1)

            fuse(0)
            turn(0)
            with pe.Fori(0, NG - 1, 1) as g:
                fuse(g + 1)
                products(g)
                turn(g + 1)
            products(NG - 1)


def edge_hidden(nc, m, a):
    with ExitStack() as ctx:
        sb, pb, sem = place(nc, ctx, "eh")
        w1c = sb("w1c", [2, C])
        load_weights(nc, m, "eh_load", [(w1c[:], a["L2_gnn_W1"][2 * C:2 * C + 2, :])])
        window = sb("window", [P, U, C])
        message = sb("message", [P, U, C])
        stage = [sb(f"stage{h}", [P, HU], I32) for h in range(2)]
        rel_keys, src_keys = sb("rel_keys", [1, U * P], BF16), sb("src_keys", [2, U * P], BF16)
        attr = sb("attr", [2, U * P])
        distance, hot_t = sb("distance", [P, QUADS, QU * P]), sb("hot_t", [P, QUADS, QU * P])
        both = sb("both", [P, U, 2, C])
        hidden, square = both[:, :, 0, :], both[:, :, 1, :]
        junk, seen = sb("junk", [P, 2, QU, P]), sb("seen", [P, 2, QU])
        valid = sb("valid", [P, TP])
        ps = pb("ps", [P, U, C])
        ps_rel = pb("ps_rel", [P, QU * P])
        ps_src = [pb(f"ps_src{k}", [P, QU, P]) for k in range(2)]
        ps_sum = pb("ps_sum", [1, 2 * C])
        gathered, made, spread, rel_ready, added, squared, summed, counted = (
            [sem(f"{n}{q}") for q in range(QUADS)] for n in ("gathered", "made", "spread", "rel_ready", "added", "squared", "summed", "counted"))
        keys_in, stored, staged = ([sem(f"{n}{h}") for h in range(2)] for n in ("keys_in", "stored", "staged"))
        window_in = [sem(f"window_in{q}") for q in range(QUADS)]
        carried, distance_ready, counts, zeroed, cleared = sem("carried", "distance_ready", "counts", "zeroed", "cleared")
        masked = [sem(f"masked{q}") for q in range(QUADS)]
        mask = sb("mask", [P, U])
        block = ctx.enter_context(nc.Block())
        quad = lambda q: slice(q * QU, (q + 1) * QU)
        edges_of = lambda q: slice(q * QU * P, (q + 1) * QU * P)

        @block.sync
        def _(sp):
            def load(it, h):
                edges, slot = bass.ds((it * U + h * HU) * P, HU * P), slice(h * HU * P, (h + 1) * HU * P)
                sp.dma_start(rel_keys[:, slot], m.t_keys[REL:REL + 1, edges]).then_inc(keys_in[h], 16)
                sp.dma_start(src_keys[:, slot], m.t_keys[LOW:HIGH + 1, edges]).then_inc(keys_in[h], 16)
                sp.dma_start(attr[:, slot], m.t_ea[:, edges]).then_inc(keys_in[h], 16)
                window_load(nc, m, sp, window, m.t_q, C, it, h, window_in)

            def store(it, h):
                for q in (2 * h, 2 * h + 1):
                    sp.wait_ge(added[q], it + 1)
                sp.dma_start(m.t_hidden[bass.ds((it * U + h * HU) * P, HU * P), :].rearrange("(t p) f -> p t f", p=P),
                             hidden[:, h * HU:(h + 1) * HU, :]).then_inc(stored[h], 16)

            for h in range(2):
                load(0, h)
            with sp.Fori(0, ITERS - 1, 1) as it:
                for h in range(2):
                    for q in (2 * h, 2 * h + 1):
                        sp.wait_ge(made[q], it + 1)
                    load(it + 1, h)
                    store(it, h)
            for h in range(2):
                store(ITERS - 1, h)
            for h in range(2):
                sp.wait_ge(stored[h], 16 * ITERS)

        @block.gpsimd
        def _(pool):
            with pool.Fori(0, ITERS, 1) as it:
                for u in range(U):
                    h, k = divmod(u, HU)
                    if k == 0:
                        pool.wait_ge(carried, it * 2 + h)
                        pool.wait_ge(staged[h], it + 1)
                        nc.gpsimd.tensor_tensor(m.carrier[:], m.ones_i[:], m.ones_i[:], ALU.add).then_inc(carried, 1)
                    pool.indirect_dma_start(message[:, u, :], None, m.t_p,
                                            bass.IndirectOffsetOnAxis(ap=stage[h][:, k:k + 1], axis=0)).then_inc(gathered[u // QU], 16)

        @block.scalar
        def _(act):
            def stage_indices(it, h):
                nc.scalar.copy(stage[h][:], m.src[:, bass.ds(it * U + h * HU, HU)]).then_inc(staged[h], 1)

            def one_hot(it, q):
                act.wait_ge(spread[q], it + 1)
                turned_one_hot(nc, m, act, ps_rel[:], distance[:, q], hot_t[:, q], distance_ready, it * QUADS + q + 1, rel_ready[q])

            for h in range(2):
                stage_indices(0, h)
            for q in range(QUADS):
                one_hot(0, q)
            with act.Fori(0, ITERS - 1, 1) as it:
                for q in range(QUADS):
                    act.wait_ge(added[q], it + 1)
                    if q % 2 == 1:
                        stage_indices(it + 1, q // 2)
                    act.wait_ge(summed[q], it)
                    nc.scalar.copy(mask[:, quad(q)], valid[:, bass.ds(it * U + q * QU, QU)]).then_inc(masked[q], 1)
                    nc.scalar.activation(square[:, quad(q), :], hidden[:, quad(q), :], ACT.Square).then_inc(squared[q], 1)
                    act.wait_ge(made[q], it + 1)
                    one_hot(it + 1, q)
            for q in range(QUADS):
                act.wait_ge(added[q], ITERS)
                act.wait_ge(summed[q], ITERS - 1)
                nc.scalar.copy(mask[:, quad(q)], valid[:, (ITERS - 1) * U + q * QU:(ITERS - 1) * U + (q + 1) * QU]).then_inc(masked[q], 1)
                nc.scalar.activation(square[:, quad(q), :], hidden[:, quad(q), :], ACT.Square).then_inc(squared[q], 1)

        @block.vector
        def _(dve):
            nc.vector.memset(both[:, 0], 0.0).then_inc(zeroed, 1)
            nc.vector.tensor_scalar(valid[:], m.rel[:], 0.0, None, ALU.is_ge).then_inc(zeroed, 1)

            def count_seen(it, q):
                dve.wait_ge(spread[q], it + 1)
                for k in range(QU):
                    t = it * U + q * QU + k
                    nc.vector.scalar_tensor_tensor(junk[:, q % 2, k, :], ps_src[q % 2][:, k, :], m.src_key[:, bass.ds(t, 1)], m.before[:],
                                                   ALU.is_equal, ALU.mult, accum_out=seen[:, q % 2, k:k + 1]).then_inc(counts, 1)
                dve.wait_ge(counts, (it * QUADS + q + 1) * QU)
                nc.vector.tensor_copy(m.seen[:, bass.ds(it * U + q * QU, QU)], seen[:, q % 2, :]).then_inc(counted[q], 1)

            def add(it, q):
                dve.wait_ge(stored[q // 2], 16 * it)
                dve.wait_ge(summed[q], it)
                dve.wait_ge(cleared, 1)
                dve.wait_ge(gathered[q], 16 * QU * (it + 1))
                dve.wait_ge(made[q], it + 1)
                nc.vector.tensor_tensor(hidden[:, quad(q), :], ps[:, quad(q), :], message[:, quad(q), :], ALU.add).then_inc(added[q], 1)

            for q in range(QUADS):
                if q >= 2:
                    dve.wait_ge(counted[q - 2], 1)
                count_seen(0, q)
            with dve.Fori(0, ITERS - 1, 1) as it:
                for q in range(QUADS):
                    add(it, q)
                    dve.wait_ge(*bank_before(counted, it + 1, q))
                    count_seen(it + 1, q)
            for q in range(QUADS):
                add(ITERS - 1, q)
            for q in range(QUADS):
                dve.wait_ge(summed[q], ITERS)
            nc.vector.tensor_copy(m.totals[:], ps_sum[:]).then_inc(zeroed, 1)

        @block.tensor
        def _(pe):
            def spread_keys(it, q, waits):
                pe.wait_ge(keys_in[q // 2], 48 * (it + 1))
                for sem_, count in waits:
                    pe.wait_ge(sem_, count)
                nc.tensor.matmul(ps_rel[:], m.spread_one[:], rel_keys[:, edges_of(q)], start=True, stop=True)
                nc.tensor.matmul(ps_src[q % 2][:].rearrange("p k e -> p (k e)"), m.spread_src[:], src_keys[:, edges_of(q)],
                                 start=True, stop=True).then_inc(spread[q], 1)

            def look_up(it, q):
                pe.wait_ge(rel_ready[q], it + 1)
                pe.wait_ge(window_in[q], 16 * QU * (it + 1))
                for k in range(QU):
                    u = q * QU + k
                    nc.tensor.matmul(ps[:, u, :], hot_t[:, q, k * P:(k + 1) * P], window[:, u, :], start=True, stop=False)
                    last = nc.tensor.matmul(ps[:, u, :], attr[:, u * P:(u + 1) * P], w1c[:], start=False, stop=True)
                last.then_inc(made[q], 1)

            def add_up(it, q):
                pe.wait_ge(squared[q], it + 1)
                pe.wait_ge(masked[q], it + 1)
                for k in range(QU):
                    u = q * QU + k
                    last = nc.tensor.matmul(ps_sum[:], mask[:, u:u + 1], both[:, u].rearrange("p c f -> p (c f)"), start=False, stop=True,
                                            skip_group_check=True)
                last.then_inc(summed[q], 1)

            pe.wait_ge(zeroed, 2)
            nc.tensor.matmul(ps_sum[:], m.ones[:, 0:1], both[:, 0].rearrange("p c f -> p (c f)"), start=True, stop=False,
                             skip_group_check=True).then_inc(cleared, 1)
            for q in range(QUADS):
                spread_keys(0, q, ([(rel_ready[q - 1], 1)] if q >= 1 else []) + ([(counted[q - 2], 1)] if q >= 2 else []))
                look_up(0, q)
            with pe.Fori(0, ITERS - 1, 1) as it:
                for q in range(QUADS):
                    before = (rel_ready[q - 1], it + 2) if q >= 1 else (rel_ready[QUADS - 1], it + 1)
                    spread_keys(it + 1, q, [before, bank_before(counted, it + 1, q)])
                    add_up(it, q)
                    pe.wait_ge(added[q], it + 1)
                    look_up(it + 1, q)
            for q in range(QUADS):
                add_up(ITERS - 1, q)


def batch_norm_rows(nc, m, a):
    with ExitStack() as ctx:
        sb, pb, sem = place(nc, ctx, "bn")
        gamma, beta = sb("gamma", [P, 1]), sb("beta", [P, 1])
        load_weights(nc, m, "bn_load", [(gamma[:], a["L2_gnn_gamma"].rearrange("(n a) -> n a", a=1)), (beta[:], a["L2_gnn_beta"].rearrange("(n a) -> n a", a=1))])
        v = sb("v", [P, 6])
        diag = sb("diag", [P, 2, C])
        first, target = sb("first", [P, TP]), sb("target", [P, TP])
        ps_v = pb("ps_v", [P, 2])
        columned = sem("columned")
        ps = pb("ps", [P, 2, C])
        var_ready, root_ready, diag_ready, spread = sem("var_ready", "root_ready", "diag_ready", "spread")
        block = ctx.enter_context(nc.Block())

        @block.vector
        def _(dve):
            link = chain(dve, m)
            ts, stt = nc.vector.tensor_scalar, nc.vector.scalar_tensor_tensor
            dve.wait_ge(columned, 2)
            link(ts(v[:, 0:2], ps_v[:], 1.0 / EDGES, None, ALU.mult))
            link(stt(v[:, 2:3], v[:, 0:1], v[:, 0:1], v[:, 1:2], ALU.mult, ALU.subtract))
            ts(v[:, 3:4], v[:, 2:3], -1.0, 0.0, ALU.mult, ALU.max).then_inc(var_ready, 1)
            dve.wait_ge(root_ready, 1)
            link(nc.vector.reciprocal(v[:, 5:6], v[:, 4:5]))
            link(nc.vector.tensor_tensor(v[:, 5:6], v[:, 5:6], gamma[:], ALU.mult))
            link(nc.vector.tensor_tensor(v[:, 4:5], v[:, 0:1], v[:, 5:6], ALU.mult))
            link(nc.vector.tensor_tensor(v[:, 4:5], beta[:], v[:, 4:5], ALU.subtract))
            ts(diag[:, 0], m.ident[:], v[:, 5:6], None, ALU.mult).then_inc(diag_ready, 1)
            ts(diag[:, 1], m.ident[:], v[:, 4:5], None, ALU.mult).then_inc(diag_ready, 1)
            link(ts(first[:], m.seen[:], 0.5, None, ALU.is_lt))
            link(ts(target[:], m.rel[:], 0.0, None, ALU.is_ge))
            link(nc.vector.tensor_tensor(first[:], first[:], target[:], ALU.mult))
            link(ts(m.column[:], m.column[:], float(ROWS), None, ALU.add))
            link(ts(target[:], m.src_key[:], m.column[:], None, ALU.subtract))
            link(nc.vector.tensor_tensor(target[:], target[:], first[:], ALU.mult))
            link(ts(target[:], target[:], m.column[:], None, ALU.add))
            link(nc.vector.tensor_copy(m.target[:], target[:]))
            dve.wait_ge(spread, 2)
            link(nc.vector.tensor_copy(m.norm_rows[:], ps[:]))

        @block.scalar
        def _(act):
            act.wait_ge(var_ready, 1)
            nc.scalar.activation(v[:, 4:5], v[:, 3:4], ACT.Sqrt, bias=m.epsilon[:], scale=1.0).then_inc(root_ready, 1)

        @block.tensor
        def _(pe):
            for k in range(2):
                nc.tensor.matmul(ps_v[:, k:k + 1], m.totals[:, k * C:(k + 1) * C], m.ones[0:1, 0:1], start=True, stop=True).then_inc(columned, 1)
            pe.wait_ge(diag_ready, 2)
            for k in range(2):
                nc.tensor.matmul(ps[:, k, :], m.ones[:], diag[:, k], start=True, stop=True).then_inc(spread, 1)


def scatter_by_source(nc, m, a):
    assert COPIES == 2 * QU
    with ExitStack() as ctx:
        sb, pb, sem = place(nc, ctx, "sc")
        rows = sb("rows", [P, 2, HU, C])
        message = sb("message", [P, 2, HU, SW])
        src_keys = sb("src_keys", [2, 2, HU * P], BF16)
        same = sb("same", [P, U, P])
        total = sb("total", [P, U, SW])
        stage = [sb(f"stage{q}", [P, QU], I32) for q in range(QUADS)]
        ps_src = [pb(f"ps_src{k}", [P, QU, P]) for k in range(2)]
        ps = [pb(f"ps{k}", [P, QU, 256]) for k in range(2)]
        rows_in, keys_in, scaled, shifted, relued = ([sem(f"{n}{h}") for h in range(2)] for n in ("rows_in", "keys_in", "scaled", "shifted", "relued"))
        spread, matched, summed, taken, staged = (
            [sem(f"{n}{q}") for q in range(QUADS)] for n in ("spread", "matched", "summed", "taken", "staged"))
        scattered = [sem(f"scattered{k}") for k in range(COPIES)]
        carried, counts_set = sem("carried", "counts_set")
        block = ctx.enter_context(nc.Block())

        @block.sync
        def _(sp):
            with sp.Fori(0, ITERS, 1) as it:
                for h in range(2):
                    edges = bass.ds((it * U + h * HU) * P, HU * P)
                    sp.wait_ge(spread[2 * h + 1], it)
                    sp.dma_start(src_keys[:, h], m.t_keys[LOW:HIGH + 1, edges]).then_inc(keys_in[h], 16)
                    sp.wait_ge(relued[h], it)
                    sp.dma_start(rows[:, h], m.t_hidden[edges, :].rearrange("(t p) f -> p t f", p=P)).then_inc(rows_in[h], 16)

        @block.vector
        def _(dve):
            nc.vector.memset(message[:], 1.0).then_inc(counts_set, 1)

            def normalise(it, h):
                wide = lambda k: m.norm_rows[:, k:k + 1, :].to_broadcast([P, HU, C])
                dve.wait_ge(rows_in[h], 16 * (it + 1))
                nc.vector.tensor_tensor(rows[:, h], rows[:, h], wide(0), ALU.mult).then_inc(scaled[h], 1)
                dve.wait_ge(scaled[h], it + 1)
                nc.vector.tensor_tensor(rows[:, h], rows[:, h], wide(1), ALU.add).then_inc(shifted[h], 1)

            def match(it, q):
                dve.wait_ge(spread[q], it + 1)
                dve.wait_ge(summed[q], it)
                for k in range(QU):
                    u = q * QU + k
                    nc.vector.tensor_scalar(same[:, u, :], ps_src[q % 2][:, k, :], m.src_key[:, bass.ds(it * U + u, 1)], None,
                                            ALU.is_equal).then_inc(matched[q], 1)

            def take(it, q):
                dve.wait_ge(staged[q], it + 1)
                dve.wait_ge(summed[q], it + 1)
                nc.vector.tensor_copy(total[:, q * QU:(q + 1) * QU, :], ps[q % 2][:, :, 0:SW]).then_inc(taken[q], 1)

            with dve.Fori(0, ITERS, 1) as it:
                for q in range(QUADS):
                    if q % 2 == 0:
                        normalise(it, q // 2)
                    match(it, q)
                    if q >= 1:
                        take(it, q - 1)
                take(it, QUADS - 1)

        @block.scalar
        def _(act):
            act.wait_ge(counts_set, 1)
            with act.Fori(0, ITERS, 1) as it:
                for q in range(QUADS):
                    h, even = divmod(q, 2)
                    if even == 0:
                        for r in (q, q + 1):
                            act.wait_ge(summed[r], it)
                        act.wait_ge(shifted[h], it + 1)
                        nc.scalar.activation(message[:, h, :, 0:C], rows[:, h], ACT.Relu).then_inc(relued[h], 1)
                    for k in range(QU):
                        act.wait_ge(scattered[(q % 2) * QU + k], 32 * it)
                    nc.scalar.copy(stage[q][:], m.target[:, bass.ds(it * U + q * QU, QU)]).then_inc(staged[q], 1)

        @block.tensor
        def _(pe):
            def add_up(it, q):
                pe.wait_ge(relued[q // 2], it + 1)
                pe.wait_ge(matched[q], QU * (it + 1))
                pe.wait_ge(*bank_before(taken, it, q))
                for k in range(QU):
                    u = q * QU + k
                    last = nc.tensor.matmul(ps[q % 2][:, k, 0:SW], same[:, u, :], message[:, u // HU, u % HU, :], start=True, stop=True)
                last.then_inc(summed[q], 1)

            with pe.Fori(0, ITERS, 1) as it:
                for q in range(QUADS):
                    h = q // 2
                    pe.wait_ge(keys_in[h], 16 * (it + 1))
                    earlier, count = bank_before(matched, it, q)
                    pe.wait_ge(earlier, QU * count)
                    nc.tensor.matmul(ps_src[q % 2][:].rearrange("p k e -> p (k e)"), m.spread_src[:],
                                     src_keys[:, h, (q % 2) * QU * P:(q % 2 + 1) * QU * P], start=True, stop=True).then_inc(spread[q], 1)
                    if q >= 1:
                        add_up(it, q - 1)
                add_up(it, QUADS - 1)

        @block.gpsimd
        def _(pool):
            with pool.Fori(0, ITERS, 1) as it:
                for q in range(QUADS):
                    pool.wait_ge(carried, it * QUADS + q)
                    pool.wait_ge(taken[q], it + 1)
                    for k in range(QU):
                        pool.wait_ge(scattered[(q % 2) * QU + k], 16 * (it * 2 + q // 2))
                    nc.gpsimd.tensor_tensor(m.carrier[:], m.ones_i[:], m.ones_i[:], ALU.add).then_inc(carried, 1)
                    for k in range(QU):
                        copy = (q % 2) * QU + k
                        pool.indirect_dma_start(m.scatter[copy], bass.IndirectOffsetOnAxis(ap=stage[q][:, k:k + 1], axis=0), total[:, q * QU + k, :],
                                                None, compute_op=ALU.add).then_inc(scattered[copy], 16)
            for c in range(COPIES):
                pool.wait_ge(scattered[c], 16 * 2 * ITERS)


def after_block2(nc, m, a):
    with ExitStack() as ctx:
        sb, pb, sem = place(nc, ctx, "n5")
        w2, w0, w8 = sb("w2", [P, C]), sb("w0", [P, C]), sb("w8", [P, R8, C])
        b2 = sb("b2", [P, C])
        load_weights(nc, m, "n5_load", [(w2[:], a["L2_gnn_W2"]), (w0[:], a["L3_gnn_W0"]), (w8[:], a["L3_gnn_W"].rearrange("r k n -> k r n")),
                                        (b2[:], row_of(a["L2_gnn_b2"]).to_broadcast([P, C]))])
        HC = COPIES // 2
        copies = [sb(f"copies{k}", [P, HC, GN, SW]) for k in range(2)]
        first_sum, sums = sb("first_sum", [P, GN, SW]), sb("sums", [P, GN, SW])
        sums_t = sb("sums_t", [P, GN, P])
        count = sb("count", [P, 2, GN])
        y = sb("y", [P, GN, C])
        x, x_t = sb("x", [P, GN, C]), sb("x_t", [P, GN, P])
        h = sb("h", [P, GN, R8, C])
        ps_t, ps, ps_h = pb("ps_t", [P, 8, P]), pb("ps", [P, 8, C]), pb("ps_h", [P, 4, 512])
        b = NormBuffers(sb, sem)
        loaded, folded, folded_twice = ([sem(f"{n}{k}") for k in range(2)] for n in ("loaded", "folded", "folded_twice"))
        steps, summed, turned, kept, made, joined, taken = sem("steps", "summed", "turned", "kept", "made", "joined", "taken")
        turned2, kept2, root_made, root_taken, h_made, h_taken, stored, x_kept, tail_cleared = sem(
            "turned2", "kept2", "root_made", "root_taken", "h_made", "h_taken", "stored", "x_kept", "tail_cleared")
        block = ctx.enter_context(nc.Block())
        root = ps[:].rearrange("p (b j) n -> p b (j n)", b=2)[:, :, 0:GW // 2]
        BANKS = 2 * GN
        EARLY = 8

        @block.sync
        def _(sp):
            def load(g, k):
                for c in range(HC):
                    sp.dma_start(copies[k][:, c], node_rows(m.scatter[k * HC + c], g, SW)).then_inc(loaded[k], 16)

            for k in range(2):
                load(0, k)
            with sp.Fori(0, NG - 1, 1) as g:
                sp.wait_ge(folded_twice[0], g + 1)
                load(g + 1, 0)
                sp.wait_ge(summed, g + 1)
                load(g + 1, 1)

        @block.gpsimd
        def _(pool):
            with pool.Fori(0, NG, 1) as g:
                for k in range(2):
                    pool.wait_ge(loaded[k], 16 * HC * (g + 1))
                    nc.gpsimd.tensor_tensor(copies[k][:, 0:2], copies[k][:, 0:2], copies[k][:, 2:4], ALU.add).then_inc(folded[k], 1)
                    pool.wait_ge(folded[k], g + 1)
                    if k == 0:
                        pool.wait_ge(summed, g)
                    out = first_sum[:] if k == 0 else copies[1][:, 0]
                    nc.gpsimd.tensor_tensor(out, copies[k][:, 0], copies[k][:, 1], ALU.add).then_inc(folded_twice[k], 1)
                pool.wait_ge(folded_twice[1], g + 1)
                pool.wait_ge(joined, g * GN)
                nc.gpsimd.tensor_tensor(sums[:], first_sum[:], copies[1][:, 0], ALU.add).then_inc(summed, 1)

        @block.vector
        def _(dve):
            nc.vector.memset(m.acc[:, :, ROWS:ACCW], 0.0).then_inc(tail_cleared, 1)
            with dve.Fori(0, NG, 1) as g:
                b.g = g
                link = LoopChain(dve, steps, g, 2 + 1 + 2)
                dve.wait_ge(summed, g + 1)
                link(nc.vector.tensor_scalar(count[:, 0], sums[:, :, C], 1.0, None, ALU.add))
                link(nc.vector.reciprocal(count[:, 1], count[:, 0]))
                dve.wait_ge(made, g + 1)
                for j in range(GN):
                    nc.vector.scalar_tensor_tensor(y[:, j, :], b2[:], sums[:, j, C:C + 1], ps[:, j, :], ALU.mult, ALU.add).then_inc(joined, 1)
                dve.wait_ge(joined, (g + 1) * GN)
                for j in range(GN):
                    nc.vector.scalar_tensor_tensor(y[:, j, :], y[:, j, :], count[:, 1, j:j + 1], m.x[:, bass.ds(g * GN + j, 1), :],
                                                   ALU.mult, ALU.add).then_inc(taken, 1)
                dve.wait_ge(taken, (g + 1) * GN)
                link(nc.vector.tensor_tensor(y[:], y[:], m.x[:, group_tiles(g), :], ALU.add))
                dve.wait_ge(x_kept, g)
                dve.wait_ge(turned2, g)
                layer_norm(nc, dve, link, b, y, x)
                link.end()

        @block.scalar
        def _(act):
            def take(g, banks):
                act.wait_ge(stored, 16 * g)
                for n in banks:
                    act.wait_ge(h_made, g * BANKS + n + 1)
                    out = h[:, n // 2, (n % 2) * 4:(n % 2) * 4 + 4].rearrange("p r n -> p (r n)")
                    nc.scalar.copy(out, ps_h[:, n % 4, :]).then_inc(h_taken, 1)

            def first(g):
                act.wait_ge(turned, g + 1)
                act.wait_ge(made, g)
                nc.scalar.copy(sums_t[:], ps_t[:, 0:GN, :]).then_inc(kept, 1)

            def second(g):
                b.g = g
                layer_norm_root(nc, act, m, b)

            def third(g):
                act.wait_ge(b.norm_ready, (g + 1) * GN)
                nc.scalar.copy(m.x[:, group_tiles(g), :], x[:]).then_inc(x_kept, 1)
                act.wait_ge(turned2, g + 1)
                act.wait_ge(h_made, BANKS * g)
                nc.scalar.copy(x_t[:], ps_t[:, 0:GN, :]).then_inc(kept2, 1)
                act.wait_ge(root_made, g + 1)
                nc.scalar.copy(m.acc[:, 0, group_cols(g)].rearrange("p (b n) -> p b n", b=2), root).then_inc(root_taken, 1)

            def store(g):
                act.wait_ge(h_taken, (g + 1) * BANKS)
                act.dma_start(node_rows(m.t_rel8, g, R8 * C), h[:].rearrange("p j r n -> p j (r n)")).then_inc(stored, 16)

            first(0)
            second(0)
            third(0)
            with act.Fori(0, NG - 1, 1) as g:
                first(g + 1)
                take(g, range(EARLY))
                second(g + 1)
                take(g, range(EARLY, BANKS))
                store(g)
                third(g + 1)
            take(NG - 1, range(BANKS))
            store(NG - 1)
            act.wait_ge(stored, 16 * NG)

        @block.tensor
        def _(pe):
            def project(g):
                pe.wait_ge(summed, g + 1)
                pe.wait_ge(kept2, g)
                for j in range(GN):
                    last = nc.tensor.transpose(ps_t[:, j, :], sums[:, j, 0:C], m.ident[:])
                last.then_inc(turned, 1)
                pe.wait_ge(kept, g + 1)
                pe.wait_ge(root_taken, g)
                for j in range(GN):
                    last = nc.tensor.matmul(ps[:, j, :], sums_t[:, j, :], w2[:], start=True, stop=True)
                last.then_inc(made, 1)

            def root_term(g):
                pe.wait_ge(b.norm_ready, (g + 1) * GN)
                for j in range(GN):
                    last = nc.tensor.transpose(ps_t[:, j, :], x[:, j, :], m.ident[:])
                last.then_inc(turned2, 1)
                pe.wait_ge(kept2, g + 1)
                for c in range(2):
                    nodes = x_t[:].rearrange("p j n -> p (j n)")[:, c * (GW // 2):(c + 1) * (GW // 2)]
                    last = nc.tensor.matmul(root[:, c, :], w0[:], nodes, start=True, stop=True)
                last.then_inc(root_made, 1)

            def messages(g):
                for n in range(BANKS):
                    pe.wait_ge(h_taken, g * BANKS + n - 3 if n >= 4 else g * BANKS)
                    nc.tensor.matmul(ps_h[:, n % 4, :], x_t[:, n // 2, :], w8[:, (n % 2) * 4:(n % 2) * 4 + 4].rearrange("p r n -> p (r n)"),
                                     start=True, stop=True).then_inc(h_made, 1)

            project(0)
            root_term(0)
            with pe.Fori(0, NG - 1, 1) as g:
                project(g + 1)
                messages(g)
                root_term(g + 1)
            messages(NG - 1)


def after_block3(nc, m, a):
    with ExitStack() as ctx:
        sb, pb, sem = place(nc, ctx, "n6")
        scaled = sb("scaled", [P, GN, P])
        y = sb("y", [P, GN, C])
        ps = pb("ps", [P, 8, C])
        b = NormBuffers(sb, sem)
        staged, made, taken, steps, stored = sem("staged", "made", "taken", "steps", "stored")
        block = ctx.enter_context(nc.Block())

        @block.tensor
        def _(pe):
            with pe.Fori(0, NG, 1) as g:
                pe.wait_ge(staged, g + 1)
                pe.wait_ge(taken, g)
                for j in range(GN):
                    last = nc.tensor.transpose(ps[:, j, :], scaled[:, j, :], m.ident[:])
                last.then_inc(made, 1)

        @block.scalar
        def _(act):
            with act.Fori(0, NG, 1) as g:
                b.g = g
                layer_norm_root(nc, act, m, b)

        @block.vector
        def _(dve):

            def scale(g):
                nc.vector.tensor_tensor(scaled[:].rearrange("p j n -> p (j n)"), m.acc[:, 0, group_cols(g)],
                                        m.inv_degree[:, group_cols(g)], ALU.mult).then_inc(staged, 1)

            def join(g):
                dve.wait_ge(made, g + 1)
                dve.wait_ge(b.norm_ready, g * GN)
                nc.vector.tensor_tensor(y[:], ps[:, 0:GN, :], m.x[:, group_tiles(g), :], ALU.add).then_inc(taken, 1)

            def norm(g):
                b.g = g
                link = LoopChain(dve, steps, g, 2)
                dve.wait_ge(taken, g + 1)
                layer_norm(nc, dve, link, b, y, m.x[:, group_tiles(g), :])
                link.end()

            scale(0)
            with dve.Fori(0, NG - 1, 1) as g:
                join(g)
                scale(g + 1)
                norm(g)
            join(NG - 1)
            norm(NG - 1)

        @block.sync
        def _(sp):
            with sp.Fori(0, NG - 1, 1) as g:
                sp.wait_ge(b.norm_ready, (g + 1) * GN)
                sp.dma_start(node_rows(a["out"], g, C), m.x[:, group_tiles(g), :]).then_inc(stored, 16)
            first = (NG - 1) * GN
            sp.wait_ge(b.norm_ready, NG * GN)
            sp.dma_start(a["out"][first * P:(NT - 1) * P, :].rearrange("(j p) f -> p j f", p=P), m.x[:, first:NT - 1, :]).then_inc(stored, 16)
            sp.dma_start(a["out"][(NT - 1) * P:NODES, :], m.x[0:TAIL, NT - 1, :]).then_inc(stored, 16)
            sp.wait_ge(stored, 16 * (NG + 1))


class Memory:
    pass


class EdgeSemaphores:
    def __init__(self, sem):
        self.passes, self.hots = 0, 0
        self.gathered = [sem(f"gathered{u}") for u in range(U)]
        self.half_used = [sem(f"half_used{h}") for h in range(2)]
        self.staged, self.carried, self.hot_ready, self.window_ready, self.window_used = sem(
            "staged", "carried", "hot_ready", "window_ready", "window_used")


def gnn_blocks(nc, a):
    with ExitStack() as ctx:
        sb, _, sem = place(nc, ctx, "all")
        m = Memory()
        m.steps, m.step = 0, sem("step")
        m.edge = EdgeSemaphores(sem)
        table = lambda name, *shape: nc.dram_tensor(name, shape, F32, kind="Internal").ap()
        m.t_x, m.t_f, m.t_p, m.t_q = table("t_x", ROWS, C), table("t_f", ROWS, C), table("t_p", ROWS, C), table("t_q", ACCW, C)
        m.t_s1, m.t_h, m.t_al = table("t_s1", ROWS, H), table("t_h", ROWS, 2 * H), table("t_al", ROWS, 4)
        m.t_rel4, m.t_rel8 = table("t_rel4", ROWS, R4 * C), table("t_rel8", ROWS, R8 * C)
        m.t_hidden, m.t_self = table("t_hidden", T * P, C), table("t_self", TP * P, 2)
        m.t_ea, m.t_last = table("t_ea", 2, TP * P), table("t_last", TP * P, 4)
        m.t_keys = nc.dram_tensor("t_keys", (3, TP * P), BF16, kind="Internal").ap()
        m.scatter = [table(f"scatter{k}", SROWS, SW) for k in range(COPIES)]
        m.iota, m.ident, m.before, m.ones = (sb(n, [P, P]) for n in ("iota", "ident", "before", "ones"))
        m.column, m.minus_column, m.epsilon = (sb(n, [P, 1]) for n in ("column", "minus_column", "epsilon"))
        m.spread_one, m.spread_src = sb("spread_one", [1, P], BF16), sb("spread_src", [2, P], BF16)
        m.ones_i, m.carrier = sb("ones_i", [1, 1], I32), sb("carrier", [1, 1], I32)
        m.x = sb("x", [P, NT, C])
        m.src, m.src4, m.src8 = (sb(n, [P, TP], I32) for n in ("src", "src4", "src8"))
        m.rel, m.w_rgcn, m.w_edge, m.src_key, m.src_high = (sb(n, [P, TP]) for n in ("rel", "w_rgcn", "w_edge", "src_key", "src_high"))
        m.base = sb("base", [1, TP], I32)
        m.last_edge_f, m.has_edges = sb("last_edge_f", [P, NT]), sb("has_edges", [P, NT])
        m.last_edge = sb("last_edge", [P, NT], I32)
        m.self_weight = sb("self_weight", [P, NT, 2])
        m.totals, m.norm_rows = sb("totals", [1, 2 * C]), sb("norm_rows", [P, 2, C])

        with nc.cleanup_on_exit():
            constants(nc, m, a)
            edge_setup(nc, m, a)
        m.inv_degree = sb("inv_degree", [P, ROWS])
        with nc.cleanup_on_exit(), ExitStack() as scope:
            scoped, _, _ = place(nc, scope, "first")
            m.acc = scoped("acc", [P, 2, ACCW])
            aggregate(nc, m, "block0", a["x"], m.src, [], 1, degree=True)
            degrees(nc, m)
            after_block0(nc, m, a)
            aggregate(nc, m, "sage1", m.t_x, m.src, [], 1, clears_tables=True)
            after_sage1(nc, m, a)
            aggregate(nc, m, "sage2", m.t_s1, m.src, [], 2)
            after_sage2(nc, m, a)
        m.alpha = sb("alpha", [P, 2, TP])
        with nc.cleanup_on_exit(), ExitStack() as scope:
            scoped, _, _ = place(nc, scope, "attention")
            m.e = scoped("e", [P, 2, TP])
            attention_terms(nc, m)
            attention_softmax(nc, m, a)
        with nc.cleanup_on_exit(), ExitStack() as scope:
            scoped, _, _ = place(nc, scope, "second")
            m.acc = scoped("acc", [P, 2, ACCW])
            aggregate(nc, m, "gat", m.t_h, m.src, [m.alpha[:, 0], m.alpha[:, 1]], 2)
            after_gat(nc, m, a)
            aggregate(nc, m, "rgcn", m.t_rel4.rearrange("n (r f) -> (n r) f", f=C), m.src4, [m.w_rgcn], 1, clear=False)
            after_rgcn(nc, m, a)
        m.seen, m.target = m.alpha[:, 0], m.alpha[:, 1].bitcast(I32)
        with nc.cleanup_on_exit():
            edge_hidden(nc, m, a)
            batch_norm_rows(nc, m, a)
            scatter_by_source(nc, m, a)
        with ExitStack() as scope:
            scoped, _, _ = place(nc, scope, "third")
            m.acc = scoped("acc", [P, 1, ACCW])
            after_block2(nc, m, a)
            aggregate(nc, m, "block3", m.t_rel8.rearrange("n (r f) -> (n r) f", f=C), m.src8, [m.w_edge], 1, clear=False)
            after_block3(nc, m, a)


NAMES = ["x", "src", "dst", "edge_attr_2", "edge_type_4", "edge_type_8", "edge_weight", "L0_gnn_W_neigh", "L0_gnn_b_neigh",
         "L1_gnn_sage1_Wl", "L1_gnn_sage1_Wr", "L1_gnn_sage1_b", "L1_gnn_sage2_Wl", "L1_gnn_sage2_Wr", "L1_gnn_sage2_b", "L1_gnn_gat_W",
         "L1_gnn_gat_att_src", "L1_gnn_gat_att_dst", "L1_gnn_gat_b", "L1_gnn_rgcn_Wrel", "L1_gnn_rgcn_Wroot", "L1_gnn_rgcn_b",
         "L1_gnn_fusion_W", "L1_gnn_fusion_b", "L2_gnn_W1", "L2_gnn_b1", "L2_gnn_gamma", "L2_gnn_beta", "L2_gnn_W2", "L2_gnn_b2",
         "L3_gnn_W", "L3_gnn_W0"]


def kernel(**inputs):
    import concourse.bacc as bacc
    from concourse.bass_utils import run_bass_kernel_spmd

    nc = bacc.Bacc("TRN2", target_bir_lowering=False, num_devices=1)
    arrays, a = {}, {}
    for name in NAMES:
        arrays[f"in_{name}"] = np.ascontiguousarray(inputs[name])
        a[name] = nc.dram_tensor(f"in_{name}", arrays[f"in_{name}"].shape, mybir.dt.from_np(arrays[f"in_{name}"].dtype), kind="ExternalInput").ap()
    a["out"] = nc.dram_tensor("out", (NODES, C), F32, kind="ExternalOutput").ap()
    gnn_blocks(nc, a)
    return run_bass_kernel_spmd(nc, [arrays], core_ids=[0]).results[0]["out"]
```
